# Optimizing a Trainium2 kernel written in Bass

```python
import numpy as np
import jax
import jax.numpy as jnp

def _softmax(x, axis=-1):
    return jax.nn.softmax(x, axis=axis)

def _gelu(x):
    return jax.nn.gelu(x, approximate=True)

def _silu(x):
    return jax.nn.silu(x)

def _sigmoid(x):
    return jax.nn.sigmoid(x)

def _layernorm(x, axis=-1, eps=1e-05):
    m = jnp.mean(x, axis=axis, keepdims=True)
    v = jnp.var(x, axis=axis, keepdims=True)
    return (x - m) / jnp.sqrt(v + eps)

def _scatter_add(tgt, idx, src, axis=0):
    return tgt.at[idx].add(src)

def _segment_sum(src, seg, n):
    return jax.ops.segment_sum(src, seg, n)
kernel_name = 'mk_xattn_ffn_d4_seqx_r8_21d7cd'

def setup_inputs(seed: int=0):
    np.random.seed(seed)
    _w = jnp.asarray

    def _rec_inputs():
        import jax
        import jax.numpy as jnp
        _rk = jax.random.key(seed)
        x = -0.0005207 + 1.001 * jax.random.normal(jax.random.fold_in(_rk, 1), (4, 256, 256), jnp.float32)
        _lenS = 256 - jax.random.randint(jax.random.fold_in(_rk, 7), (4,), 0, max(1, 256 // 4) + 1, jnp.int32)
        _lenS2 = 256 - jax.random.randint(jax.random.fold_in(_rk, 8), (4,), 0, max(1, 256 // 4) + 1, jnp.int32)
        _ctx_2048P = jax.random.normal(jax.random.fold_in(_rk, 11), (4, 16, 256), jnp.float32)
        _ctx_2048c = jax.random.dirichlet(jax.random.fold_in(_rk, 511), 0.3 * jnp.ones((16,), jnp.float32), (4, 256))
        _ctx_2048t = jnp.einsum('bsk,bkd->bsd', _ctx_2048c, _ctx_2048P)
        _ctx_2048t = _ctx_2048t * jax.lax.rsqrt(jnp.mean(jnp.square(_ctx_2048t)) + 1e-12) * 0.953939
        ctx_2048 = -0.000514642 + 1.00011 * (_ctx_2048t + 0.3 * jax.random.normal(jax.random.fold_in(_rk, 611), (4, 256, 256), jnp.float32))
        return (x, ctx_2048)
    x, ctx_2048 = _rec_inputs()

    def _L0_xattn_setup():
        import jax, jax.numpy as jnp
        import numpy as np
        from math import sqrt
        key = jax.random.key(seed)
        kq, kk, kv = jax.random.split(key, 3)
        B, D, N = (8, 128, 256)
        Q = jax.random.normal(kq, (B, D, N), dtype=jnp.float32)
        K = jax.random.normal(kk, (B, D, N), dtype=jnp.float32)
        V = jax.random.normal(kv, (B, D, N), dtype=jnp.float32)
        return {'Q': Q, 'K': K, 'V': V}
    _L0_xattn_all = _L0_xattn_setup()
    _L0_xattn_in = {k: v for k, v in _L0_xattn_all.items() if k in ()}
    del _L0_xattn_all

    def _L0_ffn_setup():
        import jax, jax.numpy as jnp
        import numpy as np
        ALPHA = 1.702
        LIMIT = 7.0
        TOP_K = 4
        B, S, H = (1, 128, 256)
        E, D = (16, 256)
        key = jax.random.key(seed)
        ks = jax.random.split(key, 7)
        s = 0.02
        return {'hidden_states': jax.random.normal(ks[0], (B, S, H), dtype=jnp.float32), 'router_weight': jax.random.normal(ks[1], (E, H), dtype=jnp.float32) * s, 'router_bias': jax.random.normal(ks[2], (E,), dtype=jnp.float32) * s, 'gate_up_proj': jax.random.normal(ks[3], (E, H, 2 * D), dtype=jnp.float32) * s, 'gate_up_proj_bias': jax.random.normal(ks[4], (E, 2 * D), dtype=jnp.float32) * s, 'down_proj': jax.random.normal(ks[5], (E, D, H), dtype=jnp.float32) * s, 'down_proj_bias': jax.random.normal(ks[6], (E, H), dtype=jnp.float32) * s}
    _L0_ffn_all = _L0_ffn_setup()
    _L0_ffn_in = {k: v for k, v in _L0_ffn_all.items() if k in ('router_weight', 'router_bias', 'gate_up_proj', 'gate_up_proj_bias', 'down_proj', 'down_proj_bias')}
    del _L0_ffn_all

    def _L1_xattn_setup():
        import jax, jax.numpy as jnp
        import numpy as np
        FP8_MAX = 448.0
        ACT_EPS = 0.0001
        W_EPS = 1e-06
        BLK = 128

        def quant_dequant_act_1x128(x):
            E, M, K = x.shape
            xb = x.reshape(E, M, K // BLK, BLK)
            amax = jnp.max(jnp.abs(xb), axis=-1, keepdims=True)
            safe = jnp.maximum(amax, ACT_EPS)
            q = (xb * (FP8_MAX / safe)).astype(jnp.float8_e4m3fn)
            return (q.astype(jnp.float32) * (safe / FP8_MAX)).reshape(E, M, K)

        def quant_dequant_weight_128x128(w):
            E, N, K = w.shape
            wb = w.reshape(E, N // BLK, BLK, K // BLK, BLK)
            amax = jnp.max(jnp.abs(wb), axis=(2, 4), keepdims=True)
            safe = jnp.maximum(amax, W_EPS)
            q = (wb * (FP8_MAX / safe)).astype(jnp.float8_e4m3fn)
            return (q.astype(jnp.float32) * (safe / FP8_MAX)).reshape(E, N, K)
        key = jax.random.key(seed)
        kx, kw = jax.random.split(key)
        E, M, K, N = (8, 512, 256, 256)
        x = jax.random.normal(kx, (E, M, K), dtype=jnp.float32)
        weight = jax.random.normal(kw, (E, N, K), dtype=jnp.float32) * 0.02
        return {'x': x, 'weight': weight}
    _L1_xattn_all = _L1_xattn_setup()
    _L1_xattn_in = {k: v for k, v in _L1_xattn_all.items() if k in ()}
    del _L1_xattn_all

    def _L1_ffn_setup():
        import jax, jax.numpy as jnp
        import numpy as np
        HIDDEN = 256
        INTER = 704
        B, S = (2, 256)

        def _ternary(key, shape):
            return jax.random.randint(key, shape, -1, 2).astype(jnp.float32)
        key = jax.random.key(seed)
        ks = jax.random.split(key, 7)
        x = jax.random.normal(ks[0], (B, S, HIDDEN), dtype=jnp.float32)
        gate_w = _ternary(ks[1], (INTER, HIDDEN))
        up_w = _ternary(ks[2], (INTER, HIDDEN))
        down_w = _ternary(ks[3], (HIDDEN, INTER))
        gate_s = jax.random.uniform(ks[4], (INTER,), minval=0.01, maxval=0.1, dtype=jnp.float32)
        up_s = jax.random.uniform(ks[5], (INTER,), minval=0.01, maxval=0.1, dtype=jnp.float32)
        down_s = jax.random.uniform(ks[6], (HIDDEN,), minval=0.01, maxval=0.1, dtype=jnp.float32)
        return {'x': x, 'gate_w': gate_w, 'up_w': up_w, 'down_w': down_w, 'gate_s': gate_s, 'up_s': up_s, 'down_s': down_s}
    _L1_ffn_all = _L1_ffn_setup()
    _L1_ffn_in = {k: v for k, v in _L1_ffn_all.items() if k in ('gate_w', 'up_w', 'down_w', 'gate_s', 'up_s', 'down_s')}
    del _L1_ffn_all

    def _L2_xattn_setup():
        import jax, jax.numpy as jnp
        import numpy as np
        B, S, E, NH = (2, 128, 256, 16)
        DH = E // NH
        EPS = 1e-06

        def _mlstm_forward(q, k, v, Wi, bi, Wf, bf, ln_scale):
            b, s, e = q.shape
            nh = Wi.shape[1]
            dh = e // nh
            x = jnp.concatenate([q, k, v], axis=-1)
            ig = (x @ Wi + bi).transpose(0, 2, 1)[..., None]
            fg = (x @ Wf + bf).transpose(0, 2, 1)[..., None]
            split = lambda t: t.reshape(b, s, nh, dh).transpose(0, 2, 1, 3)
            qh, kh, vh = (split(q), split(k), split(v))
            log_f = jax.nn.log_sigmoid(fg)
            log_f_cum = jnp.concatenate([jnp.zeros((b, nh, 1, 1), q.dtype), jnp.cumsum(log_f, axis=2)], axis=2)
            fg_mat = log_f_cum - jnp.transpose(log_f_cum, (0, 1, 3, 2))
            ltr = jnp.tril(jnp.ones((s, s), dtype=bool))
            log_fg = jnp.where(ltr, fg_mat[:, :, 1:, 1:], -jnp.inf)
            log_D = log_fg + jnp.transpose(ig, (0, 1, 3, 2))
            max_log_D = jnp.max(log_D, axis=-1, keepdims=True)
            D = jnp.exp(log_D - max_log_D)
            qk = jnp.einsum('bhsd,bhtd->bhst', qh, kh) / jnp.sqrt(jnp.asarray(dh, q.dtype))
            C = qk * D
            normalizer = jnp.maximum(jnp.abs(C.sum(-1, keepdims=True)), jnp.exp(-max_log_D))
            Cn = C / (normalizer + EPS)
            h = jnp.einsum('bhst,bhtd->bhsd', Cn, vh)
            mu = h.mean(-1, keepdims=True)
            var = ((h - mu) ** 2).mean(-1, keepdims=True)
            hn = (h - mu) * jax.lax.rsqrt(var + EPS)
            hn = hn * ln_scale.reshape(1, nh, 1, dh)
            return hn.transpose(0, 2, 1, 3).reshape(b, s, e)
        key = jax.random.key(seed)
        ks = jax.random.split(key, 6)
        q = jax.random.normal(ks[0], (B, S, E), dtype=jnp.float32)
        k = jax.random.normal(ks[1], (B, S, E), dtype=jnp.float32)
        v = jax.random.normal(ks[2], (B, S, E), dtype=jnp.float32)
        Wi = jax.random.normal(ks[3], (3 * E, NH), dtype=jnp.float32) * 0.02
        bi = jax.random.normal(ks[4], (NH,), dtype=jnp.float32) * 0.1
        Wf = jax.random.normal(ks[5], (3 * E, NH), dtype=jnp.float32) * 0.02
        bf = jnp.linspace(3.0, 6.0, NH, dtype=jnp.float32)
        ln_scale = jnp.ones((E,), dtype=jnp.float32)
        return {'q': q, 'k': k, 'v': v, 'Wi': Wi, 'bi': bi, 'Wf': Wf, 'bf': bf, 'ln_scale': ln_scale}
    _L2_xattn_all = _L2_xattn_setup()
    _L2_xattn_in = {k: v for k, v in _L2_xattn_all.items() if k in ('Wi', 'bi', 'Wf', 'bf', 'ln_scale')}
    del _L2_xattn_all

    def _L2_ffn_setup():
        import jax, jax.numpy as jnp
        import numpy as np
        EPS = 1e-05

        def _ternary_weight(w, eps=EPS):
            alpha = jnp.maximum(jnp.mean(jnp.abs(w)), eps)
            return jnp.clip(jnp.round(w / alpha), -1.0, 1.0) * alpha

        def _absmax_act(x, eps=EPS):
            scale = jnp.maximum(jnp.max(jnp.abs(x), axis=-1, keepdims=True), eps) / 127.0
            return jnp.clip(jnp.round(x / scale), -128.0, 127.0) * scale
        key = jax.random.key(seed)
        k1, k2, k3 = jax.random.split(key, 3)
        B, S, D_IN, D_OUT = (4, 1024, 256, 256)
        x = jax.random.normal(k1, (B, S, D_IN), dtype=jnp.float32)
        bound_w = 1.0 / np.sqrt(D_IN)
        weight = jax.random.uniform(k2, (D_OUT, D_IN), dtype=jnp.float32, minval=-bound_w, maxval=bound_w)
        bias = jax.random.uniform(k3, (D_OUT,), dtype=jnp.float32, minval=-bound_w, maxval=bound_w)
        return {'x': x, 'weight': weight, 'bias': bias}
    _L2_ffn_all = _L2_ffn_setup()
    _L2_ffn_in = {k: v for k, v in _L2_ffn_all.items() if k in ('weight', 'bias')}
    del _L2_ffn_all

    def _L3_xattn_setup():
        import jax, jax.numpy as jnp
        import numpy as np
        FP8_MAX = 448.0
        EPS = 1e-05

        def _fp8_roundtrip(x):
            return x.astype(jnp.float8_e4m3fn).astype(jnp.float32)

        def _div_clamp_fp8(x, scale):
            y = jnp.clip(x.astype(jnp.float32) / scale, -FP8_MAX, FP8_MAX)
            y = y.astype(jnp.bfloat16).astype(jnp.float32)
            return _fp8_roundtrip(y)

        def _ln(x, w, b):
            mu = jnp.mean(x, axis=-1, keepdims=True)
            var = jnp.mean(jnp.square(x - mu), axis=-1, keepdims=True)
            return (x - mu) * jax.lax.rsqrt(var + EPS) * w + b

        def _fp8_linear_pertensor(x, wq, w_scale, in_scale):
            xq = _div_clamp_fp8(x, in_scale)
            return jnp.einsum('bsi,oi->bso', xq * in_scale, wq) * w_scale

        def _gqa(q, k, v):
            scale = 1.0 / np.sqrt(q.shape[-1])
            scores = jnp.einsum('bsghd,btgd->bghst', q, k) * scale
            p = jax.nn.softmax(scores, axis=-1)
            return jnp.einsum('bghst,btgd->bsghd', p, v)
        key = jax.random.key(seed)
        ks = jax.random.split(key, 8)
        B, S, SC, H, NH, G, D = (2, 256, 64, 256, 16, 8, 128)

        def qw(k, out_f, in_f):
            w = jax.random.normal(k, (out_f, in_f), jnp.float32) * 0.02
            sc = jnp.max(jnp.abs(w)) / FP8_MAX
            return (_fp8_roundtrip(w / sc), sc.astype(jnp.float32))
        wq, wq_s = qw(ks[0], NH * D, H)
        wqx, wqx_s = qw(ks[1], NH * D, H)
        wk, wk_s = qw(ks[2], G * D, H)
        wv, wv_s = qw(ks[3], G * D, H)
        wproj, wp_s = qw(ks[4], H, 2 * NH * D)
        return {'hidden_states': jax.random.normal(ks[5], (B, S, H), jnp.float32), 'cond': jax.random.normal(ks[6], (B, SC, H), jnp.float32), 'ln_w': jnp.ones((H,), jnp.float32), 'ln_b': jnp.zeros((H,), jnp.float32), 'wq': wq, 'wq_scale': wq_s, 'q_in_scale': jnp.full((H,), 0.05, jnp.float32), 'wqx': wqx, 'wqx_scale': wqx_s, 'qx_in_scale': jnp.full((H,), 0.05, jnp.float32), 'wk': wk, 'wk_scale': wk_s, 'k_in_scale': jnp.full((H,), 0.05, jnp.float32), 'wv': wv, 'wv_scale': wv_s, 'v_in_scale': jnp.full((H,), 0.05, jnp.float32), 'w_kv_x': jax.random.normal(ks[7], (2 * G * D, H), jnp.float32) * 0.02, 'qln_w': jnp.ones((D,), jnp.float32), 'qln_b': jnp.zeros((D,), jnp.float32), 'kln_w': jnp.ones((D,), jnp.float32), 'kln_b': jnp.zeros((D,), jnp.float32), 'qxln_w': jnp.ones((D,), jnp.float32), 'qxln_b': jnp.zeros((D,), jnp.float32), 'kxln_w': jnp.ones((D,), jnp.float32), 'kxln_b': jnp.zeros((D,), jnp.float32), 'wproj': wproj, 'proj_w_scale': wp_s, 'proj_in_scale': jnp.asarray(0.05, jnp.float32), 'proj_smooth': jnp.full((2 * NH * D,), 0.05, jnp.float32)}
    _L3_xattn_all = _L3_xattn_setup()
    _L3_xattn_in = {k: v for k, v in _L3_xattn_all.items() if k in ('ln_w', 'ln_b', 'wq', 'wq_scale', 'q_in_scale', 'wqx', 'wqx_scale', 'qx_in_scale', 'wk', 'wk_scale', 'k_in_scale', 'wv', 'wv_scale', 'v_in_scale', 'w_kv_x', 'qln_w', 'qln_b', 'kln_w', 'kln_b', 'qxln_w', 'qxln_b', 'kxln_w', 'kxln_b', 'wproj', 'proj_w_scale', 'proj_in_scale', 'proj_smooth')}
    del _L3_xattn_all

    def _L3_ffn_setup():
        import jax, jax.numpy as jnp
        import numpy as np
        B, S, D = (4, 512, 256)
        DFF = 4 * D
        SKIP = 0.125
        key = jax.random.key(seed)
        ks = jax.random.split(key, 4)
        s_in = 1.0 / np.sqrt(D).astype(np.float32)
        s_ff = 1.0 / np.sqrt(DFF).astype(np.float32)
        return {'x': jax.random.normal(ks[0], (B, S, D), jnp.float32), 'Wr': jax.random.normal(ks[1], (D, 1), jnp.float32) * s_in, 'br': jnp.zeros((1,), jnp.float32), 'W1': jax.random.normal(ks[2], (D, DFF), jnp.float32) * s_in, 'b1': jnp.zeros((DFF,), jnp.float32), 'W2': jax.random.normal(ks[3], (DFF, D), jnp.float32) * s_ff, 'b2': jnp.zeros((D,), jnp.float32)}
    _L3_ffn_all = _L3_ffn_setup()
    _L3_ffn_in = {k: v for k, v in _L3_ffn_all.items() if k in ('Wr', 'br', 'W1', 'b1', 'W2', 'b2')}
    del _L3_ffn_all
    return {'x': x, 'ctx_2048': ctx_2048, 'L0_ffn_router_weight': _L0_ffn_in['router_weight'], 'L0_ffn_router_bias': _L0_ffn_in['router_bias'], 'L0_ffn_gate_up_proj': _L0_ffn_in['gate_up_proj'], 'L0_ffn_gate_up_proj_bias': _L0_ffn_in['gate_up_proj_bias'], 'L0_ffn_down_proj': _L0_ffn_in['down_proj'], 'L0_ffn_down_proj_bias': _L0_ffn_in['down_proj_bias'], 'L1_ffn_gate_w': _L1_ffn_in['gate_w'], 'L1_ffn_up_w': _L1_ffn_in['up_w'], 'L1_ffn_down_w': _L1_ffn_in['down_w'], 'L1_ffn_gate_s': _L1_ffn_in['gate_s'], 'L1_ffn_up_s': _L1_ffn_in['up_s'], 'L1_ffn_down_s': _L1_ffn_in['down_s'], 'L2_xattn_Wi': _L2_xattn_in['Wi'], 'L2_xattn_bi': _L2_xattn_in['bi'], 'L2_xattn_Wf': _L2_xattn_in['Wf'], 'L2_xattn_bf': _L2_xattn_in['bf'], 'L2_xattn_ln_scale': _L2_xattn_in['ln_scale'], 'L2_ffn_weight': _L2_ffn_in['weight'], 'L2_ffn_bias': _L2_ffn_in['bias'], 'L3_xattn_ln_w': _L3_xattn_in['ln_w'], 'L3_xattn_ln_b': _L3_xattn_in['ln_b'], 'L3_xattn_wq': _L3_xattn_in['wq'], 'L3_xattn_wq_scale': _L3_xattn_in['wq_scale'], 'L3_xattn_q_in_scale': _L3_xattn_in['q_in_scale'], 'L3_xattn_wqx': _L3_xattn_in['wqx'], 'L3_xattn_wqx_scale': _L3_xattn_in['wqx_scale'], 'L3_xattn_qx_in_scale': _L3_xattn_in['qx_in_scale'], 'L3_xattn_wk': _L3_xattn_in['wk'], 'L3_xattn_wk_scale': _L3_xattn_in['wk_scale'], 'L3_xattn_k_in_scale': _L3_xattn_in['k_in_scale'], 'L3_xattn_wv': _L3_xattn_in['wv'], 'L3_xattn_wv_scale': _L3_xattn_in['wv_scale'], 'L3_xattn_v_in_scale': _L3_xattn_in['v_in_scale'], 'L3_xattn_w_kv_x': _L3_xattn_in['w_kv_x'], 'L3_xattn_qln_w': _L3_xattn_in['qln_w'], 'L3_xattn_qln_b': _L3_xattn_in['qln_b'], 'L3_xattn_kln_w': _L3_xattn_in['kln_w'], 'L3_xattn_kln_b': _L3_xattn_in['kln_b'], 'L3_xattn_qxln_w': _L3_xattn_in['qxln_w'], 'L3_xattn_qxln_b': _L3_xattn_in['qxln_b'], 'L3_xattn_kxln_w': _L3_xattn_in['kxln_w'], 'L3_xattn_kxln_b': _L3_xattn_in['kxln_b'], 'L3_xattn_wproj': _L3_xattn_in['wproj'], 'L3_xattn_proj_w_scale': _L3_xattn_in['proj_w_scale'], 'L3_xattn_proj_in_scale': _L3_xattn_in['proj_in_scale'], 'L3_xattn_proj_smooth': _L3_xattn_in['proj_smooth'], 'L3_ffn_Wr': _L3_ffn_in['Wr'], 'L3_ffn_br': _L3_ffn_in['br'], 'L3_ffn_W1': _L3_ffn_in['W1'], 'L3_ffn_b1': _L3_ffn_in['b1'], 'L3_ffn_W2': _L3_ffn_in['W2'], 'L3_ffn_b2': _L3_ffn_in['b2']}

def reference(x, ctx_2048, L0_ffn_router_weight, L0_ffn_router_bias, L0_ffn_gate_up_proj, L0_ffn_gate_up_proj_bias, L0_ffn_down_proj, L0_ffn_down_proj_bias, L1_ffn_gate_w, L1_ffn_up_w, L1_ffn_down_w, L1_ffn_gate_s, L1_ffn_up_s, L1_ffn_down_s, L2_xattn_Wi, L2_xattn_bi, L2_xattn_Wf, L2_xattn_bf, L2_xattn_ln_scale, L2_ffn_weight, L2_ffn_bias, L3_xattn_ln_w, L3_xattn_ln_b, L3_xattn_wq, L3_xattn_wq_scale, L3_xattn_q_in_scale, L3_xattn_wqx, L3_xattn_wqx_scale, L3_xattn_qx_in_scale, L3_xattn_wk, L3_xattn_wk_scale, L3_xattn_k_in_scale, L3_xattn_wv, L3_xattn_wv_scale, L3_xattn_v_in_scale, L3_xattn_w_kv_x, L3_xattn_qln_w, L3_xattn_qln_b, L3_xattn_kln_w, L3_xattn_kln_b, L3_xattn_qxln_w, L3_xattn_qxln_b, L3_xattn_kxln_w, L3_xattn_kxln_b, L3_xattn_wproj, L3_xattn_proj_w_scale, L3_xattn_proj_in_scale, L3_xattn_proj_smooth, L3_ffn_Wr, L3_ffn_br, L3_ffn_W1, L3_ffn_b1, L3_ffn_W2, L3_ffn_b2):
    import jax
    import jax.numpy as jnp

    def _L0_xattn_ref(Q, K, V):
        import jax, jax.numpy as jnp
        import numpy as np
        from math import sqrt
        dk = Q.shape[1]
        x = jnp.einsum('bdn,bdm->bnm', Q, K) / sqrt(dk)
        score = jax.nn.sigmoid(x)
        out = jnp.einsum('bvn,bnm->bvm', V, score)
        return out

    def _L0_ffn_ref(hidden_states, router_weight, router_bias, gate_up_proj, gate_up_proj_bias, down_proj, down_proj_bias):
        import jax, jax.numpy as jnp
        import numpy as np
        ALPHA = 1.702
        LIMIT = 7.0
        TOP_K = 4
        B, S, H = (1, 128, 256)
        E, D = (16, 256)
        batch, seq, hdim = hidden_states.shape
        x = hidden_states.reshape(-1, hdim)
        T = x.shape[0]
        logits = x @ router_weight.T + router_bias
        top_val, top_idx = jax.lax.top_k(logits, TOP_K)
        top_val = jax.nn.softmax(top_val, axis=-1)
        router_scores = jnp.zeros_like(logits).at[jnp.arange(T)[:, None], top_idx].set(top_val)
        gate_up = jnp.einsum('th,ehd->etd', x, gate_up_proj) + gate_up_proj_bias[:, None, :]
        gate = gate_up[..., ::2]
        up = gate_up[..., 1::2]
        gate = jnp.minimum(gate, LIMIT)
        up = jnp.clip(up, -LIMIT, LIMIT)
        glu = gate * jax.nn.sigmoid(gate * ALPHA)
        out = jnp.einsum('etd,edh->eth', (up + 1.0) * glu, down_proj) + down_proj_bias[:, None, :]
        out = out * router_scores.T[:, :, None]
        out = out.sum(axis=0)
        return out.reshape(batch, seq, hdim)

    def _L1_xattn_ref(x, weight):
        import jax, jax.numpy as jnp
        import numpy as np
        FP8_MAX = 448.0
        ACT_EPS = 0.0001
        W_EPS = 1e-06
        BLK = 128

        def quant_dequant_act_1x128(x):
            E, M, K = x.shape
            xb = x.reshape(E, M, K // BLK, BLK)
            amax = jnp.max(jnp.abs(xb), axis=-1, keepdims=True)
            safe = jnp.maximum(amax, ACT_EPS)
            q = (xb * (FP8_MAX / safe)).astype(jnp.float8_e4m3fn)
            return (q.astype(jnp.float32) * (safe / FP8_MAX)).reshape(E, M, K)

        def quant_dequant_weight_128x128(w):
            E, N, K = w.shape
            wb = w.reshape(E, N // BLK, BLK, K // BLK, BLK)
            amax = jnp.max(jnp.abs(wb), axis=(2, 4), keepdims=True)
            safe = jnp.maximum(amax, W_EPS)
            q = (wb * (FP8_MAX / safe)).astype(jnp.float8_e4m3fn)
            return (q.astype(jnp.float32) * (safe / FP8_MAX)).reshape(E, N, K)
        xq = quant_dequant_act_1x128(x)
        wq = quant_dequant_weight_128x128(weight)
        return jnp.einsum('emk,enk->emn', xq, wq)

    def _L1_ffn_ref(x, gate_w, up_w, down_w, gate_s, up_s, down_s):
        import jax, jax.numpy as jnp
        import numpy as np
        HIDDEN = 256
        INTER = 704
        B, S = (2, 256)

        def _ternary(key, shape):
            return jax.random.randint(key, shape, -1, 2).astype(jnp.float32)
        b, s, h = x.shape
        xf = x.reshape(b * s, h)
        g = jnp.einsum('th,ih->ti', xf, gate_w) * gate_s
        u = jnp.einsum('th,ih->ti', xf, up_w) * up_s
        hdn = jax.nn.silu(g) * u
        out = jnp.einsum('ti,hi->th', hdn, down_w) * down_s
        return out.reshape(b, s, -1)

    def _L2_xattn_ref(q, k, v, Wi, bi, Wf, bf, ln_scale):
        import jax, jax.numpy as jnp
        import numpy as np
        B, S, E, NH = (2, 128, 256, 16)
        DH = E // NH
        EPS = 1e-06

        def _mlstm_forward(q, k, v, Wi, bi, Wf, bf, ln_scale):
            b, s, e = q.shape
            nh = Wi.shape[1]
            dh = e // nh
            x = jnp.concatenate([q, k, v], axis=-1)
            ig = (x @ Wi + bi).transpose(0, 2, 1)[..., None]
            fg = (x @ Wf + bf).transpose(0, 2, 1)[..., None]
            split = lambda t: t.reshape(b, s, nh, dh).transpose(0, 2, 1, 3)
            qh, kh, vh = (split(q), split(k), split(v))
            log_f = jax.nn.log_sigmoid(fg)
            log_f_cum = jnp.concatenate([jnp.zeros((b, nh, 1, 1), q.dtype), jnp.cumsum(log_f, axis=2)], axis=2)
            fg_mat = log_f_cum - jnp.transpose(log_f_cum, (0, 1, 3, 2))
            ltr = jnp.tril(jnp.ones((s, s), dtype=bool))
            log_fg = jnp.where(ltr, fg_mat[:, :, 1:, 1:], -jnp.inf)
            log_D = log_fg + jnp.transpose(ig, (0, 1, 3, 2))
            max_log_D = jnp.max(log_D, axis=-1, keepdims=True)
            D = jnp.exp(log_D - max_log_D)
            qk = jnp.einsum('bhsd,bhtd->bhst', qh, kh) / jnp.sqrt(jnp.asarray(dh, q.dtype))
            C = qk * D
            normalizer = jnp.maximum(jnp.abs(C.sum(-1, keepdims=True)), jnp.exp(-max_log_D))
            Cn = C / (normalizer + EPS)
            h = jnp.einsum('bhst,bhtd->bhsd', Cn, vh)
            mu = h.mean(-1, keepdims=True)
            var = ((h - mu) ** 2).mean(-1, keepdims=True)
            hn = (h - mu) * jax.lax.rsqrt(var + EPS)
            hn = hn * ln_scale.reshape(1, nh, 1, dh)
            return hn.transpose(0, 2, 1, 3).reshape(b, s, e)
        return _mlstm_forward(q, k, v, Wi, bi, Wf, bf, ln_scale)

    def _L2_ffn_ref(x, weight, bias):
        import jax, jax.numpy as jnp
        import numpy as np
        EPS = 1e-05

        def _ternary_weight(w, eps=EPS):
            alpha = jnp.maximum(jnp.mean(jnp.abs(w)), eps)
            return jnp.clip(jnp.round(w / alpha), -1.0, 1.0) * alpha

        def _absmax_act(x, eps=EPS):
            scale = jnp.maximum(jnp.max(jnp.abs(x), axis=-1, keepdims=True), eps) / 127.0
            return jnp.clip(jnp.round(x / scale), -128.0, 127.0) * scale
        q_w = _ternary_weight(weight).astype(x.dtype)
        q_x = _absmax_act(x)
        return jnp.einsum('bsi,oi->bso', q_x, q_w) + bias.astype(x.dtype)

    def _L3_xattn_ref(hidden_states, cond, ln_w, ln_b, wq, wq_scale, q_in_scale, wqx, wqx_scale, qx_in_scale, wk, wk_scale, k_in_scale, wv, wv_scale, v_in_scale, w_kv_x, qln_w, qln_b, kln_w, kln_b, qxln_w, qxln_b, kxln_w, kxln_b, wproj, proj_w_scale, proj_in_scale, proj_smooth):
        import jax, jax.numpy as jnp
        import numpy as np
        FP8_MAX = 448.0
        EPS = 1e-05

        def _fp8_roundtrip(x):
            return x.astype(jnp.float8_e4m3fn).astype(jnp.float32)

        def _div_clamp_fp8(x, scale):
            y = jnp.clip(x.astype(jnp.float32) / scale, -FP8_MAX, FP8_MAX)
            y = y.astype(jnp.bfloat16).astype(jnp.float32)
            return _fp8_roundtrip(y)

        def _ln(x, w, b):
            mu = jnp.mean(x, axis=-1, keepdims=True)
            var = jnp.mean(jnp.square(x - mu), axis=-1, keepdims=True)
            return (x - mu) * jax.lax.rsqrt(var + EPS) * w + b

        def _fp8_linear_pertensor(x, wq, w_scale, in_scale):
            xq = _div_clamp_fp8(x, in_scale)
            return jnp.einsum('bsi,oi->bso', xq * in_scale, wq) * w_scale

        def _gqa(q, k, v):
            scale = 1.0 / np.sqrt(q.shape[-1])
            scores = jnp.einsum('bsghd,btgd->bghst', q, k) * scale
            p = jax.nn.softmax(scores, axis=-1)
            return jnp.einsum('bghst,btgd->bsghd', p, v)
        b, s, _ = hidden_states.shape
        sc = cond.shape[1]
        d = qln_w.shape[0]
        nh = wq.shape[0] // d
        g = wk.shape[0] // d
        hpg = nh // g
        ln_out = _ln(hidden_states, ln_w, ln_b)
        q = _fp8_linear_pertensor(ln_out, wq, wq_scale, q_in_scale).reshape(b, s, g, hpg, d)
        q = _ln(q, qln_w, qln_b)
        k = _fp8_linear_pertensor(ln_out, wk, wk_scale, k_in_scale).reshape(b, s, g, d)
        k = _ln(k, kln_w, kln_b)
        v = _fp8_linear_pertensor(ln_out, wv, wv_scale, v_in_scale).reshape(b, s, g, d)
        core = _gqa(q, k, v).reshape(b, s, nh * d)
        qx = _fp8_linear_pertensor(ln_out, wqx, wqx_scale, qx_in_scale).reshape(b, s, g, hpg, d)
        qx = _ln(qx, qxln_w, qxln_b)
        kvx = jnp.einsum('bsi,oi->bso', cond, w_kv_x)
        kx, vx = jnp.split(kvx, 2, axis=-1)
        kx = _ln(kx.reshape(b, sc, g, d), kxln_w, kxln_b)
        vx = vx.reshape(b, sc, g, d)
        xout = _gqa(qx, kx, vx).reshape(b, s, nh * d)
        cat = jnp.concatenate([core, xout], axis=-1)
        catq = _div_clamp_fp8(cat, proj_smooth)
        return jnp.einsum('bsi,oi->bso', catq, wproj) * (proj_in_scale * proj_w_scale)

    def _L3_ffn_ref(x, Wr, br, W1, b1, W2, b2):
        import jax, jax.numpy as jnp
        import numpy as np
        B, S, D = (4, 512, 256)
        DFF = 4 * D
        SKIP = 0.125
        Bs, Ss, Ds = x.shape
        k = max(int(Ss * SKIP), 1)
        logits = (x @ Wr + br)[..., 0]
        weights, idx = jax.lax.top_k(logits, k)
        perm = jnp.argsort(idx, axis=1)
        tokens = jnp.take_along_axis(idx, perm, axis=1)
        fx = jnp.take_along_axis(x, tokens[..., None], axis=1)
        h = jax.nn.gelu(fx @ W1 + b1, approximate=False)
        out_l = h @ W2 + b2
        tw = jax.nn.softmax(weights, axis=1)
        rw = jnp.take_along_axis(tw, perm, axis=1)
        xw = rw[..., None] * out_l
        bidx = jnp.arange(Bs)[:, None]
        return x.at[bidx, tokens].add(xw)
    x = x + _L0_xattn_ref(_layernorm(x, axis=-1), ctx_2048, ctx_2048)
    x = x + _L0_ffn_ref(_layernorm(x, axis=-1), L0_ffn_router_weight, L0_ffn_router_bias, L0_ffn_gate_up_proj, L0_ffn_gate_up_proj_bias, L0_ffn_down_proj, L0_ffn_down_proj_bias)
    x = x + _L1_xattn_ref(_layernorm(x, axis=-1), ctx_2048)
    x = x + _L1_ffn_ref(_layernorm(x, axis=-1), L1_ffn_gate_w, L1_ffn_up_w, L1_ffn_down_w, L1_ffn_gate_s, L1_ffn_up_s, L1_ffn_down_s)
    x = x + _L2_xattn_ref(_layernorm(x, axis=-1), ctx_2048, ctx_2048, L2_xattn_Wi, L2_xattn_bi, L2_xattn_Wf, L2_xattn_bf, L2_xattn_ln_scale)
    x = x + _L2_ffn_ref(_layernorm(x, axis=-1), L2_ffn_weight, L2_ffn_bias)
    x = x + _L3_xattn_ref(_layernorm(x, axis=-1), ctx_2048, L3_xattn_ln_w, L3_xattn_ln_b, L3_xattn_wq, L3_xattn_wq_scale, L3_xattn_q_in_scale, L3_xattn_wqx, L3_xattn_wqx_scale, L3_xattn_qx_in_scale, L3_xattn_wk, L3_xattn_wk_scale, L3_xattn_k_in_scale, L3_xattn_wv, L3_xattn_wv_scale, L3_xattn_v_in_scale, L3_xattn_w_kv_x, L3_xattn_qln_w, L3_xattn_qln_b, L3_xattn_kln_w, L3_xattn_kln_b, L3_xattn_qxln_w, L3_xattn_qxln_b, L3_xattn_kxln_w, L3_xattn_kxln_b, L3_xattn_wproj, L3_xattn_proj_w_scale, L3_xattn_proj_in_scale, L3_xattn_proj_smooth)
    x = x + _L3_ffn_ref(_layernorm(x, axis=-1), L3_ffn_Wr, L3_ffn_br, L3_ffn_W1, L3_ffn_b1, L3_ffn_W2, L3_ffn_b2)
    return x

_drawn_inputs = setup_inputs


def setup_inputs(seed=0):
    import zlib

    import numpy as np

    out = dict(_drawn_inputs(seed))
    spreads = {'L2_xattn_ln_scale': (1.0, 0.2),
     'L3_xattn_ln_w': (1.0, 0.2),
     'L3_xattn_ln_b': (0.0, 0.1),
     'L3_xattn_q_in_scale': (0.05000000074505806, 0.2),
     'L3_xattn_qx_in_scale': (0.05000000074505806, 0.2),
     'L3_xattn_k_in_scale': (0.05000000074505806, 0.2),
     'L3_xattn_v_in_scale': (0.05000000074505806, 0.2),
     'L3_xattn_qln_w': (1.0, 0.2),
     'L3_xattn_qln_b': (0.0, 0.1),
     'L3_xattn_kln_w': (1.0, 0.2),
     'L3_xattn_kln_b': (0.0, 0.1),
     'L3_xattn_qxln_w': (1.0, 0.2),
     'L3_xattn_qxln_b': (0.0, 0.1),
     'L3_xattn_kxln_w': (1.0, 0.2),
     'L3_xattn_kxln_b': (0.0, 0.1),
     'L3_xattn_proj_smooth': (0.05000000074505806, 0.2),
     'L3_ffn_b1': (0.0, 0.1),
     'L3_ffn_b2': (0.0, 0.1)}
    factors = {}
    for name, (base, spread) in spreads.items():
        noise = np.random.default_rng([zlib.crc32(name.encode()), seed]).standard_normal(out[name].shape)
        drawn = base * np.exp(spread * noise) if base else spread * noise
        out[name] = jnp.asarray(drawn.astype(out[name].dtype))
    for name, factor in factors.items():
        out[name] = (out[name] * factor).astype(out[name].dtype)
    return out
```

```python
from contextlib import ExitStack

import concourse.bass as bass
from concourse import mybir

F32 = mybir.dt.float32
BF16 = mybir.dt.bfloat16
U16 = mybir.dt.uint16
I32 = mybir.dt.int32
ALU = mybir.AluOpType
ACT = mybir.ActivationFunctionType
AX = mybir.AxisListType
RMAX = bass.bass_isa.ReduceOp.max
RADD = bass.bass_isa.ReduceOp.add

P = 128
B, S, D = 4, 256, 256
T = B * S // P
KD = D // P
NE, TOPK = 16, 4
INTER = 704
NI = 6
NH, DH = 16, 16
G, HD = 8, 128
SLOTS = 32
NF = 8
EPS = 1e-5
ROUND23 = 12582912.0
FP8_MAX = 448.0
FP8_MAGIC = 1572864.0
FP8_TINY = 2.0 ** -6
BIG = 1e30

COLS = {}
_at = 0
for _n, _w in [("bgu", 64), ("gs", NI), ("us", NI), ("bi", 1), ("bf", 1), ("lnw", 2), ("lnb", 2),
               ("sc_q", 2), ("sc_qx", 2), ("sc_k", 2), ("sc_v", 2), ("qw", 1), ("qb", 1), ("kw", 1), ("kb", 1),
               ("qxw", 1), ("qxb", 1), ("kxw", 1), ("kxb", 1), ("smooth", 32), ("Wr", 2), ("b1", NF)]:
    COLS[_n] = (_at, _at + _w)
    _at += _w
NCOL = _at
ROWS = {}
_at = 0
for _n, _w in [("rb", 16), ("ds", D), ("lns", D), ("b2f", D), ("b2", D), ("s_q", 1), ("s_qx", 1), ("s_k", 1),
               ("s_v", 1), ("s_pw", 1), ("s_pi", 1), ("br", 1)]:
    ROWS[_n] = (_at, _at + _w)
    _at += _w
NROW = _at
CST = {"ident": (0, 128), "causal": (128, 256), "parity": (256, 258), "iota": (258, 290), "head": (290, 306)}
NCST = 312
STAGES = 8


class Chain:

    def __init__(self, eng, sem):
        self.eng, self.sem, self.n = eng, sem, 0

    def do(self, ins):
        ins.then_inc(self.sem, 1)
        self.n += 1
        return self.n

    def sync(self):
        if self.n:
            self.eng.wait_ge(self.sem, self.n)


def build(nc, x_d, ctx_d, ctxT_d, cst_d, cols_d, rows_d, rw_d, guw_d, dw_d, bd_d, gwT_d, uwT_d, dwT_d,
          wif_d, w2T_d, wg_d, wp_d, W1_d, W2_d, out_d):
    ctx_mgr = ExitStack()
    with ctx_mgr:
        def sb(name, shape, dt=F32):
            return ctx_mgr.enter_context(nc.sbuf_tensor(name, shape, dt))

        def sem(name):
            return ctx_mgr.enter_context(nc.semaphore(name))

        x = sb("x", [P, T, D])
        y = sb("y", [P, T, D])
        yT = sb("yT", [P, KD, T * P])
        cx = sb("cx", [P, T, D])
        cxT = sb("cxT", [P, KD, T * P])
        cst = sb("cst", [P, NCST])
        cols = sb("cols", [P, NCOL])
        rows = sb("rows", [P, NROW])
        identb = sb("identb", [P, P], BF16)
        causal = sb("causal", [P, P], BF16)
        bst = sb("bst", [P, 16, 6])
        mv = sb("mv", [P, T, 2])
        rs = sb("rs", [P, T])
        mhalf = sb("mhalf", [P, 32])
        mhalf32 = mhalf
        arena = sb("arena", [P, 37000])
        psum = [ctx_mgr.enter_context(nc.psum_tensor(f"bank{i}", [P, 512], F32)) for i in range(8)]
        ident = cst[:, 0:128]

        def col(name, i=0, p=P):
            return cols[0:p, COLS[name][0] + i:COLS[name][0] + i + 1]

        def row(name, p=P):
            return rows[0:p, ROWS[name][0]:ROWS[name][1]]

        class Region:

            def __init__(self, at, end):
                self.at, self.end = at, end

            def take(self, shape, dt=F32):
                n = 1
                for s_ in shape:
                    n *= s_
                words = n if dt == F32 else (n + 1) // 2
                ap = arena[:, self.at:self.at + words]
                self.at += words
                assert self.at <= self.end, (self.at, self.end)
                if dt != F32:
                    ap = ap.bitcast(dt)
                if len(shape) > 1:
                    names = "abcde"[:len(shape)]
                    ap = ap.rearrange("p (%s) -> p %s" % (" ".join(names), " ".join(names)),
                                      **{n_: s_ for n_, s_ in zip(names, shape)})
                return ap

        filled = [sem(f"filled{i}") for i in range(8)]
        emptied = [sem(f"emptied{i}") for i in range(8)]
        s_dve, s_act, s_pool = sem("dve_done"), sem("act_done"), sem("pool_done")
        s_x, s_ctx, s_ctxT, s_cst = sem("x_loaded"), sem("ctx_loaded"), sem("ctxT_loaded"), sem("cst_loaded")
        s_stage = sem("stage_done")
        s_stat, s_rs, s_y = sem("ln_stats"), sem("ln_rstd"), sem("ln_out")
        s_cb = sem("bf16_consts")

        uses, count = {}, [0] * 8

        def plan(key, bank):
            assert key not in uses, key
            uses[key] = (bank, count[bank])
            count[bank] += 1

        def claim(pe, key):
            b_, n = uses[key]
            if n:
                pe.wait_ge(emptied[b_], n)
            return psum[b_]

        def fill(ins, key):
            ins.then_inc(filled[uses[key][0]], 1)

        def take(eng, key):
            b_, n = uses[key]
            eng.wait_ge(filled[b_], n + 1)
            return psum[b_]

        def empty(ins, key):
            ins.then_inc(emptied[uses[key][0]], 1)

        def have(eng, key):
            b_, n = uses[key]
            eng.wait_ge(emptied[b_], n + 1)

        LN = {"n": 0, "dve": 0, "pool": 0}

        def ln_dve(dve, V, k, src, eps, after=None):
            if after is not None:
                dve.wait_ge(s_y, after)
            for t in range(T):
                V.do(dve.bn_stats(bst[:, t, :], src[:, t, :]))
            V.sync()
            for t in range(T):
                i = dve.bn_aggr(mv[:, t, :], bst[:, t, :])
            i.then_inc(s_stat, 1)
            dve.wait_ge(s_rs, k + 1)
            for t in range(T):
                dve.tensor_scalar(y[:, t, :], src[:, t, :], mv[:, t, 0:1], rs[:, t:t + 1],
                                  ALU.subtract, ALU.mult).then_inc(s_y, 1)

        def ln_pool(pool, C, k, eps):
            pool.wait_ge(s_stat, k + 1)
            C.do(pool.tensor_scalar(rs[:, :], mv[:, :, 1], eps, None, ALU.add))
            C.sync()
            pool.tensor_tensor(rs[:, :], rs[:, :], mhalf[:, 0:T], ALU.pow).then_inc(s_rs, 1)

        def yt_pe(pe, k, tag):
            for b in range(B):
                o = claim(pe, (tag, "yt", b))
                pe.wait_ge(s_y, 8 * k + 2 * b + 2)
                for d in range(KD):
                    for h in range(2):
                        m = pe.transpose(o[:, d * 256 + h * 128:d * 256 + h * 128 + 128],
                                         y[:, 2 * b + h, d * P:d * P + P], ident)
                fill(m, (tag, "yt", b))

        def yt_act(act, tag):
            for b in range(B):
                o = take(act, (tag, "yt", b))
                empty(act.copy(yT[:, :, b * 256:b * 256 + 256], o[:, :].rearrange("p (d n) -> p d n", d=KD)),
                      (tag, "yt", b))

        K_A, K_B, K_C, K_D, K_E, K_F, K_G, K_G2, K_H = range(9)

        wreg = Region(0, 0)
        c_reg = Region(27600, 37000)
        c_v = c_reg.take([T, 2, P])
        c_e = c_reg.take([T * 2 * P])
        c_m = c_reg.take([T * 2 * P])
        c_q = c_reg.take([T, 2, P], BF16)
        c_qT = c_reg.take([KD, T * P], BF16)
        cw_q = sb("cw_q", [P, KD, B, 2, P], BF16)
        c_sw = sb("c_sw", [P, KD, B, 2])
        c_aw = sb("c_aw", [P, 16])
        c_ax = sb("c_ax", [P, T, 2])
        c_sx = sb("c_sx", [P, T, 2])
        c_rx = sb("c_rx", [P, T, 2])
        c_rw = sb("c_rw", [P, 16])
        c_c = sb("c_c", [P, T, 2, 2])
        s_cw, s_cwr = sem("ctx_amax"), sem("ctx_amax_all")
        s_cq = sem("c_quantised")

        def fp8_round(dve, V, v, e, m, q):
            V.do(dve.tensor_scalar(e.bitcast(I32), v.bitcast(I32), 0x7F800000, None, ALU.bitwise_and))
            V.sync()
            V.do(dve.tensor_scalar(m, e, FP8_TINY, FP8_MAGIC, ALU.max, ALU.mult))
            V.sync()
            V.do(dve.tensor_tensor(e, v, m, ALU.add))
            V.sync()
            V.do(dve.tensor_tensor(q, e, m, ALU.subtract))

        def setup_dve(dve, V):
            dve.wait_ge(s_cst, 48)
            V.do(dve.tensor_copy(identb[:, :], ident))
            dve.tensor_copy(causal[:, :], cst[:, 128:256]).then_inc(s_cb, 1)
            dve.wait_ge(s_ctxT, 16)
            blocks = cxT[:, :, :].rearrange("p k (c n) -> p (k c) n", n=P)
            dve.tensor_reduce(c_aw[:, :], blocks, AX.X, ALU.max, apply_absolute_value=True).then_inc(s_cw, 1)

        def ctx_quant_dve(dve, V):
            dve.wait_ge(s_cwr, 1)
            sw = c_sw[:, :, :, :].rearrange("p k b n -> p (k b n)")
            V.do(dve.tensor_scalar(sw, sw, 1e-6, 1.0 / FP8_MAX, ALU.max, ALU.mult))
            V.sync()
            V.do(dve.reciprocal(c_rw[:, :], sw))
            V.sync()
            vv = c_v.rearrange("p a b n -> p (a b) n")
            V.do(dve.tensor_tensor(vv, cxT[:, :, :].rearrange("p k (c n) -> p (k c) n", n=P),
                                   c_rw[:, :].unsqueeze(2).to_broadcast([P, 16, P]), ALU.mult))
            V.sync()
            fp8_round(dve, V, c_v.rearrange("p a b n -> p (a b n)"), c_e, c_m,
                      cw_q[:, :, :, :, :].rearrange("p k b m n -> p (k b m n)"))

        def setup_pool(pool, C):
            C.do(pool.memset(mhalf[:, :], -0.5))
            C.sync()

        def ctx_quant_pool(pool, C):
            pool.wait_ge(s_cw, 1)
            pool.partition_all_reduce(c_sw[:, :, :, :].rearrange("p k b n -> p (k b n)"), c_aw[:, :], P, RMAX)\
                .then_inc(s_cwr, 1)

        a_reg = Region(25000, 27600)
        a_sc = a_reg.take([2, 2, 256])
        for b in range(B + 1):
            if b < B:
                plan(("A", "s", b), b % 4)
            if b > 0:
                plan(("A", "o", b - 1), 4 + b % 4)

        def A_pe(pe):
            pe.wait_ge(s_ctx, 16)
            pe.wait_ge(s_ctxT, 16)
            pe.wait_ge(s_cst, 48)
            for b in range(B + 1):
                if b < B:
                    o = claim(pe, ("A", "s", b))
                    pe.wait_ge(s_y, 8 * K_A + 2 * b + 2)
                    for n in range(2):
                        for k in range(2):
                            m = pe.matmul(o[:, n * 256:n * 256 + 256], y[:, 2 * b + k, n * P:n * P + P],
                                          cx[:, 2 * b + k, :], start=(k == 0), stop=(k == 1))
                    fill(m, ("A", "s", b))
                if b > 0:
                    c = b - 1
                    o = claim(pe, ("A", "o", c))
                    have(pe, ("A", "s", c))
                    for v in range(2):
                        for n in range(2):
                            m = pe.matmul(o[:, v * 256:v * 256 + 256],
                                          cxT[:, n, c * 256 + v * P:c * 256 + v * P + P],
                                          a_sc[:, c % 2, n, :], start=(n == 0), stop=(n == 1))
                    fill(m, ("A", "o", c))

        def A_act(act):
            for b in range(B):
                if b >= 2:
                    uk = uses[("A", "o", b - 2)]
                    act.wait_ge(filled[uk[0]], uk[1] + 1)
                o = take(act, ("A", "s", b))
                empty(act.activation(a_sc[:, b % 2, :, :], o[:, :].rearrange("p (n m) -> p n m", n=2),
                                     ACT.Sigmoid, scale=1.0 / 16.0), ("A", "s", b))

        def A_dve(dve, V):
            for b in range(B):
                o = take(dve, ("A", "o", b))
                xb = x[:, 2 * b:2 * b + 2, :].rearrange("p t d -> p (t d)")
                empty(dve.tensor_tensor(xb, xb, o[:, :], ALU.add), ("A", "o", b))
            for b in range(B):
                have(dve, ("A", "o", b))

        b_reg = Region(0, 14800)
        NWB = 3
        b_w = [b_reg.take([KD, 4 * P]) for _ in range(NWB)]
        b_d = [b_reg.take([KD, D]) for _ in range(NWB)]
        b_g = b_reg.take([2, 2, 512])
        b_sg = b_reg.take([2, 2, 512])
        b_u = b_reg.take([2, 2, 512])
        b_h = b_reg.take([2, 2, 512])
        b_rw = sb("b_rw", [P, KD, NE])
        b_lg = sb("b_lg", [P, T, NE])
        b_m8 = sb("b_m8", [P, T, 8])
        b_gt = sb("b_gt", [P, T, NE])
        b_eq = sb("b_eq", [P, T, NE])
        b_cs = sb("b_cs", [P, T, NE])
        b_n = sb("b_n", [P, T])
        b_s = sb("b_s", [P, T, NE])
        b_z = sb("b_z", [P, 256])
        b_sT = b_reg.take([T * P])
        b_bd = b_reg.take([D])
        s_bw = [sem(f"expert_loaded{i}") for i in range(NWB)]
        s_small = sem("small_loaded")
        s_blg, s_bex, s_bs = sem("b_logits"), sem("b_exp"), sem("b_scores")
        s_bu, s_bt, s_bsg, s_bh = sem("b_up"), sem("b_gated"), sem("b_sig"), sem("b_hidden")
        for b in range(B):
            plan(("B", "yt", b), b % 4)
        plan(("B", "lg"), 6)
        for c in range(2):
            plan(("B", "sT", c), 6 + c)
        for c in range(4):
            plan(("B", "bd", c), 6 + c % 2)
        NIT = 2 * NE
        gi = 0
        for i in range(NIT + 1):
            if i < NIT:
                for d in range(2):
                    for gu in range(2):
                        plan(("B", "gu", i, d, gu), gi % 6)
                        gi += 1
            if i > 0:
                for c in range(2):
                    plan(("B", "dn", i - 1, c), 6 + c)

        def B_sp(sp):
            for e in range(NE):
                s_ = e % NWB
                if e >= NWB:
                    bk, n = uses[("B", "dn", 2 * (e - NWB) + 1, 1)]
                    sp.wait_ge(filled[bk], n + 1)
                sp.dma_start(b_w[s_], guw_d[e]).then_inc(s_bw[s_], 16)
                sp.dma_start(b_d[s_], dw_d[e]).then_inc(s_bw[s_], 16)

        def B_pe(pe):
            yt_pe(pe, K_B, "B")
            pe.wait_ge(s_small, 32)
            o = claim(pe, ("B", "lg"))
            for b in range(B):
                have(pe, ("B", "yt", b))
            for t in range(T):
                for k in range(KD):
                    m = pe.matmul(o[:, t * NE:t * NE + NE], yT[:, k, t * P:t * P + P], b_rw[:, k, :],
                                  start=(k == 0), stop=(k == 1))
            fill(m, ("B", "lg"))

            def route():
                pe.wait_ge(s_bs, 1)
                for c in range(2):
                    o = claim(pe, ("B", "sT", c))
                    for j in range(4):
                        m = pe.transpose(o[0:NE, j * P:j * P + P], b_s[:, 4 * c + j, :], ident)
                    fill(m, ("B", "sT", c))
                for c in range(4):
                    o = claim(pe, ("B", "bd", c))
                    if c == 0:
                        have(pe, ("B", "sT", 0))
                        have(pe, ("B", "sT", 1))
                    for j in range(2):
                        t = 2 * c + j
                        m = pe.matmul(o[:, j * D:j * D + D], b_sT[0:NE, t * P:t * P + P], b_bd[0:NE, :],
                                      start=True, stop=True)
                    fill(m, ("B", "bd", c))

            for i in range(NIT + 1):
                if i < NIT:
                    e, half = i // 2, i % 2
                    if half == 0:
                        pe.wait_ge(s_bw[e % NWB], 32 * (e // NWB + 1))
                    for d in range(2):
                        for gu in range(2):
                            key = ("B", "gu", i, d, gu)
                            o = claim(pe, key)
                            c0 = (gu * 2 + d) * P
                            for k in range(KD):
                                m = pe.matmul(o[:, :], b_w[e % NWB][:, k, c0:c0 + P],
                                              yT[:, k, half * 512:half * 512 + 512], start=(k == 0), stop=(k == 1))
                            fill(m, key)
                if i == 0:
                    route()
                if i > 0:
                    j = i - 1
                    e = j // 2
                    pe.wait_ge(s_bh, 2 * (j + 1))
                    for c in range(2):
                        o = claim(pe, ("B", "dn", j, c))
                        for q in range(2):
                            for d in range(2):
                                m = pe.matmul(o[:, q * D:q * D + D],
                                              b_h[:, j % 2, d, (2 * c + q) * P:(2 * c + q) * P + P],
                                              b_d[e % NWB][:, d, :], start=(d == 0), stop=(d == 1))
                        fill(m, ("B", "dn", j, c))

        def B_act(act):
            yt_act(act, "B")
            act.wait_ge(s_blg, 1)
            act.activation(b_s[:, :, :], b_lg[:, :, :], ACT.Exp).then_inc(s_bex, 1)
            for i in range(NIT):
                e, w = i // 2, i % 2
                for d in range(2):
                    n = 2 * i + d
                    if n >= 4:
                        act.wait_ge(s_bt, n - 3)
                    have(act, ("B", "gu", i, d, 0))
                    act.activation(b_sg[:, w, d, :], b_g[:, w, d, :], ACT.Sigmoid, scale=1.702).then_inc(s_bsg, 1)
                    if n >= 4:
                        act.wait_ge(s_bh, n - 3)
                    o = take(act, ("B", "gu", i, d, 1))
                    empty(act.activation(b_u[:, w, d, :], o[:, :], ACT.Identity, bias=col("bgu", e * 4 + 2 + d)),
                          ("B", "gu", i, d, 1))

        def B_pool(pool, C):
            for i in range(NIT):
                w = i % 2
                for d in range(2):
                    n = 2 * i + d
                    pool.wait_ge(s_bsg, n + 1)
                    pool.tensor_tensor(b_g[:, w, d, :], b_g[:, w, d, :], b_sg[:, w, d, :], ALU.mult).then_inc(s_bt, 1)
                    have(pool, ("B", "gu", i, d, 1))
                    pool.tensor_scalar(b_u[:, w, d, :], b_u[:, w, d, :], -7.0, 7.0, ALU.max, ALU.min)\
                        .then_inc(s_bu, 1)

        def B_dve(dve, V):
            o = take(dve, ("B", "lg"))
            lgf = b_lg[:, :, :]
            empty(dve.tensor_tensor(lgf, o[:, 0:T * NE].rearrange("p (t e) -> p t e", e=NE),
                                    row("rb").unsqueeze(1).to_broadcast([P, T, NE]), ALU.add), ("B", "lg"))
            V.do(dve.memset(b_z[:, :], 0.0))
            have(dve, ("B", "lg"))
            V.sync()
            for t in range(T):
                V.do(dve.max(out=b_m8[:, t, :], in_=b_lg[:, t, :]))
            V.sync()
            v4 = b_m8[:, :, TOPK - 1:TOPK].to_broadcast([P, T, NE])
            V.do(dve.tensor_tensor(b_gt[:, :, :], lgf, v4, ALU.is_gt))
            V.do(dve.tensor_tensor(b_eq[:, :, :], lgf, v4, ALU.is_equal))
            V.sync()
            for t in range(T):
                V.do(dve.tensor_tensor_scan(b_cs[:, t, :], b_z[:, 0:NE], b_eq[:, t, :], 0.0, ALU.add, ALU.add))
            V.do(dve.tensor_reduce(b_n[:, :], b_gt[:, :, :], AX.X, ALU.add))
            V.sync()
            V.do(dve.tensor_tensor(b_cs[:, :, :], b_cs[:, :, :], b_n[:, :].unsqueeze(2).to_broadcast([P, T, NE]),
                                   ALU.add))
            V.sync()
            V.do(dve.scalar_tensor_tensor(out=b_eq[:, :, :], in0=b_cs[:, :, :], scalar=float(TOPK),
                                          in1=b_eq[:, :, :], op0=ALU.is_le, op1=ALU.mult))
            V.sync()
            V.do(dve.tensor_tensor(b_gt[:, :, :], b_gt[:, :, :], b_eq[:, :, :], ALU.add))
            dve.tensor_tensor(lgf, lgf, b_m8[:, :, 0:1].to_broadcast([P, T, NE]), ALU.subtract).then_inc(s_blg, 1)
            V.sync()
            dve.wait_ge(s_bex, 1)
            V.do(dve.tensor_tensor(b_s[:, :, :], b_s[:, :, :], b_gt[:, :, :], ALU.mult))
            V.sync()
            V.do(dve.tensor_reduce(b_n[:, :], b_s[:, :, :], AX.X, ALU.add))
            V.sync()
            V.do(dve.reciprocal(b_n[:, :], b_n[:, :]))
            V.sync()
            dve.tensor_tensor(b_s[:, :, :], b_s[:, :, :], b_n[:, :].unsqueeze(2).to_broadcast([P, T, NE]),
                              ALU.mult).then_inc(s_bs, 1)

            def gate(i):
                e, w = i // 2, i % 2
                for d in range(2):
                    if i >= 2:
                        dve.wait_ge(s_bh, 2 * (i - 2) + d + 1)
                    o = take(dve, ("B", "gu", i, d, 0))
                    empty(dve.tensor_scalar(b_g[:, w, d, :], o[:, :], col("bgu", e * 4 + d), 7.0,
                                            ALU.add, ALU.min), ("B", "gu", i, d, 0))

            def hidden(i):
                w = i % 2
                for d in range(2):
                    n = 2 * i + d
                    if i >= 2:
                        bk, m = uses[("B", "dn", i - 2, 1)]
                        dve.wait_ge(filled[bk], m + 1)
                    dve.wait_ge(s_bt, n + 1)
                    dve.wait_ge(s_bu, n + 1)
                    dve.scalar_tensor_tensor(out=b_h[:, w, d, :], in0=b_u[:, w, d, :], scalar=1.0,
                                             in1=b_g[:, w, d, :], op0=ALU.add, op1=ALU.mult).then_inc(s_bh, 1)

            def add_out(i):
                e, half = i // 2, i % 2
                for c in range(2):
                    o = take(dve, ("B", "dn", i, c))
                    for q in range(2):
                        t = half * 4 + 2 * c + q
                        m = dve.scalar_tensor_tensor(out=x[:, t, :], in0=o[:, q * D:q * D + D],
                                                     scalar=b_s[:, t, e:e + 1], in1=x[:, t, :],
                                                     op0=ALU.mult, op1=ALU.add)
                        if q == 0:
                            V.do(m)
                    empty(m, ("B", "dn", i, c))

            gate(0)
            for c in range(2):
                o = take(dve, ("B", "sT", c))
                empty(dve.tensor_copy(b_sT[0:NE, c * 512:c * 512 + 512], o[0:NE, :]), ("B", "sT", c))
            for c in range(4):
                o = take(dve, ("B", "bd", c))
                xb = x[:, 2 * c:2 * c + 2, :].rearrange("p t d -> p (t d)")
                empty(dve.tensor_tensor(xb, xb, o[:, :], ALU.add), ("B", "bd", c))
            for c in range(4):
                have(dve, ("B", "bd", c))
            dve.wait_ge(s_bs, 1)
            hidden(0)
            for i in range(1, NIT):
                gate(i)
                if i >= 2:
                    if i >= 3:
                        have(dve, ("B", "dn", i - 3, 1))
                        V.sync()
                    add_out(i - 2)
                hidden(i)
            V.sync()
            add_out(NIT - 2)
            V.sync()
            add_out(NIT - 1)
            have(dve, ("B", "dn", NIT - 1, 0))
            have(dve, ("B", "dn", NIT - 1, 1))

        for c in range(4):
            plan(("C", "qT", c), c)
        for t in range(T):
            plan(("C", "o", t), 4 + t % 4)

        def C_pe(pe):
            pe.wait_ge(s_cb, 1)
            pe.wait_ge(s_cq, 1)
            for c in range(4):
                o = claim(pe, ("C", "qT", c))
                ob = o[:, :].bitcast(BF16)
                for k in range(KD):
                    for h in range(2):
                        m = pe.transpose(ob[:, k * 256 + h * P:k * 256 + h * P + P], c_q[:, 2 * c + h, k, :],
                                         identb[:, :])
                fill(m, ("C", "qT", c))
            for t in range(T):
                o = claim(pe, ("C", "o", t))
                have(pe, ("C", "qT", t // 2))
                for k in range(KD):
                    m = pe.matmul(o[:, k * 256:k * 256 + 256], c_qT[:, k, t * P:t * P + P],
                                  cw_q[:, k, t // 2, :, :].rearrange("p a n -> p (a n)"), start=True, stop=True)
                fill(m, ("C", "o", t))

        def C_act(act):
            for c in range(4):
                o = take(act, ("C", "qT", c))
                empty(act.copy(c_qT[:, :, c * 256:c * 256 + 256],
                               o[:, :].bitcast(BF16)[:, 0:512].rearrange("p (k n) -> p k n", k=KD)), ("C", "qT", c))

        def C_dve(dve, V):
            yb = y[:, :, :].rearrange("p t (k n) -> p (t k) n", k=2)
            flat = "p t k -> p (t k)"
            dve.wait_ge(s_y, 8 * K_C + 8)
            V.do(dve.tensor_reduce(c_ax[:, :, :].rearrange(flat), yb, AX.X, ALU.max, apply_absolute_value=True))
            V.sync()
            V.do(dve.tensor_scalar(c_sx[:, :, :], c_ax[:, :, :], 1e-4, 1.0 / FP8_MAX, ALU.max, ALU.mult))
            V.sync()
            V.do(dve.reciprocal(c_rx[:, :, :], c_sx[:, :, :]))
            V.sync()
            V.do(dve.tensor_tensor(c_v.rearrange("p t k n -> p (t k) n"), yb,
                                   c_rx[:, :, :].rearrange(flat).unsqueeze(2).to_broadcast([P, 16, P]), ALU.mult))
            for t in range(T):
                for k in range(KD):
                    V.do(dve.tensor_scalar(c_c[:, t, k, :], c_sw[:, k, t // 2, :], c_sx[:, t, k:k + 1], None,
                                           ALU.mult))
            V.sync()
            fp8_round(dve, V, c_v.rearrange("p t k n -> p (t k n)"), c_e, c_m,
                      c_q.rearrange("p t k n -> p (t k n)"))
            V.sync()
            dve.tensor_copy(c_ax[:, 0, 0:1], c_sx[:, 0, 0:1]).then_inc(s_cq, 1)
            for t in range(T):
                o = take(dve, ("C", "o", t))
                for k in range(KD):
                    for n in range(2):
                        xs_ = x[:, t, n * P:n * P + P]
                        m = dve.scalar_tensor_tensor(out=xs_, in0=o[:, k * 256 + n * P:k * 256 + n * P + P],
                                                     scalar=c_c[:, t, k, n:n + 1], in1=xs_,
                                                     op0=ALU.mult, op1=ALU.add)
                        if (k, n) != (1, 1):
                            V.do(m)
                    if k == 0:
                        V.sync()
                empty(m, ("C", "o", t))
            for t in range(T):
                have(dve, ("C", "o", t))

        d_reg = Region(14800, 27600)
        d_gw = d_reg.take([KD, INTER])
        d_uw = d_reg.take([KD, INTER])
        d_dw = d_reg.take([NI, D])
        d_h = d_reg.take([NI, 512])
        d_sg = d_reg.take([2, 512])
        d_t = d_reg.take([2, 512])
        d_o = d_reg.take([2, 512])
        s_dw, s_dsg = sem("d_loaded"), sem("d_sig")
        for b in range(B):
            plan(("D", "yt", b), b)
        di = 4
        for half in range(2):
            for it in range(NI):
                for gu in range(2):
                    plan(("D", "gu", half, it, gu), di % 8)
                    di += 1
            for c in range(2):
                plan(("D", "dn", half, c), di % 8)
                di += 1
        rows_of = [P] * (NI - 1) + [INTER - P * (NI - 1)]

        def D_sp(sp):
            sp.dma_start(d_gw, gwT_d).then_inc(s_dw, 16)
            sp.dma_start(d_uw, uwT_d).then_inc(s_dw, 16)
            sp.dma_start(d_dw[:, 0:NI - 1, :], dwT_d[0:(NI - 1) * P, :].rearrange("(i p) d -> p i d", p=P))\
                .then_inc(s_dw, 16)
            sp.dma_start(d_dw[0:rows_of[-1], NI - 1, :], dwT_d[(NI - 1) * P:INTER, :]).then_inc(s_dw, 16)

        def D_pe(pe):
            yt_pe(pe, K_D, "D")
            pe.wait_ge(s_dw, 64)
            for half in range(2):
                have(pe, ("D", "yt", 2 * half))
                have(pe, ("D", "yt", 2 * half + 1))
                for it in range(NI):
                    r = rows_of[it]
                    for gu, w in enumerate((d_gw, d_uw)):
                        key = ("D", "gu", half, it, gu)
                        o = claim(pe, key)
                        for k in range(KD):
                            m = pe.matmul(o[0:r, :], w[:, k, it * P:it * P + r],
                                          yT[:, k, half * 512:half * 512 + 512], start=(k == 0), stop=(k == 1))
                        fill(m, key)
                for c in range(2):
                    key = ("D", "dn", half, c)
                    o = claim(pe, key)
                    pe.wait_ge(emptied[uses[("D", "gu", half, NI - 1, 1)][0]],
                               uses[("D", "gu", half, NI - 1, 1)][1] + 1)
                    for q in range(2):
                        for it in range(NI):
                            r = rows_of[it]
                            m = pe.matmul(o[:, q * D:q * D + D], d_h[0:r, it, (2 * c + q) * P:(2 * c + q) * P + P],
                                          d_dw[0:r, it, :], start=(it == 0), stop=(it == NI - 1))
                    fill(m, key)

        def D_act(act):
            yt_act(act, "D")
            for half in range(2):
                for it in range(NI):
                    n = half * NI + it
                    r = rows_of[it]
                    if n >= 2:
                        have(act, ("D", "gu", (n - 2) // NI, (n - 2) % NI, 0))
                    o = take(act, ("D", "gu", half, it, 0))
                    act.activation(d_sg[0:r, n % 2, :], o[0:r, :], ACT.Sigmoid, scale=col("gs", it, r))\
                        .then_inc(s_dsg, 1)

        def D_dve(dve, V):
            for half in range(2):
                for it in range(NI):
                    n = half * NI + it
                    r = rows_of[it]
                    dve.wait_ge(s_dsg, n + 1)
                    o = take(dve, ("D", "gu", half, it, 0))
                    empty(dve.scalar_tensor_tensor(out=d_t[0:r, n % 2, :], in0=o[0:r, :], scalar=col("gs", it, r),
                                                   in1=d_sg[0:r, n % 2, :], op0=ALU.mult, op1=ALU.mult),
                          ("D", "gu", half, it, 0))
                    have(dve, ("D", "gu", half, it, 0))
                    o = take(dve, ("D", "gu", half, it, 1))
                    if half == 1 and it == 0:
                        bk, m_ = uses[("D", "dn", 0, 1)]
                        dve.wait_ge(filled[bk], m_ + 1)
                    empty(dve.scalar_tensor_tensor(out=d_h[0:r, it, :], in0=o[0:r, :], scalar=col("us", it, r),
                                                   in1=d_t[0:r, n % 2, :], op0=ALU.mult, op1=ALU.mult),
                          ("D", "gu", half, it, 1))
                for c in range(2):
                    key = ("D", "dn", half, c)
                    o = take(dve, key)
                    empty(dve.tensor_tensor(d_o[:, c, :].rearrange("p (q d) -> p q d", q=2),
                                            o[:, :].rearrange("p (q d) -> p q d", q=2),
                                            row("ds").unsqueeze(1).to_broadcast([P, 2, D]), ALU.mult), key)
                    have(dve, key)
                    t = half * 4 + 2 * c
                    xb = x[:, t:t + 2, :].rearrange("p t d -> p (t d)")
                    V.do(dve.tensor_tensor(xb, xb, d_o[:, c, :], ALU.add))

        e_reg = Region(0, 14800)
        e_cm = e_reg.take([8, 256])
        e_v = e_reg.take([T, NH, 32])
        e_sel = e_reg.take([NH, P], BF16)
        e_mp = e_reg.take([T * P], BF16)
        e_wif = e_reg.take([6, 32])
        e_hT = e_reg.take([4, 256])
        e_reg2 = Region(14800, 27600)
        e_i = e_reg2.take([T * P])
        e_f = e_reg2.take([T * P])
        e_l = e_reg2.take([T * P])
        e_F = e_reg2.take([T * P])
        e_M = e_reg2.take([T * P])
        e_D = e_reg2.take([8, 384])
        e_C = e_reg2.take([8, 384])
        e_h = e_reg2.take([2, NH, DH])
        e_q = e_reg2.take([2, NH, DH])
        e_hs = e_l.rearrange("p (q n) -> p q n", q=2)
        e_aT = sb("e_aT", [P, T, NH])
        e_em = sb("e_em", [P, T, NH])
        e_n = sb("e_n", [P, 2, NH])
        e_r = sb("e_r", [P, 2, NH])
        s_eprep, s_wif = sem("e_ctx_prepared"), sem("e_weights_loaded")
        s_e1, s_e2, s_emp, s_eM, s_em, s_eD = (sem("e_absf"), sem("e_log1p"), sem("e_negM_parts"), sem("e_a_and_m"),
                                               sem("e_exp_m"), sem("e_decay"))
        s_ev, s_er = sem("e_head_var"), sem("e_head_rstd")
        NB = B * NH
        for b in range(B):
            plan(("E", "yt", b), b)
        for half in range(2):
            for gi_ in range(2):
                plan(("E", "g", half, gi_), 4 + 2 * half + gi_)
        plan(("E", "tr"), 0)
        NQ = NB // 4

        def head(n):
            b, quad, i = n // NH, n % NH // 4, n % 4
            return b, 8 * (quad // 2) + 2 * i + quad % 2, i

        ld_bank = 1
        for s_ in range(NQ + 3):
            if s_ < NQ:
                for i in range(4):
                    plan(("E", "ld", 4 * s_ + i), ld_bank)
                    ld_bank ^= 1
                for i in range(4):
                    plan(("E", "qk", 4 * s_ + i), 2 + i)
            if s_ >= 6 and s_ % 4 == 2:
                for q in range(2):
                    plan(("E", "hv", s_ // 4 - 1, q), ld_bank)
                    ld_bank ^= 1
            if 1 <= s_ <= NQ and (s_ - 1) % 2 == 0:
                plan(("E", "hT", (s_ - 1) // 2), 6 + (s_ - 1) // 2 % 2)

        def E_sp(sp):
            sp.wait_ge(s_stage, 2)
            sp.dma_start(e_wif, wif_d).then_inc(s_wif, 16)

        def E_prep_pool(pool, C):
            pool.wait_ge(s_stage, 2)
            C.do(pool.memset(e_v, 1.0))
            C.do(pool.memset(e_mp, 0.0))
            C.sync()
            for t in range(T):
                C.do(pool.tensor_copy(e_v[:, t, :, 0:DH], cx[:, t, :].rearrange("p (h c) -> p h c", c=DH)))
            pool.tensor_copy(e_sel[0:96, :, :], cst[0:96, 296:312].unsqueeze(2).to_broadcast([96, NH, P]))\
                .then_inc(s_eprep, 1)

        def E_pe(pe):
            yt_pe(pe, K_E, "E")
            pe.wait_ge(s_wif, 16)
            for half in range(2):
                have(pe, ("E", "yt", 2 * half))
                have(pe, ("E", "yt", 2 * half + 1))
                for gi_ in range(2):
                    o = claim(pe, ("E", "g", half, gi_))
                    for k in range(6):
                        src = yT[:, k, :] if k < KD else cxT[:, k % KD, :]
                        m = pe.matmul(o[0:NH, :], e_wif[:, k, gi_ * NH:gi_ * NH + NH],
                                      src[:, half * 512:half * 512 + 512], start=(k == 0), stop=(k == 5))
                    fill(m, ("E", "g", half, gi_))
            o = claim(pe, ("E", "tr"))
            pe.wait_ge(s_eM, 1)
            for w, src in enumerate((e_i, e_f)):
                for t in range(T):
                    m = pe.transpose(o[:, (w * T + t) * NH:(w * T + t) * NH + NH], src[0:NH, t * P:t * P + P],
                                     ident[0:NH, 0:NH])
            fill(m, ("E", "tr"))
            pe.wait_ge(s_emp, 1)
            pe.wait_ge(s_eprep, 1)
            for s_ in range(NQ + 3):
                if s_ < NQ:
                    for n2 in (4 * s_, 4 * s_ + 2):
                        for n in (n2, n2 + 1):
                            b, h, _ = head(n)
                            o = claim(pe, ("E", "ld", n))
                            pe.matmul(o[:, 0:256], e_sel[0:96, h, :], e_mp[0:96, b * 256:b * 256 + 256],
                                      start=True, stop=False, skip_group_check=True)
                            pe.matmul(o[:, 256:384], e_sel[0:96, h, :], e_mp[0:96, b * 256 + P:b * 256 + 256],
                                      start=False, stop=False, skip_group_check=True)
                            pe.matmul(o[:, 0:P], identb[:, :], causal[:, :], start=False, stop=False,
                                      skip_group_check=True)
                            fill(pe.matmul(o[:, 256:384], identb[:, :], causal[:, :], start=False, stop=True,
                                           skip_group_check=True), ("E", "ld", n))
                        for n in (n2, n2 + 1):
                            b, h, _ = head(n)
                            o = claim(pe, ("E", "qk", n))
                            pe.wait_ge(s_ecm, n + 1)
                            for tb in range(2):
                                m = pe.matmul(o[:, 256 * tb:256 * tb + 256 - P * tb], e_cm[:, n % 8, tb * P:tb * P + P],
                                              yT[:, h // 8, b * 256 + tb * P:b * 256 + 256], start=True, stop=True)
                            fill(m, ("E", "qk", n))
                if s_ >= 6 and s_ % 4 == 2:
                    b = s_ // 4 - 1
                    have(pe, ("E", "hT", 2 * b))
                    have(pe, ("E", "hT", 2 * b + 1))
                    for q in range(2):
                        o = claim(pe, ("E", "hv", b, q))
                        for gr in range(4):
                            m = pe.transpose(o[:, gr * P:gr * P + P], e_hT[:, gr, q * P:q * P + P], ident)
                        fill(m, ("E", "hv", b, q))
                if 1 <= s_ <= NQ:
                    c, odd = (s_ - 1) // 2, (s_ - 1) % 2
                    o = psum[uses[("E", "hT", c)][0]]
                    if not odd:
                        claim(pe, ("E", "hT", c))
                    for tb in range(2):
                        for j in range(4 * s_ - 4, 4 * s_):
                            b, h, i = head(j)
                            if tb == 0:
                                have(pe, ("E", "qk", j))
                            r, c0 = 32 * i, 256 * odd
                            m = pe.matmul(o[r:r + 32, c0 + tb * P:c0 + 256], e_v[:, 2 * b + tb, h, :],
                                          e_C[:, j % 8, 256 * tb:256 * tb + 256 - P * tb],
                                          start=(tb == 0), stop=(tb == 1))
                    if odd:
                        fill(m, ("E", "hT", c))
                    else:
                        m.then_inc(s_ehv, 1)

        s_ehv, s_ecm = sem("e_quad_used"), sem("e_ctx_masked")

        def used_C(eng, quad):
            if quad % 2:
                take(eng, ("E", "hT", quad // 2))
            else:
                eng.wait_ge(s_ehv, quad // 2 + 1)

        def E_act(act):
            yt_act(act, "E")
            act.wait_ge(s_e1, 1)
            act.activation(e_l[0:NH, :], e_l[0:NH, :], ACT.Exp, scale=-1.0).then_inc(s_e2, 1)
            act.wait_ge(s_e2, 1)
            act.activation(e_l[0:NH, :], e_l[0:NH, :], ACT.Ln, bias=1.0).then_inc(s_e2, 1)
            o = take(act, ("E", "tr"))
            act.wait_ge(s_em, 1)
            empty(act.activation(e_em[:, :, :], o[:, P:256].rearrange("p (t h) -> p t h", h=NH), ACT.Exp,
                                 scale=-1.0), ("E", "tr"))
            for s_ in range(NQ + 3):
                if s_ < NQ:
                    for n in range(4 * s_, 4 * s_ + 4):
                        b, h, _ = head(n)
                        if n >= 8:
                            have(act, ("E", "qk", n - 8))
                        o = take(act, ("E", "ld", n))
                        act.activation(e_D[:, n % 8, 0:256], o[:, 0:256], ACT.Exp, bias=e_aT[:, 2 * b, h:h + 1])
                        empty(act.activation(e_D[:, n % 8, 256:384], o[:, 256:384], ACT.Exp,
                                             bias=e_aT[:, 2 * b + 1, h:h + 1]), ("E", "ld", n))
                if s_ >= 3 and s_ % 2 == 1 and (s_ - 3) // 2 < 2 * B:
                    c = (s_ - 3) // 2
                    if c >= 2:
                        take(act, ("E", "hv", c // 2 - 1, 1))
                    o = take(act, ("E", "hT", c))
                    empty(act.copy(e_hT[:, 2 * (c % 2):2 * (c % 2) + 2, :],
                                   o[:, :].rearrange("p (g s) -> p g s", g=2)), ("E", "hT", c))
                if s_ >= 6 and s_ % 4 == 2:
                    b = s_ // 4 - 1
                    if b >= 1:
                        act.wait_ge(s_ev, b)
                    for q in range(2):
                        o = take(act, ("E", "hv", b, q))
                        for k in range(2):
                            m = act.copy(e_hs[:, q, k * 256:k * 256 + 256].rearrange("p (i r c) -> p i r c", i=4, r=2),
                                         o[:, k * 256:k * 256 + 256].rearrange("p (r i c) -> p i r c", r=2, i=4))
                        empty(m, ("E", "hv", b, q))

        def E_dve(dve, V):
            def mask_ctx(quad):
                for n in range(4 * quad, 4 * quad + 4):
                    b, h, _ = head(n)
                    dve.tensor_scalar(e_cm[:, n % 8, :], cxT[:, h // 8, b * 256:b * 256 + 256],
                                      cst[:, 256 + h % 8:257 + h % 8], None, ALU.mult).then_inc(s_ecm, 1)

            mask_ctx(0)
            mask_ctx(1)
            h16 = slice(0, NH)
            for half in range(2):
                hs = slice(half * 512, half * 512 + 512)
                for gi_, (dst, bias) in enumerate(((e_i, "bi"), (e_f, "bf"))):
                    o = take(dve, ("E", "g", half, gi_))
                    empty(dve.tensor_scalar(dst[h16, hs], o[h16, :], col(bias, 0, NH), None, ALU.add),
                          ("E", "g", half, gi_))
            for half in range(2):
                have(dve, ("E", "g", half, 0))
                have(dve, ("E", "g", half, 1))
            dve.scalar_tensor_tensor(out=e_l[h16, :], in0=e_f[h16, :], scalar=-1.0, in1=e_f[h16, :],
                                     op0=ALU.mult, op1=ALU.max).then_inc(s_e1, 1)
            dve.wait_ge(s_e2, 2)
            V.do(dve.scalar_tensor_tensor(out=e_l[h16, :], in0=e_f[h16, :], scalar=0.0, in1=e_l[h16, :],
                                          op0=ALU.min, op1=ALU.subtract))
            V.sync()
            for b in range(B):
                bs = slice(b * 256, b * 256 + 256)
                V.do(dve.tensor_tensor_scan(e_F[h16, bs], b_z[h16, :], e_l[h16, bs], 0.0, ALU.add, ALU.add))
            V.sync()
            V.do(dve.tensor_tensor(e_i[h16, :], e_i[h16, :], e_F[h16, :], ALU.subtract))
            V.sync()
            for b in range(B):
                bs = slice(b * 256, b * 256 + 256)
                V.do(dve.tensor_tensor_scan(e_M[h16, bs], e_i[h16, bs], e_i[h16, bs], -3e38, ALU.max, ALU.max))
            V.sync()
            dve.tensor_tensor(e_f[h16, :], e_F[h16, :], e_M[h16, :], ALU.add).then_inc(s_eM, 1)
            dve.wait_ge(s_eprep, 1)
            V.do(dve.tensor_scalar(e_mp[0:NH, :], e_M[h16, :], -1.0, None, ALU.mult))
            V.sync()
            V.do(dve.scalar_tensor_tensor(out=e_l[h16, :], in0=e_M[h16, :], scalar=-1.0, in1=e_mp[0:NH, :],
                                          op0=ALU.mult, op1=ALU.subtract))
            V.sync()
            V.do(dve.tensor_copy(e_mp[32:32 + NH, :], e_l[h16, :]))
            V.do(dve.tensor_copy(e_F[h16, :].bitcast(BF16)[:, 0:T * P], e_l[h16, :]))
            V.sync()
            V.do(dve.tensor_tensor(e_l[h16, :], e_l[h16, :], e_F[h16, :].bitcast(BF16)[:, 0:T * P], ALU.subtract))
            V.sync()
            dve.tensor_copy(e_mp[64:64 + NH, :], e_l[h16, :]).then_inc(s_emp, 1)
            o = take(dve, ("E", "tr"))
            dve.tensor_copy(e_aT[:, :, :], o[:, 0:P].rearrange("p (t h) -> p t h", h=NH)).then_inc(s_em, 1)
            have(dve, ("E", "tr"))

            def post_a(b):
                have(dve, ("E", "hv", b, 0))
                have(dve, ("E", "hv", b, 1))
                hv = e_hs.rearrange("p q (h c) -> p q h c", c=32)
                V.do(dve.scalar_tensor_tensor(out=e_n[:, :, :], in0=hv[:, :, :, DH], scalar=-1.0,
                                              in1=e_em[:, 2 * b:2 * b + 2, :], op0=ALU.mult, op1=ALU.max))
                V.sync()
                V.do(dve.tensor_tensor(e_n[:, :, :], hv[:, :, :, DH], e_n[:, :, :], ALU.max))
                V.sync()
                V.do(dve.tensor_scalar(e_n[:, :, :], e_n[:, :, :], 1e-6, None, ALU.add))
                V.sync()
                V.do(dve.reciprocal(e_n[:, :, :], e_n[:, :, :]))
                V.sync()
                for q in range(2):
                    V.do(dve.tensor_tensor(e_h[:, q, :, :], hv[:, q, :, 0:DH],
                                           e_n[:, q, :].unsqueeze(2).to_broadcast([P, NH, DH]), ALU.mult))
                V.sync()
                hf = e_h.rearrange("p q h c -> p (q h) c")
                qf = e_q.rearrange("p q h c -> p (q h) c")
                nf = e_n[:, :, :].rearrange("p q h -> p (q h)")
                V.do(dve.tensor_reduce(nf, hf, AX.X, ALU.add))
                V.sync()
                V.do(dve.tensor_scalar(nf, nf, 1.0 / DH, None, ALU.mult))
                V.sync()
                V.do(dve.tensor_tensor(hf, hf, nf.unsqueeze(2).to_broadcast([P, 2 * NH, DH]), ALU.subtract))
                V.sync()
                V.do(dve.tensor_tensor(qf, hf, hf, ALU.mult))
                V.sync()
                dve.tensor_reduce(e_r[:, :, :].rearrange("p q h -> p (q h)"), qf, AX.X, ALU.add).then_inc(s_ev, 1)

            def post_b(b):
                dve.wait_ge(s_er, b + 1)
                hf = e_h.rearrange("p q h c -> p (q h) c")
                V.do(dve.tensor_tensor(hf, hf, e_r[:, :, :].rearrange("p q h -> p (q h)").unsqueeze(2)
                                       .to_broadcast([P, 2 * NH, DH]), ALU.mult))
                V.sync()
                h2 = e_h.rearrange("p q h c -> p q (h c)")
                V.do(dve.tensor_tensor(h2, h2, row("lns").unsqueeze(1).to_broadcast([P, 2, D]), ALU.mult))
                V.sync()
                V.do(dve.tensor_tensor(x[:, 2 * b:2 * b + 2, :], x[:, 2 * b:2 * b + 2, :], h2, ALU.add))

            for s_ in range(NQ + 6):
                if s_ < NQ:
                    if s_ >= 2:
                        used_C(dve, s_ - 2)
                    for n in range(4 * s_, 4 * s_ + 4):
                        have(dve, ("E", "ld", n))
                        o = take(dve, ("E", "qk", n))
                        empty(dve.scalar_tensor_tensor(out=e_C[:, n % 8, :], in0=o[:, 0:384], scalar=0.25,
                                                       in1=e_D[:, n % 8, :], op0=ALU.mult, op1=ALU.mult),
                              ("E", "qk", n))
                if s_ + 2 < NQ:
                    mask_ctx(s_ + 2)
                if s_ >= 7 and s_ % 4 == 3:
                    post_a(s_ // 4 - 1)
                if s_ >= 9 and s_ % 4 == 1:
                    post_b(s_ // 4 - 2)

        def E_pool(pool, C):
            for b in range(B):
                pool.wait_ge(s_ev, b + 1)
                C.do(pool.tensor_scalar(e_r[:, :, :], e_r[:, :, :], 1.0 / DH, 1e-6, ALU.mult, ALU.add))
                C.sync()
                pool.tensor_tensor(e_r[:, :, :].rearrange("p q h -> p (q h)"),
                                   e_r[:, :, :].rearrange("p q h -> p (q h)"), mhalf32[:, :], ALU.pow)\
                    .then_inc(s_er, 1)

        f_reg = Region(0, 14800)
        f_w = f_reg.take([KD, D])
        f_wq = f_reg.take([KD, D], BF16)
        f_v = f_reg.take([T, D])
        f_q = f_reg.take([T, D], BF16)
        f_qT = f_reg.take([KD, T * P], BF16)
        f_al = sb("f_al", [P, 4])
        f_s = sb("f_s", [P, 3, T])
        s_fw, s_fa, s_far, s_fq = sem("f_loaded"), sem("f_abs_sum"), sem("f_abs_all"), sem("f_quantised")
        for c in range(4):
            plan(("F", "qT", c), c)
        for c in range(4):
            plan(("F", "o", c), 4 + c)

        def F_sp(sp):
            sp.wait_ge(s_stage, 5)
            sp.dma_start(f_w, w2T_d).then_inc(s_fw, 16)

        def F_pool(pool, C):
            pool.wait_ge(s_fa, 1)
            pool.partition_all_reduce(f_al[:, 1:2], f_al[:, 0:1], P, RADD).then_inc(s_far, 1)

        def F_pe(pe):
            pe.wait_ge(s_fq, 1)
            for c in range(4):
                o = claim(pe, ("F", "qT", c))
                ob = o[:, :].bitcast(BF16)
                for k in range(KD):
                    for h in range(2):
                        m = pe.transpose(ob[:, k * 256 + h * P:k * 256 + h * P + P],
                                         f_q[:, 2 * c + h, k * P:k * P + P], identb[:, :])
                fill(m, ("F", "qT", c))
            for c in range(4):
                o = claim(pe, ("F", "o", c))
                have(pe, ("F", "qT", c))
                for h in range(2):
                    t = 2 * c + h
                    for k in range(KD):
                        m = pe.matmul(o[:, h * D:h * D + D], f_qT[:, k, t * P:t * P + P], f_wq[:, k, :],
                                      start=(k == 0), stop=(k == 1))
                fill(m, ("F", "o", c))

        def F_act(act):
            for c in range(4):
                o = take(act, ("F", "qT", c))
                empty(act.copy(f_qT[:, :, c * 256:c * 256 + 256],
                               o[:, :].bitcast(BF16)[:, 0:512].rearrange("p (k n) -> p k n", k=KD)), ("F", "qT", c))

        def F_dve(dve, V):
            dve.wait_ge(s_fw, 16)
            wf = f_w.rearrange("p k d -> p (k d)")
            dve.tensor_reduce(f_al[:, 0:1], wf, AX.X, ALU.add, apply_absolute_value=True).then_inc(s_fa, 1)
            dve.wait_ge(s_y, 8 * K_F + 8)
            V.do(dve.tensor_tensor(x[:, :, :], x[:, :, :], row("b2f").unsqueeze(1).to_broadcast([P, T, D]), ALU.add))
            V.do(dve.tensor_reduce(f_s[:, 0, :], y[:, :, :], AX.X, ALU.max, apply_absolute_value=True))
            V.sync()
            V.do(dve.tensor_scalar(f_s[:, 0, :], f_s[:, 0, :], 1e-5, 1.0 / 127.0, ALU.max, ALU.mult))
            V.sync()
            V.do(dve.reciprocal(f_s[:, 1, :], f_s[:, 0, :]))
            V.sync()
            for t in range(T):
                V.do(dve.tensor_scalar(f_v[:, t, :], y[:, t, :], f_s[:, 1, t:t + 1], ROUND23, ALU.mult, ALU.add))
            V.sync()
            V.do(dve.tensor_scalar(f_v, f_v, ROUND23, -128.0, ALU.subtract, ALU.max))
            V.sync()
            V.do(dve.tensor_scalar(f_q, f_v, 127.0, None, ALU.min))
            dve.wait_ge(s_far, 1)
            V.do(dve.tensor_scalar(f_al[:, 2:3], f_al[:, 1:2], 1.0 / (D * D), 1e-5, ALU.mult, ALU.max))
            V.sync()
            V.do(dve.reciprocal(f_al[:, 3:4], f_al[:, 2:3]))
            V.do(dve.tensor_scalar(f_s[:, 2, :], f_s[:, 0, :], f_al[:, 2:3], None, ALU.mult))
            V.sync()
            V.do(dve.tensor_scalar(wf, wf, f_al[:, 3:4], ROUND23, ALU.mult, ALU.add))
            V.sync()
            V.do(dve.tensor_scalar(wf, wf, ROUND23, -1.0, ALU.subtract, ALU.max))
            V.sync()
            dve.tensor_scalar(f_wq.rearrange("p k d -> p (k d)"), wf, 1.0, None, ALU.min).then_inc(s_fq, 1)
            for c in range(4):
                o = take(dve, ("F", "o", c))
                for h in range(2):
                    t = 2 * c + h
                    m = dve.scalar_tensor_tensor(out=x[:, t, :], in0=o[:, h * D:h * D + D], scalar=f_s[:, 2, t:t + 1],
                                                 in1=x[:, t, :], op0=ALU.mult, op1=ALU.add)
                    if h == 0:
                        V.do(m)
                empty(m, ("F", "o", c))
            for c in range(4):
                have(dve, ("F", "o", c))

        NG = G * B
        SCALE = float(HD) ** -0.5
        g_reg = Region(0, 30856)
        g_xs = [g_reg.take([KD, T * P]) for _ in range(4)]
        g_at = g_reg.at
        g_tmp = [g_reg.take([KD, T * P]) for _ in range(2)]
        g_vb = g_reg.take([KD, T * P], BF16)
        g_eb = g_reg.take([KD * T * P], BF16)
        g_mb = g_reg.take([KD, T * P], BF16)
        g_reg.at = g_at
        g_n = [g_reg.take([12, P]) for _ in range(2)]
        g_t = [g_reg.take([6, 256]) for _ in range(2)]
        g_v = [g_reg.take([2, 2, P]) for _ in range(3)]
        g_p = [g_reg.take([4, 2, 256]) for _ in range(2)]
        g_pt = g_reg.take([4, 2, 256])
        g_o = [g_reg.take([4, 256]) for _ in range(2)]
        g_ob = g_reg.take([4 * 256], BF16)
        g_oe = g_reg.take([4 * 256], BF16)
        g_om = [g_reg.take([4 * 256], BF16) for _ in range(2)]
        g_c = [g_reg.take([4, 256]) for _ in range(2)]
        w_reg = Region(30856, 37000)
        g_w = [w_reg.take([KD, 1024]) for _ in range(2)]
        g_wp = [w_reg.take([4, D]) for _ in range(2)]
        g_rc = sb("g_rc", [P, 8])
        g_rsm = sb("g_rsm", [P, 32])
        g_bs = sb("g_bs", [P, 12, 6])
        g_mv = [sb(f"g_mv{i}", [P, 12, 2]) for i in range(2)]
        g_rs = [sb(f"g_rs{i}", [P, 12]) for i in range(2)]
        g_w1 = sb("g_w1", [P, 12])
        g_w2 = sb("g_w2", [P, 12])
        g_pc = sb("g_pc", [P, 1])
        g_mx = [sb(f"g_mx{i}", [P, 8]) for i in range(2)]
        g_sm = [sb(f"g_sm{i}", [P, 8]) for i in range(2)]
        s_gw = [sem(f"g_loaded{i}") for i in range(2)]
        g_nb = [sb(f"g_nb{i}", [P, 12]) for i in range(2)]
        s_gri = sem("g_reciprocal_sums")
        s_gk, s_gv1, s_gq, s_gx = sem("g_consts"), sem("g_scaled"), sem("g_rounded"), sem("g_inputs")
        s_gst, s_grs, s_gva, s_gnb, s_gp, s_gt, s_gc, s_gex = (
            sem("g_stats"), sem("g_rstd"), sem("g_values"), sem("g_bias"), sem("g_probs"), sem("g_magic_sum"),
            sem("g_cat"), sem("g_exps"))
        for b in range(B):
            plan(("G", "yt", b), b)
        gb = [4]
        NPT = 2

        def nxt(key):
            plan(key, gb[0] % 8)
            gb[0] += 1

        for i in range(NG + 3):
            if 0 <= i - 2 < NG:
                for c in range(NPT):
                    nxt(("G", "pt", i - 2, c))
            if 0 <= i - 1 < NG:
                for c in range(3):
                    nxt(("G", "tr", i - 1, c))
            if 0 <= i - 2 < NG:
                for c in range(NPT, 4):
                    nxt(("G", "pt", i - 2, c))
            if 0 <= i - 1 < NG:
                for c in range(4):
                    nxt(("G", "sc", i - 1, c))
            if i < NG:
                for c in range(4):
                    nxt(("G", "qkv", i, c))
            if 0 <= i - 2 < NG:
                for c in range(2):
                    nxt(("G", "pv", i - 2, c))
            if 0 <= i - 3 < NG:
                nxt(("G", "pj", i - 3))

        def G_sp(sp):
            sp.wait_ge(s_stage, 3)
            for g in range(G):
                if g >= 2:
                    take(sp, ("G", "pj", 4 * (g - 2) + 3))
                sp.dma_start(g_w[g % 2], wg_d[g]).then_inc(s_gw[g % 2], 16)
                sp.dma_start(g_wp[g % 2], wp_d[g]).then_inc(s_gw[g % 2], 16)

        def G_pt(pe, j, slots):
            for c in slots:
                o = claim(pe, ("G", "pt", j, c))
                for kt in range(2):
                    for st in range(2):
                        m = pe.transpose(o[:, kt * 256 + st * P:kt * 256 + st * P + P],
                                         g_p[j % 2][:, c, st, kt * P:kt * P + P], ident)
                fill(m, ("G", "pt", j, c))

        def G_pe(pe):
            for b in range(B):
                o = claim(pe, ("G", "yt", b))
                pe.wait_ge(s_y, 8 * K_G2 + 2 * b + 2)
                for d in range(KD):
                    for h in range(2):
                        m = pe.transpose(o[:, d * 256 + h * P:d * 256 + h * P + P],
                                         y[:, 2 * b + h, d * P:d * P + P], ident)
                fill(m, ("G", "yt", b))
            pe.wait_ge(s_gx, 8)
            for i in range(NG + 3):
                if 0 <= i - 2 < NG:
                    pe.wait_ge(s_gp, i - 1)
                    G_pt(pe, i - 2, range(NPT))
                if 0 <= i - 1 < NG:
                    j = i - 1
                    for c, hs in enumerate(((0, 1), (2, 3), (4, 5))):
                        o = claim(pe, ("G", "tr", j, c))
                        if c == 0:
                            for q in range(4):
                                have(pe, ("G", "qkv", j, q))
                        for q, h in enumerate(hs):
                            for tt in range(2):
                                m = pe.transpose(o[:, q * 256 + tt * P:q * 256 + tt * P + P],
                                                 g_n[j % 2][:, tt * 6 + h, :], ident)
                        fill(m, ("G", "tr", j, c))
                if 0 <= i - 2 < NG:
                    G_pt(pe, i - 2, range(NPT, 4))
                if 0 <= i - 1 < NG:
                    j = i - 1
                    for c in range(4):
                        o = claim(pe, ("G", "sc", j, c))
                        have(pe, ("G", "tr", j, c // 2))
                        have(pe, ("G", "tr", j, 2))
                        for st in range(2):
                            m = pe.matmul(o[:, st * 256:st * 256 + 256], g_t[j % 2][:, c, st * P:st * P + P],
                                          g_t[j % 2][:, 4 + c // 2, :], start=True, stop=True)
                        fill(m, ("G", "sc", j, c))
                if i < NG:
                    g, b = i // B, i % B
                    if b == 0:
                        pe.wait_ge(s_gw[g % 2], 32 * (g // 2 + 1))
                    w = g_w[g % 2]
                    for tt in range(2):
                        ts_ = slice(b * 256 + tt * P, b * 256 + tt * P + P)
                        o = claim(pe, ("G", "qkv", i, tt))
                        for v, c0 in ((0, 0), (1, 256)):
                            for k in range(KD):
                                m = pe.matmul(o[:, c0:c0 + 256], g_xs[v][:, k, ts_], w[:, k, c0:c0 + 256],
                                              start=(k == 0), stop=(k == 1))
                        fill(m, ("G", "qkv", i, tt))
                    for tt in range(2):
                        ts_ = slice(b * 256 + tt * P, b * 256 + tt * P + P)
                        o = claim(pe, ("G", "qkv", i, 2 + tt))
                        for src, c0, cw in ((g_xs[2], 512, P), (g_xs[3], 640, P), (cxT, 768, 256)):
                            for k in range(KD):
                                m = pe.matmul(o[:, c0 - 512:c0 - 512 + cw], src[:, k, ts_], w[:, k, c0:c0 + cw],
                                              start=(k == 0), stop=(k == 1))
                        fill(m, ("G", "qkv", i, 2 + tt))
                if 0 <= i - 2 < NG:
                    j = i - 2
                    for a in range(2):
                        o = claim(pe, ("G", "pv", j, a))
                        for q in range(2):
                            have(pe, ("G", "pt", j, 2 * a + q))
                            for kt in range(2):
                                m = pe.matmul(o[:, q * 256:q * 256 + 256], g_v[j % 3][:, kt, a, :],
                                              g_pt[:, 2 * a + q, kt, :], start=(kt == 0), stop=(kt == 1))
                        fill(m, ("G", "pv", j, a))
                if 0 <= i - 3 < NG:
                    j = i - 3
                    o = claim(pe, ("G", "pj", j))
                    pe.wait_ge(s_gc, j + 1)
                    for st in range(2):
                        for c in range(4):
                            m = pe.matmul(o[:, st * D:st * D + D], g_c[j % 2][:, c, st * P:st * P + P],
                                          g_wp[j // B % 2][:, c, :], start=(c == 0), stop=(c == 3))
                    fill(m, ("G", "pj", j))

        names = ("q", "qx", "k", "v")

        G_PT_ACT = ((0,), (3,))
        G_PT_DVE = (1, 2)

        def G_pt_act(act, j, c):
            o = take(act, ("G", "pt", j, c))
            empty(act.copy(g_pt[:, c, :, :], o[:, :].rearrange("p (k s) -> p k s", k=2)), ("G", "pt", j, c))

        def G_act(act):
            for b in range(B):
                o = take(act, ("G", "yt", b))
                for d in range(KD):
                    m = act.activation(yT[:, d, b * 256:b * 256 + 256], o[:, d * 256:d * 256 + 256], ACT.Identity,
                                       scale=col("lnw", d), bias=col("lnb", d))
                empty(m, ("G", "yt", b))
            for b in range(B):
                have(act, ("G", "yt", b))
            act.wait_ge(s_gk, 1)
            for v in range(5):
                if v < 4:
                    if v >= 2:
                        act.wait_ge(s_gx, 2 * (v - 1))
                    for d in range(KD):
                        act.activation(g_tmp[v % 2][:, d, :], yT[:, d, :], ACT.Identity,
                                       scale=g_rc[:, 2 * v + d:2 * v + d + 1]).then_inc(s_gv1, 1)
                if v >= 1:
                    act.wait_ge(s_gq, v)
                    for d in range(KD):
                        act.activation(g_xs[v - 1][:, d, :], g_tmp[(v - 1) % 2][:, d, :], ACT.Identity,
                                       scale=col("sc_" + names[v - 1], d)).then_inc(s_gx, 1)
            act.wait_ge(s_gx, 8)
            for i in range(NG + 3):
                if 0 <= i - 2 < NG:
                    if i >= 3:
                        take(act, ("G", "pv", i - 3, 1))
                    for c in G_PT_ACT[0]:
                        G_pt_act(act, i - 2, c)
                if 0 <= i - 1 < NG:
                    j = i - 1
                    if j >= 2:
                        take(act, ("G", "sc", j - 2, 3))
                    for c, w_ in ((0, "q"), (1, "qx")):
                        o = take(act, ("G", "tr", j, c))
                        empty(act.activation(g_t[j % 2][:, 2 * c:2 * c + 2, :],
                                             o[:, :].rearrange("p (q s) -> p q s", q=2),
                                             ACT.Identity, scale=col(w_ + "w"), bias=col(w_ + "b")), ("G", "tr", j, c))
                    o = take(act, ("G", "tr", j, 2))
                    act.activation(g_t[j % 2][:, 4, :], o[:, 0:256], ACT.Identity, scale=col("kw"), bias=col("kb"))
                    empty(act.activation(g_t[j % 2][:, 5, :], o[:, 256:512], ACT.Identity, scale=col("kxw"),
                                         bias=col("kxb")), ("G", "tr", j, 2))
                if 0 <= i - 2 < NG:
                    for c in G_PT_ACT[1]:
                        G_pt_act(act, i - 2, c)
                if 0 <= i - 1 < NG:
                    j = i - 1
                    if j >= 2:
                        take(act, ("G", "pt", j - 2, 3))
                    for c in range(4):
                        act.wait_ge(s_gnb, 4 * j + c + 1)
                        o = psum[uses[("G", "sc", j, c)][0]]
                        for st in range(2):
                            m = act.activation(g_p[j % 2][:, c, st, :], o[:, st * 256:st * 256 + 256], ACT.Exp,
                                               scale=SCALE, bias=g_mx[j % 2][:, 2 * c + st:2 * c + st + 1],
                                               accum_out=g_sm[j % 2][:, 2 * c + st:2 * c + st + 1])
                        empty(m, ("G", "sc", j, c))
                if i < NG:
                    if i >= 3:
                        take(act, ("G", "pv", i - 3, 1))
                    for tt in range(2):
                        o = take(act, ("G", "qkv", i, 2 + tt))
                        act.activation(g_v[i % 3][:, tt, 0, :], o[:, P:2 * P], ACT.Identity, scale=row("s_v"))
                        act.copy(g_v[i % 3][:, tt, 1, :], o[:, 3 * P:4 * P]).then_inc(s_gva, 1)
                if i < NG:
                    act.wait_ge(s_grs, i + 1)
                    if i >= 2:
                        take(act, ("G", "tr", i - 2, 2))
                    for tt in range(2):
                        o = psum[uses[("G", "qkv", i, 2 + tt)][0]]
                        for h, a0 in ((4, 0), (5, 256)):
                            s_ = tt * 6 + h
                            m = act.activation(g_n[i % 2][:, s_, :], o[:, a0:a0 + P], ACT.Identity,
                                               scale=g_rs[i % 2][:, s_:s_ + 1], bias=g_nb[i % 2][:, s_:s_ + 1])
                        empty(m, ("G", "qkv", i, 2 + tt))
                if 0 <= i - 2 < NG:
                    j = i - 2
                    if j >= 2:
                        act.wait_ge(s_gc, j - 1)
                    for a in range(2):
                        o = take(act, ("G", "pv", j, a))
                        for q in range(2):
                            f = a * 16 + 2 * (j // B) + q
                            m = act.activation(g_o[j % 2][:, 2 * a + q, :], o[:, q * 256:q * 256 + 256], ACT.Identity,
                                               scale=g_rsm[:, f:f + 1])
                        empty(m, ("G", "pv", j, a))

        def G_dve(dve, V):
            ln_dve(dve, V, K_G2, y, EPS, after=8 * K_G + 8)
            c0 = COLS["sc_q"][0]
            V.do(dve.reciprocal(g_rc[:, :], cols[:, c0:c0 + 8]))
            V.do(dve.reciprocal(g_rsm[:, :], cols[:, COLS["smooth"][0]:COLS["smooth"][1]]))
            V.do(dve.tensor_tensor(g_pc[:, :], row("s_pw"), row("s_pi"), ALU.mult))
            V.do(dve.memset(g_w1[:, :], 1.0))
            V.sync()
            for tt in range(2):
                for s_, n in ((0, "s_q"), (1, "s_q"), (2, "s_qx"), (3, "s_qx"), (4, "s_k")):
                    V.do(dve.tensor_copy(g_w1[:, tt * 6 + s_:tt * 6 + s_ + 1], row(n)))
            V.sync()
            V.do(dve.tensor_tensor(g_w2[:, :], g_w1[:, :], g_w1[:, :], ALU.mult))
            V.sync()
            V.do(dve.reciprocal(g_w2[:, :], g_w2[:, :]))
            V.sync()
            dve.tensor_scalar(g_w2[:, :], g_w2[:, :], EPS, None, ALU.mult).then_inc(s_gk, 1)
            flat = "p k n -> p (k n)"
            for v in range(4):
                dve.wait_ge(s_gv1, 2 * (v + 1))
                tmp, vb, mb = g_tmp[v % 2].rearrange(flat), g_vb.rearrange(flat), g_mb.rearrange(flat)
                V.do(dve.tensor_scalar(vb, tmp, FP8_MAX, -FP8_MAX, ALU.min, ALU.max))
                V.sync()
                V.do(dve.tensor_scalar(g_eb.bitcast(U16), vb.bitcast(U16), 0x7F80, None, ALU.bitwise_and))
                V.sync()
                V.do(dve.tensor_scalar(mb, g_eb, FP8_TINY, FP8_MAGIC, ALU.max, ALU.mult))
                V.sync()
                V.do(dve.tensor_tensor(tmp, vb, mb, ALU.add))
                V.sync()
                dve.tensor_tensor(tmp, tmp, mb, ALU.subtract).then_inc(s_gq, 1)
                dve.wait_ge(s_gq, v + 1)
            dve.wait_ge(s_gx, 8)
            for i in range(NG + 3):
                if 0 <= i - 2 < NG:
                    j = i - 2
                    if j >= 1:
                        take(dve, ("G", "pv", j - 1, 1))
                    for c in G_PT_DVE:
                        o = take(dve, ("G", "pt", j, c))
                        empty(dve.tensor_copy(g_pt[:, c, :, :], o[:, :].rearrange("p (k s) -> p k s", k=2)),
                              ("G", "pt", j, c))
                if 0 <= i - 1 < NG:
                    j = i - 1
                    for c in range(4):
                        o = take(dve, ("G", "sc", j, c))
                        V.do(dve.tensor_reduce(g_mx[j % 2][:, 2 * c:2 * c + 2], o[:, :].rearrange("p (q s) -> p q s", q=2),
                                               AX.X, ALU.max, negate=True))
                        V.sync()
                        dve.tensor_scalar(g_mx[j % 2][:, 2 * c:2 * c + 2], g_mx[j % 2][:, 2 * c:2 * c + 2], SCALE,
                                          None, ALU.mult).then_inc(s_gnb, 1)
                if 0 <= i - 1 < NG:
                    j = i - 1
                    for c in range(4):
                        have(dve, ("G", "sc", j, c))
                    dve.reciprocal(g_sm[j % 2][:, :], g_sm[j % 2][:, :]).then_inc(s_gri, 1)
                if i < NG:
                    for tt in range(2):
                        o = take(dve, ("G", "qkv", i, tt))
                        for h in range(4):
                            V.do(dve.bn_stats(g_bs[:, tt * 6 + h, :], o[:, h * P:h * P + P]))
                    for tt in range(2):
                        o = take(dve, ("G", "qkv", i, 2 + tt))
                        dve.wait_ge(s_gva, 2 * i + tt + 1)
                        for h in range(2):
                            V.do(dve.bn_stats(g_bs[:, tt * 6 + 4 + h, :], o[:, h * 256:h * 256 + P]))
                    V.sync()
                    for s_ in range(12):
                        m = dve.bn_aggr(g_mv[i % 2][:, s_, :], g_bs[:, s_, :])
                    m.then_inc(s_gst, 1)
                if i < NG:
                    dve.wait_ge(s_grs, i + 1)
                    if i >= 2:
                        take(dve, ("G", "tr", i - 2, 2))
                    for tt in range(2):
                        o = psum[uses[("G", "qkv", i, tt)][0]]
                        for h in range(4):
                            s_ = tt * 6 + h
                            m = dve.tensor_scalar(g_n[i % 2][:, s_, :], o[:, h * P:h * P + P],
                                                  g_mv[i % 2][:, s_, 0:1], g_rs[i % 2][:, s_:s_ + 1],
                                                  ALU.subtract, ALU.mult)
                        empty(m, ("G", "qkv", i, tt))
                if 0 <= i - 2 < NG:
                    j = i - 2
                    have(dve, ("G", "pv", j, 0))
                    have(dve, ("G", "pv", j, 1))
                    if j >= 2:
                        dve.wait_ge(s_gc, j - 1)
                    V.do(dve.tensor_scalar(g_ob, g_o[j % 2].rearrange(flat), FP8_MAX, -FP8_MAX, ALU.min, ALU.max))
                    V.sync()
                    V.do(dve.tensor_scalar(g_oe.bitcast(U16), g_ob.bitcast(U16), 0x7F80, None, ALU.bitwise_and))
                    V.sync()
                    V.do(dve.tensor_scalar(g_om[j % 2], g_oe, FP8_TINY, FP8_MAGIC, ALU.max, ALU.mult))
                    V.sync()
                    dve.tensor_tensor(g_o[j % 2].rearrange(flat), g_ob, g_om[j % 2], ALU.add).then_inc(s_gt, 1)
                if 0 <= i - 3 < NG:
                    j = i - 3
                    o = take(dve, ("G", "pj", j))
                    b = j % B
                    xb = x[:, 2 * b:2 * b + 2, :].rearrange("p t d -> p (t d)")
                    if j >= B:
                        have(dve, ("G", "pj", j - B))
                    empty(dve.scalar_tensor_tensor(out=xb, in0=o[:, :], scalar=g_pc[:, :], in1=xb,
                                                   op0=ALU.mult, op1=ALU.add), ("G", "pj", j))
            for j in range(NG - B, NG):
                have(dve, ("G", "pj", j))

        def G_pool(pool, C):
            ln_pool(pool, C, K_G2, EPS)
            pool.wait_ge(s_gk, 1)
            for i in range(NG + 2):
                if 1 <= i <= NG:
                    j = i - 1
                    pool.wait_ge(s_gri, j + 1)
                    pf = g_p[j % 2].rearrange("p c q s -> p (c q) s")
                    pool.tensor_tensor(pf, pf, g_sm[j % 2][:, :].unsqueeze(2).to_broadcast([P, 8, 256]), ALU.mult)\
                        .then_inc(s_gp, 1)
                if i < NG:
                    pool.wait_ge(s_gst, i + 1)
                    if i >= 2:
                        have(pool, ("G", "qkv", i - 2, 1))
                        have(pool, ("G", "qkv", i - 2, 3))
                    r_, n_ = g_rs[i % 2][:, :], g_nb[i % 2][:, :]
                    C.do(pool.tensor_tensor(r_, g_mv[i % 2][:, :, 1], g_w2[:, :], ALU.add))
                    C.do(pool.tensor_scalar(n_, g_mv[i % 2][:, :, 0], -1.0, None, ALU.mult))
                    C.sync()
                    C.do(pool.tensor_tensor(r_, r_, mhalf32[:, 0:12], ALU.pow))
                    C.sync()
                    pool.tensor_tensor(n_, n_, r_, ALU.mult).then_inc(s_grs, 1)
                if i >= 2:
                    j = i - 2
                    pool.wait_ge(s_gt, j + 1)
                    if j >= 2:
                        take(pool, ("G", "pj", j - 2))
                    pool.tensor_tensor(g_c[j % 2].rearrange("p c s -> p (c s)"), g_o[j % 2].rearrange("p c s -> p (c s)"),
                                       g_om[j % 2], ALU.subtract).then_inc(s_gc, 1)

        h_reg = Region(0, 30000)
        h_w2 = h_reg.take([NF, D])
        h_w1 = cx[:, :, :].rearrange("p t d -> p (t d)").rearrange("p (k f) -> p k f", k=KD)
        h_wr = h_reg.take([KD, B * B])
        h_lg = h_reg.take([256])
        h_wk = h_reg.take([2, 256])
        h_m8 = h_reg.take([SLOTS])
        h_sel = h_reg.take([256])
        h_pos = h_reg.take([256])
        h_ew = h_reg.take([256])
        h_sm = h_reg.take([2])
        h_pT = h_reg.take([2, 2, B])
        h_oh = h_reg.take([T, SLOTS])
        h_ohT = h_reg.take([2, P])
        h_fx = h_reg.take([KD, P])
        h_h = h_reg.take([NF, P])
        h_out = h_reg.take([D])
        s_hw1, s_hw2, s_hwr = sem("h_w1_loaded"), sem("h_w2_loaded"), sem("h_router_weights")
        s_hmx, s_hex, s_hpos, s_hoh = sem("h_shifted"), sem("h_exp"), sem("h_slots"), sem("h_onehot")
        for b in range(B):
            plan(("H", "yt", b), b)
        plan(("H", "lg"), 4)
        plan(("H", "pT"), 5)
        plan(("H", "fx"), 6)
        for c in range(2):
            plan(("H", "ohT", c), 4 + c)
        for c in range(2):
            plan(("H", "h", c), c)
        plan(("H", "out"), 7)
        for b in range(B):
            plan(("H", "add", b), b)

        def H_sp(sp):
            sp.wait_ge(s_stage, 5)
            sp.dma_start(h_w1, W1_d).then_inc(s_hw1, 16)
            sp.wait_ge(s_stage, 7)
            sp.dma_start(h_w2, W2_d).then_inc(s_hw2, 16)

        def H_pe(pe):
            yt_pe(pe, K_H, "H")
            pe.wait_ge(s_hwr, 1)
            o = claim(pe, ("H", "lg"))
            for b in range(B):
                have(pe, ("H", "yt", b))
                for k in range(KD):
                    m = pe.matmul(o[0:B, 0:256], h_wr[:, k, b * B:b * B + B], yT[:, k, b * 256:b * 256 + 256],
                                  start=(b == 0 and k == 0), stop=(b == B - 1 and k == 1))
            fill(m, ("H", "lg"))
            o = claim(pe, ("H", "pT"))
            pe.wait_ge(s_hpos, 1)
            for w, src in enumerate((h_pos, h_ew)):
                for q in range(2):
                    m = pe.transpose(o[:, (w * 2 + q) * B:(w * 2 + q) * B + B], src[0:B, q * P:q * P + P],
                                     ident[0:B, 0:B])
            fill(m, ("H", "pT"))
            o = claim(pe, ("H", "fx"))
            pe.wait_ge(s_hoh, 1)
            for d in range(KD):
                for b in range(B):
                    for q in range(2):
                        m = pe.matmul(o[:, d * P + b * SLOTS:d * P + b * SLOTS + SLOTS],
                                      y[:, 2 * b + q, d * P:d * P + P], h_oh[:, 2 * b + q, :],
                                      start=(q == 0), stop=(q == 1))
            fill(m, ("H", "fx"))
            for c in range(2):
                o = claim(pe, ("H", "ohT", c))
                for j in range(4):
                    m = pe.transpose(o[0:SLOTS, j * P:j * P + P], h_oh[:, 4 * c + j, :], ident)
                fill(m, ("H", "ohT", c))
            pe.wait_ge(s_hw1, 16)
            have(pe, ("H", "fx"))
            for c in range(2):
                o = claim(pe, ("H", "h", c))
                for j in range(4):
                    f = 4 * c + j
                    for k in range(KD):
                        m = pe.matmul(o[:, j * P:j * P + P], h_w1[:, k, f * P:f * P + P], h_fx[:, k, :],
                                      start=(k == 0), stop=(k == 1))
                fill(m, ("H", "h", c))
            o = claim(pe, ("H", "out"))
            pe.wait_ge(s_hw2, 16)
            for f in range(NF):
                have(pe, ("H", "h", f // 4))
                m = pe.matmul(o[:, 0:D], h_h[:, f, :], h_w2[:, f, :], start=(f == 0), stop=(f == NF - 1))
            fill(m, ("H", "out"))
            have(pe, ("H", "out"))
            have(pe, ("H", "ohT", 0))
            have(pe, ("H", "ohT", 1))
            for b in range(B):
                o = claim(pe, ("H", "add", b))
                r = 32 * b
                for q in range(2):
                    m = pe.matmul(o[:, q * D:q * D + D], h_ohT[r:r + 32, q, :], h_out[r:r + 32, :],
                                  start=True, stop=True)
                fill(m, ("H", "add", b))

        def H_act(act):
            yt_act(act, "H")
            act.wait_ge(s_hmx, 1)
            act.activation(h_ew[0:B, :], h_lg[0:B, :], ACT.Exp).then_inc(s_hex, 1)
            for c in range(2):
                o = take(act, ("H", "h", c))
                for j in range(4):
                    f = 4 * c + j
                    m = act.activation(h_h[:, f, :], o[:, j * P:j * P + P], ACT.Gelu, bias=col("b1", f))
                empty(m, ("H", "h", c))

        def H_dve(dve, V):
            V.do(dve.memset(h_wr, 0.0))
            V.sync()
            for k in range(KD):
                m = dve.tensor_copy(h_wr[:, k, 0:B * B:B + 1], col("Wr", k).to_broadcast([P, B]))
            m.then_inc(s_hwr, 1)
            b4 = slice(0, B)
            o = take(dve, ("H", "lg"))
            empty(dve.tensor_scalar(h_lg[b4, :], o[b4, 0:256], row("br", B), None, ALU.add), ("H", "lg"))
            have(dve, ("H", "lg"))
            V.do(dve.tensor_copy(h_wk[b4, 0, :], h_lg[b4, :]))
            V.sync()
            for r in range(SLOTS // 8):
                V.do(dve.max(out=h_m8[b4, 8 * r:8 * r + 8], in_=h_wk[b4, r % 2, :]))
                V.sync()
                V.do(dve.match_replace(out=h_wk[b4, 1 - r % 2, :], in_to_replace=h_m8[b4, 8 * r:8 * r + 8],
                                       in_values=h_wk[b4, r % 2, :], imm_value=-3e38))
                V.sync()
            V.do(dve.tensor_tensor(h_sel[b4, :], h_wk[b4, 0, :], h_lg[b4, :], ALU.not_equal))
            V.sync()
            V.do(dve.tensor_tensor_scan(h_pos[b4, :], b_z[b4, :], h_sel[b4, :], 0.0, ALU.add, ALU.add))
            dve.tensor_scalar(h_lg[b4, :], h_lg[b4, :], h_m8[b4, 0:1], None, ALU.subtract).then_inc(s_hmx, 1)
            V.sync()
            V.do(dve.tensor_tensor(h_pos[b4, :], h_pos[b4, :], h_sel[b4, :], ALU.mult))
            V.sync()
            V.do(dve.tensor_scalar(h_pos[b4, :], h_pos[b4, :], -1.0, None, ALU.add))
            dve.wait_ge(s_hex, 1)
            V.do(dve.tensor_tensor(h_ew[b4, :], h_ew[b4, :], h_sel[b4, :], ALU.mult))
            V.sync()
            V.do(dve.tensor_reduce(h_sm[b4, 0:1], h_ew[b4, :], AX.X, ALU.add))
            V.sync()
            V.do(dve.reciprocal(h_sm[b4, 1:2], h_sm[b4, 0:1]))
            V.sync()
            dve.tensor_scalar(h_ew[b4, :], h_ew[b4, :], h_sm[b4, 1:2], None, ALU.mult).then_inc(s_hpos, 1)
            o = take(dve, ("H", "pT"))
            empty(dve.tensor_copy(h_pT.rearrange("p a b c -> p (a b c)"), o[:, 0:16]), ("H", "pT"))
            have(dve, ("H", "pT"))
            for t in range(T):
                m = dve.tensor_scalar(h_oh[:, t, :], cst[:, 264:296], h_pT[:, 0, t % 2, t // 2:t // 2 + 1], None,
                                      ALU.is_equal)
                if t < T - 1:
                    V.do(m)
            m.then_inc(s_hoh, 1)
            dve.wait_ge(s_y, 8 * K_H + 8)
            V.do(dve.tensor_tensor(x[:, :, :], x[:, :, :], y[:, :, :], ALU.add))
            o = take(dve, ("H", "fx"))
            empty(dve.tensor_copy(h_fx.rearrange("p k n -> p (k n)"), o[:, 0:256]), ("H", "fx"))
            for c in range(2):
                o = take(dve, ("H", "ohT", c))
                for j in range(4):
                    t = 4 * c + j
                    r = 32 * (t // 2)
                    m = dve.tensor_copy(h_ohT[r:r + 32, t % 2, :], o[0:SLOTS, j * P:j * P + P])
                    if j < 3:
                        V.do(m)
                empty(m, ("H", "ohT", c))
            o = take(dve, ("H", "out"))
            empty(dve.tensor_tensor(h_out, o[:, 0:D], row("b2"), ALU.add), ("H", "out"))
            V.sync()
            for b in range(B):
                o = take(dve, ("H", "add", b))
                for q in range(2):
                    t = 2 * b + q
                    m = dve.scalar_tensor_tensor(out=x[:, t, :], in0=o[:, q * D:q * D + D],
                                                 scalar=h_pT[:, 1, q, b:b + 1], in1=x[:, t, :],
                                                 op0=ALU.mult, op1=ALU.add)
                    if q == 0:
                        V.do(m)
                empty(m, ("H", "add", b))
            for b in range(B):
                have(dve, ("H", "add", b))

        s_out = sem("stored")

        block = ctx_mgr.enter_context(nc.Block())

        @block.sync
        def _(sp):
            sp.dma_start(x[:, :, :], x_d.rearrange("b (h p) d -> p (b h) d", p=P)).then_inc(s_x, 16)
            sp.dma_start(cst[:, :], cst_d).then_inc(s_cst, 16)
            sp.dma_start(cols[:, :], cols_d).then_inc(s_cst, 16)
            sp.dma_start(rows[:, :], rows_d.partition_broadcast(P)).then_inc(s_cst, 16)
            sp.dma_start(cx[:, :, :], ctx_d.rearrange("b (h p) d -> p (b h) d", p=P)).then_inc(s_ctx, 16)
            sp.dma_start(cxT[:, :, :], ctxT_d).then_inc(s_ctxT, 16)
            sp.dma_start(b_rw[:, :, :], rw_d).then_inc(s_small, 16)
            D_sp(sp)
            if STAGES > 1:
                sp.dma_start(b_bd[0:NE, :], bd_d).then_inc(s_small, 16)
                B_sp(sp)
            if STAGES > 4:
                E_sp(sp)
            if STAGES > 5:
                F_sp(sp)
            if STAGES > 6:
                G_sp(sp)
            if STAGES > 7:
                H_sp(sp)
            sp.wait_ge(s_stage, STAGES)
            sp.dma_start(out_d.rearrange("b (h p) d -> p (b h) d", p=P), x[:, :, :]).then_inc(s_out, 16)
            sp.wait_ge(s_out, 16)

        @block.tensor
        def _(pe):
            A_pe(pe)
            if STAGES > 1:
                B_pe(pe)
            if STAGES > 2:
                C_pe(pe)
            if STAGES > 3:
                D_pe(pe)
            if STAGES > 4:
                E_pe(pe)
            if STAGES > 5:
                F_pe(pe)
            if STAGES > 6:
                G_pe(pe)
            if STAGES > 7:
                H_pe(pe)

        @block.scalar
        def _(act):
            A_act(act)
            if STAGES > 1:
                B_act(act)
            if STAGES > 2:
                C_act(act)
            if STAGES > 3:
                D_act(act)
            if STAGES > 4:
                E_act(act)
            if STAGES > 5:
                F_act(act)
            if STAGES > 6:
                G_act(act)
            if STAGES > 7:
                H_act(act)

        @block.vector
        def _(dve):
            V = Chain(dve, s_dve)

            def done():
                V.sync()
                dve.tensor_copy(b_n[:, 1:2], mv[:, 0, 0:1]).then_inc(s_stage, 1)

            dve.wait_ge(s_x, 16)
            ln_dve(dve, V, K_A, x, EPS)
            setup_dve(dve, V)
            ctx_quant_dve(dve, V)
            A_dve(dve, V)
            done()
            for n, (k, f) in enumerate([(K_B, B_dve), (K_C, C_dve), (K_D, D_dve), (K_E, E_dve),
                                        (K_F, F_dve), (K_G, G_dve), (K_H, H_dve)]):
                if STAGES > n + 1:
                    ln_dve(dve, V, k, x, EPS)
                    f(dve, V)
                    done()

        @block.gpsimd
        def _(pool):
            C = Chain(pool, s_pool)
            setup_pool(pool, C)
            ln_pool(pool, C, K_A, EPS)
            ctx_quant_pool(pool, C)
            if STAGES > 1:
                ln_pool(pool, C, K_B, EPS)
                B_pool(pool, C)
            if STAGES > 2:
                ln_pool(pool, C, K_C, EPS)
            if STAGES > 4:
                E_prep_pool(pool, C)
            if STAGES > 3:
                ln_pool(pool, C, K_D, EPS)
            if STAGES > 4:
                ln_pool(pool, C, K_E, EPS)
                E_pool(pool, C)
            if STAGES > 5:
                ln_pool(pool, C, K_F, EPS)
                F_pool(pool, C)
            if STAGES > 6:
                ln_pool(pool, C, K_G, EPS)
                G_pool(pool, C)
            if STAGES > 7:
                ln_pool(pool, C, K_H, EPS)


_OUTS = [((4, 256, 256), "float32")]


def _layout(i):
    import numpy as np

    def c(a):
        return np.ascontiguousarray(a)

    def kxm(w):
        return c(w.reshape(w.shape[0] // P, P, w.shape[1]).transpose(1, 0, 2))

    def column(v, n):
        v = np.asarray(v).reshape(-1)
        full = np.zeros((n * P,), np.float32)
        full[:v.size] = v
        return full.reshape(n, P).T

    i = {k: np.asarray(v) for k, v in i.items()}
    ctx = i["ctx_2048"]
    cst = np.zeros((P, NCST), np.float32)
    cst[:, 0:128] = np.eye(P)
    r = np.arange(P)
    cst[:, 128:256] = np.where(r[None, :] >= r[:, None], 0.0, -BIG)
    cst[:, 256:264] = (r // DH)[:, None] == np.arange(8)[None, :]
    cst[:, 264:296] = np.arange(32)[None, :]
    cst[:, 296:312] = (r % 32)[:, None] == np.arange(16)[None, :]
    gu = i["L0_ffn_gate_up_proj"]
    gu = np.concatenate([gu[..., 0::2], gu[..., 1::2]], axis=-1)
    bgu = i["L0_ffn_gate_up_proj_bias"]
    bgu = np.concatenate([bgu[..., 0::2], bgu[..., 1::2]], axis=-1)
    cv = {"bgu": column(bgu, 64), "gs": column(i["L1_ffn_gate_s"], NI), "us": column(i["L1_ffn_up_s"], NI),
          "bi": column(i["L2_xattn_bi"], 1), "bf": column(i["L2_xattn_bf"], 1),
          "lnw": column(i["L3_xattn_ln_w"], 2), "lnb": column(i["L3_xattn_ln_b"], 2),
          "sc_q": column(i["L3_xattn_q_in_scale"], 2), "sc_qx": column(i["L3_xattn_qx_in_scale"], 2),
          "sc_k": column(i["L3_xattn_k_in_scale"], 2), "sc_v": column(i["L3_xattn_v_in_scale"], 2),
          "smooth": column(i["L3_xattn_proj_smooth"], 32), "Wr": column(i["L3_ffn_Wr"], 2),
          "b1": column(i["L3_ffn_b1"], NF)}
    for s, l in (("q", "q"), ("k", "k"), ("qx", "qx"), ("kx", "kx")):
        cv[s + "w"] = column(i[f"L3_xattn_{l}ln_w"], 1)
        cv[s + "b"] = column(i[f"L3_xattn_{l}ln_b"], 1)
    cols = np.zeros((P, NCOL), np.float32)
    for n, (a, z) in COLS.items():
        cols[:, a:z] = cv[n]
    rv = {"rb": i["L0_ffn_router_bias"], "ds": i["L1_ffn_down_s"], "lns": i["L2_xattn_ln_scale"],
          "b2f": i["L2_ffn_bias"], "b2": i["L3_ffn_b2"], "s_q": i["L3_xattn_wq_scale"],
          "s_qx": i["L3_xattn_wqx_scale"], "s_k": i["L3_xattn_wk_scale"], "s_v": i["L3_xattn_wv_scale"],
          "s_pw": i["L3_xattn_proj_w_scale"], "s_pi": i["L3_xattn_proj_in_scale"], "br": i["L3_ffn_br"]}
    rows = np.zeros((NROW,), np.float32)
    for n, (a, z) in ROWS.items():
        rows[a:z] = rv[n].reshape(-1)

    def heads(w, per):
        return w.reshape(G, per * HD, D).transpose(0, 2, 1)

    kv = i["L3_xattn_w_kv_x"]
    wg = np.concatenate([heads(i["L3_xattn_wq"], 2), heads(i["L3_xattn_wqx"], 2), heads(i["L3_xattn_wk"], 1),
                         heads(i["L3_xattn_wv"], 1), heads(kv[:G * HD], 1), heads(kv[G * HD:], 1)], axis=2)
    wp = i["L3_xattn_wproj"].T.reshape(2, G, 2, HD, D).transpose(1, 3, 0, 2, 4).reshape(G, HD, 4, D)
    return [
        i["x"], ctx, kxm(ctx.reshape(B * S, D).T), cst, cols, rows,
        kxm(i["L0_ffn_router_weight"].T),
        c(gu.reshape(NE, KD, P, 4 * P).transpose(0, 2, 1, 3)),
        c(i["L0_ffn_down_proj"].reshape(NE, KD, P, D).transpose(0, 2, 1, 3)),
        i["L0_ffn_down_proj_bias"],
        kxm(i["L1_ffn_gate_w"].T), kxm(i["L1_ffn_up_w"].T), c(i["L1_ffn_down_w"].T),
        kxm(np.concatenate([i["L2_xattn_Wi"], i["L2_xattn_Wf"]], axis=1)),
        kxm(i["L2_ffn_weight"].T),
        c(wg.reshape(G, KD, P, 1024).transpose(0, 2, 1, 3)), c(wp),
        kxm(i["L3_ffn_W1"]), kxm(i["L3_ffn_W2"]),
    ]


def kernel(**inputs):
    import numpy as _np
    import concourse.bacc as _bacc
    from concourse import mybir as _mybir
    from concourse.bass_utils import run_bass_kernel_spmd as _run

    nc = _bacc.Bacc("TRN2", target_bir_lowering=False, num_devices=1)
    arrays, args = {}, []
    for n, a in enumerate(_layout(inputs)):
        a = _np.ascontiguousarray(a)
        arrays[f"in_{n}_dram"] = a
        args.append(nc.dram_tensor(f"in_{n}_dram", a.shape, _mybir.dt.from_np(a.dtype), kind="ExternalInput").ap())
    for i, (shape, dtype) in enumerate(_OUTS):
        dt = _mybir.dt.from_np(_np.dtype(dtype))
        args.append(nc.dram_tensor(f"out_{i}_dram", shape, dt, kind="ExternalOutput").ap())
    build(nc, *args)
    r = _run(nc, [arrays], core_ids=[0])
    return r.results[0]["out_0_dram"]
```

```python
from contextlib import ExitStack

import concourse.bass as bass
from concourse import mybir

F32 = mybir.dt.float32
F32R = mybir.dt.float32r
BF16 = mybir.dt.bfloat16
U16 = mybir.dt.uint16
I32 = mybir.dt.int32
ALU = mybir.AluOpType
ACT = mybir.ActivationFunctionType
AX = mybir.AxisListType
RMAX = bass.bass_isa.ReduceOp.max
RADD = bass.bass_isa.ReduceOp.add

P = 128
B, S, D = 4, 256, 256
T = B * S // P
KD = D // P
NE, TOPK = 16, 4
INTER = 704
NI = 6
NH, DH = 16, 16
G, HD = 8, 128
SLOTS = 32
NF = 8
EPS = 1e-5
ROUND23 = 12582912.0
FP8_MAX = 448.0
FP8_MAGIC = 1572864.0
FP8_TINY = 2.0 ** -6
BIG = 1e30

COLS = {}
_at = 0
for _n, _w in [("bgu", 64), ("gs", NI), ("us", NI), ("bi", 1), ("bf", 1), ("lnw", 2), ("lnb", 2),
               ("sc_q", 2), ("sc_qx", 2), ("sc_k", 2), ("sc_v", 2), ("qw", 1), ("qb", 1), ("kw", 1), ("kb", 1),
               ("qxw", 1), ("qxb", 1), ("kxw", 1), ("kxb", 1), ("smooth", 32), ("Wr", 2), ("b1", NF)]:
    COLS[_n] = (_at, _at + _w)
    _at += _w
NCOL = _at
ROWS = {}
_at = 0
for _n, _w in [("rb", 16), ("ds", D), ("lns", D), ("b2f", D), ("b2", D), ("s_q", 1), ("s_qx", 1), ("s_k", 1),
               ("s_v", 1), ("s_pw", 1), ("s_pi", 1), ("br", 1)]:
    ROWS[_n] = (_at, _at + _w)
    _at += _w
NROW = _at
CST = {"ident": (0, 128), "causal": (128, 256), "parity": (256, 258), "iota": (258, 290), "head": (290, 306)}
NCST = 312
ARENA = 37000


class Chain:

    def __init__(self, eng, sem):
        self.eng, self.sem, self.n = eng, sem, 0

    def do(self, ins):
        ins.then_inc(self.sem, 1)
        self.n += 1
        return self.n

    def sync(self):
        if self.n:
            self.eng.wait_ge(self.sem, self.n)


def build(nc, x_d, ctx_d, ctxT_d, cst_d, cols_d, rows_d, rw_d, guw_d, dw_d, bd_d, gwT_d, uwT_d, dwT_d,
          wif_d, w2T_d, wg_d, wp_d, W1_d, W2_d, out_d):
    ctx_mgr = ExitStack()
    with ctx_mgr:
        def sb(name, shape, dt=F32):
            return ctx_mgr.enter_context(nc.sbuf_tensor(name, shape, dt))

        def sem(name):
            return ctx_mgr.enter_context(nc.semaphore(name))

        x = sb("x", [P, T, D])
        y = sb("y", [P, T, D])
        yT = sb("yT", [P, KD, T * P])
        cx = sb("cx", [P, T, D])
        cxT = sb("cxT", [P, KD, T * P])
        cst = sb("cst", [P, NCST])
        cols = sb("cols", [P, NCOL])
        rows = sb("rows", [P, NROW])
        identb = sb("identb", [P, P], BF16)
        causal = sb("causal", [P, P], BF16)
        bst = sb("bst", [P, 16, 6])
        mv = sb("mv", [P, T, 2])
        rs = sb("rs", [P, T])
        mhalf = sb("mhalf", [P, 32])
        with nc.sbuf_tensor("arena", [P, ARENA], F32) as arena:
            pass
        with ExitStack() as second:
            def gr(name, shape):
                return second.enter_context(nc.sbuf_tensor(name, shape, F32R))

            g_xs = [gr(f"g_xs{v}", [P, KD, T * P]) for v in range(4)]
            g_c = [gr(f"g_c{i}", [P, 4, 256]) for i in range(2)]
            g_wh = [gr(f"g_wh{i}", [P, KD, 768]) for i in range(2)]
            g_wl = [gr(f"g_wl{i}", [P, KD, 768]) for i in range(2)]
            g_ph = [gr(f"g_ph{i}", [P, 4, D]) for i in range(2)]
            g_pl = [gr(f"g_pl{i}", [P, 4, D]) for i in range(2)]
        G_AT = 4 * KD * T * P + 2 * 1024 + 4 * KD * 768 + 4 * 4 * D
        with ExitStack() as third:
            third.enter_context(nc.sbuf_tensor("b_space", [P, 19200], F32))

            def br(name, shape):
                return third.enter_context(nc.sbuf_tensor(name, shape, F32R))

            b_yh, b_yl = br("b_yh", [P, KD, T * P]), br("b_yl", [P, KD, T * P])
            b_wh = [br(f"b_wh{i}", [P, KD, 4 * P]) for i in range(2)]
            b_wl = [br(f"b_wl{i}", [P, KD, 4 * P]) for i in range(2)]
        sb("arena_space", [P, ARENA])
        psum = [ctx_mgr.enter_context(nc.psum_tensor(f"bank{i}", [P, 512], F32)) for i in range(8)]
        ident = cst[:, 0:128]

        def col(name, i=0, p=P):
            return cols[0:p, COLS[name][0] + i:COLS[name][0] + i + 1]

        def row(name, p=P):
            return rows[0:p, ROWS[name][0]:ROWS[name][1]]

        class Region:

            def __init__(self, at, end):
                self.at, self.end = at, end

            def take(self, shape, dt=F32):
                n = 1
                for s_ in shape:
                    n *= s_
                words = n if dt == F32 else (n + 1) // 2
                ap = arena[:, self.at:self.at + words]
                self.at += words
                assert self.at <= self.end, (self.at, self.end)
                if dt != F32:
                    ap = ap.bitcast(dt)
                if len(shape) > 1:
                    names = "abcde"[:len(shape)]
                    ap = ap.rearrange("p (%s) -> p %s" % (" ".join(names), " ".join(names)),
                                      **{n_: s_ for n_, s_ in zip(names, shape)})
                return ap

        filled = [sem(f"filled{i}") for i in range(8)]
        emptied = [sem(f"emptied{i}") for i in range(8)]
        s_dve, s_act, s_pool = sem("dve_done"), sem("act_done"), sem("pool_done")
        s_x, s_ctx, s_ctxT, s_cst = sem("x_loaded"), sem("ctx_loaded"), sem("ctxT_loaded"), sem("cst_loaded")
        s_stage = sem("stage_done")
        s_stat, s_rs, s_y = sem("ln_stats"), sem("ln_rstd"), sem("ln_out")
        s_cb = sem("bf16_consts")

        uses, count = {}, [0] * 8

        def plan(key, bank):
            assert key not in uses, key
            uses[key] = (bank, count[bank])
            count[bank] += 1

        def claim(pe, key):
            b_, n = uses[key]
            if n:
                pe.wait_ge(emptied[b_], n)
            return psum[b_]

        def fill(ins, key):
            ins.then_inc(filled[uses[key][0]], 1)

        def take(eng, key):
            b_, n = uses[key]
            eng.wait_ge(filled[b_], n + 1)
            return psum[b_]

        def empty(ins, key):
            ins.then_inc(emptied[uses[key][0]], 1)

        def have(eng, key):
            b_, n = uses[key]
            eng.wait_ge(emptied[b_], n + 1)

        LN = {"n": 0, "dve": 0, "pool": 0}

        def ln_dve(dve, V, k, src, eps, after=None):
            if after is not None:
                dve.wait_ge(s_y, after)
            for t in range(T):
                V.do(dve.bn_stats(bst[:, t, :], src[:, t, :]))
            V.sync()
            for t in range(T):
                i = dve.bn_aggr(mv[:, t, :], bst[:, t, :])
            i.then_inc(s_stat, 1)
            dve.wait_ge(s_rs, k + 1)
            for t in range(T):
                dve.tensor_scalar(y[:, t, :], src[:, t, :], mv[:, t, 0:1], rs[:, t:t + 1],
                                  ALU.subtract, ALU.mult).then_inc(s_y, 1)

        def ln_pool(pool, C, k, eps):
            pool.wait_ge(s_stat, k + 1)
            C.do(pool.tensor_scalar(rs[:, :], mv[:, :, 1], eps, None, ALU.add))
            C.sync()
            pool.tensor_tensor(rs[:, :], rs[:, :], mhalf[:, 0:T], ALU.pow).then_inc(s_rs, 1)

        def yt_pe(pe, k, tag):
            for b in range(B):
                o = claim(pe, (tag, "yt", b))
                pe.wait_ge(s_y, 8 * k + 2 * b + 2)
                for d in range(KD):
                    for h in range(2):
                        m = pe.transpose(o[:, d * 256 + h * 128:d * 256 + h * 128 + 128],
                                         y[:, 2 * b + h, d * P:d * P + P], ident)
                fill(m, (tag, "yt", b))

        def yt_act(act, tag):
            for b in range(B):
                o = take(act, (tag, "yt", b))
                empty(act.copy(yT[:, :, b * 256:b * 256 + 256], o[:, :].rearrange("p (d n) -> p d n", d=KD)),
                      (tag, "yt", b))

        K_A, K_B, K_C, K_D, K_E, K_F, K_G, K_G2, K_H = range(9)

        c_reg = Region(27600, 37000)
        c_v = c_reg.take([T, 2, P])
        c_e = c_reg.take([T * 2 * P])
        c_m = c_reg.take([T * 2 * P])
        c_q = c_reg.take([T, 2, P], BF16)
        c_qT = c_reg.take([KD, T * P], BF16)
        cw_q = sb("cw_q", [P, KD, B, 2, P], BF16)
        c_sw = sb("c_sw", [P, KD, B, 2])
        c_aw = sb("c_aw", [P, 16])
        c_ax = sb("c_ax", [P, T, 2])
        c_sx = sb("c_sx", [P, T, 2])
        c_rx = sb("c_rx", [P, T, 2])
        c_rw = sb("c_rw", [P, 16])
        c_c = sb("c_c", [P, T, 2, 2])
        s_cw, s_cwr = sem("ctx_amax"), sem("ctx_amax_all")
        s_cq = sem("c_quantised")

        def fp8_round(dve, V, v, e, m, q):
            V.do(dve.tensor_scalar(e.bitcast(I32), v.bitcast(I32), 0x7F800000, None, ALU.bitwise_and))
            V.sync()
            V.do(dve.tensor_scalar(m, e, FP8_TINY, FP8_MAGIC, ALU.max, ALU.mult))
            V.sync()
            V.do(dve.tensor_tensor(e, v, m, ALU.add))
            V.sync()
            V.do(dve.tensor_tensor(q, e, m, ALU.subtract))

        def setup_dve(dve, V):
            dve.wait_ge(s_cst, 48)
            V.do(dve.tensor_copy(identb[:, :], ident))
            dve.tensor_copy(causal[:, :], cst[:, 128:256]).then_inc(s_cb, 1)
            dve.wait_ge(s_ctxT, 16)
            blocks = cxT[:, :, :].rearrange("p k (c n) -> p (k c) n", n=P)
            dve.tensor_reduce(c_aw[:, :], blocks, AX.X, ALU.max, apply_absolute_value=True).then_inc(s_cw, 1)

        def ctx_quant_dve(dve, V):
            dve.wait_ge(s_cwr, 1)
            sw = c_sw[:, :, :, :].rearrange("p k b n -> p (k b n)")
            V.do(dve.tensor_scalar(sw, sw, 1e-6, 1.0 / FP8_MAX, ALU.max, ALU.mult))
            V.sync()
            V.do(dve.reciprocal(c_rw[:, :], sw))
            V.sync()
            vv = c_v.rearrange("p a b n -> p (a b) n")
            V.do(dve.tensor_tensor(vv, cxT[:, :, :].rearrange("p k (c n) -> p (k c) n", n=P),
                                   c_rw[:, :].unsqueeze(2).to_broadcast([P, 16, P]), ALU.mult))
            V.sync()
            fp8_round(dve, V, c_v.rearrange("p a b n -> p (a b n)"), c_e, c_m,
                      cw_q[:, :, :, :, :].rearrange("p k b m n -> p (k b m n)"))

        def setup_pool(pool, C):
            C.do(pool.memset(mhalf[:, :], -0.5))
            C.sync()

        def ctx_quant_pool(pool, C):
            pool.wait_ge(s_cw, 1)
            pool.partition_all_reduce(c_sw[:, :, :, :].rearrange("p k b n -> p (k b n)"), c_aw[:, :], P, RMAX)\
                .then_inc(s_cwr, 1)

        a_reg = Region(25000, 27600)
        a_sc = a_reg.take([2, 2, 256])
        for b in range(B + 1):
            if b < B:
                plan(("A", "s", b), b % 4)
            if b > 0:
                plan(("A", "o", b - 1), 4 + b % 4)

        def A_pe(pe):
            pe.wait_ge(s_ctx, 16)
            pe.wait_ge(s_ctxT, 16)
            pe.wait_ge(s_cst, 48)
            for b in range(B + 1):
                if b < B:
                    o = claim(pe, ("A", "s", b))
                    pe.wait_ge(s_y, 8 * K_A + 2 * b + 2)
                    for n in range(2):
                        for k in range(2):
                            m = pe.matmul(o[:, n * 256:n * 256 + 256], y[:, 2 * b + k, n * P:n * P + P],
                                          cx[:, 2 * b + k, :], start=(k == 0), stop=(k == 1))
                    fill(m, ("A", "s", b))
                if b > 0:
                    c = b - 1
                    o = claim(pe, ("A", "o", c))
                    have(pe, ("A", "s", c))
                    for v in range(2):
                        for n in range(2):
                            m = pe.matmul(o[:, v * 256:v * 256 + 256],
                                          cxT[:, n, c * 256 + v * P:c * 256 + v * P + P],
                                          a_sc[:, c % 2, n, :], start=(n == 0), stop=(n == 1))
                    fill(m, ("A", "o", c))

        def A_act(act):
            for b in range(B):
                if b >= 2:
                    uk = uses[("A", "o", b - 2)]
                    act.wait_ge(filled[uk[0]], uk[1] + 1)
                o = take(act, ("A", "s", b))
                empty(act.activation(a_sc[:, b % 2, :, :], o[:, :].rearrange("p (n m) -> p n m", n=2),
                                     ACT.Sigmoid, scale=1.0 / 16.0), ("A", "s", b))

        def A_dve(dve, V):
            for b in range(B):
                o = take(dve, ("A", "o", b))
                xb = x[:, 2 * b:2 * b + 2, :].rearrange("p t d -> p (t d)")
                empty(dve.tensor_tensor(xb, xb, o[:, :], ALU.add), ("A", "o", b))
            for b in range(B):
                have(dve, ("A", "o", b))

        b_reg = Region(0, 14800)
        NWB = 3
        b_w = [b_reg.take([KD, 4 * P]) for _ in range(NWB)]
        b_d = [b_reg.take([KD, D]) for _ in range(NWB)]
        b_g = b_reg.take([2, 2, 512])
        b_sg = b_reg.take([2, 2, 512])
        b_u = b_reg.take([2, 2, 512])
        b_h = b_reg.take([2, 2, 512])
        b_rw = sb("b_rw", [P, KD, NE])
        b_lg = sb("b_lg", [P, T, NE])
        b_m8 = sb("b_m8", [P, T, 8])
        b_gt = sb("b_gt", [P, T, NE])
        b_eq = sb("b_eq", [P, T, NE])
        b_cs = sb("b_cs", [P, T, NE])
        b_n = sb("b_n", [P, T])
        b_s = sb("b_s", [P, T, NE])
        b_z = sb("b_z", [P, 256])
        b_sT = b_reg.take([T * P])
        b_bd = b_reg.take([D])
        s_bw = [sem(f"expert_loaded{i}") for i in range(NWB)]
        s_small = sem("small_loaded")
        s_byh, s_byl, s_bwh, s_bwl = sem("b_y_high"), sem("b_y_low"), sem("b_weights_high"), sem("b_weights_low")

        def split_y_act(act, half):
            have(act, ("B", "yt", 2 * half))
            have(act, ("B", "yt", 2 * half + 1))
            hs = slice(half * 512, half * 512 + 512)
            act.copy(b_yh[:, :, hs], yT[:, :, hs]).then_inc(s_byh, 1)

        def split_y_dve(dve, half):
            dve.wait_ge(s_byh, half + 1)
            hs = slice(half * 512, half * 512 + 512)
            dve.tensor_tensor(b_yl[:, :, hs], yT[:, :, hs], b_yh[:, :, hs].bitcast(F32), ALU.subtract)\
                .then_inc(s_byl, 1)

        def split_e_act(act, e):
            act.wait_ge(s_bw[e % NWB], 32 * (e // NWB + 1))
            if e >= 2:
                take(act, ("B", "gu", 2 * e - 3, 1, 1))
            act.copy(b_wh[e % 2][:, :, :], b_w[e % NWB]).then_inc(s_bwh, 1)

        def split_e_dve(dve, e):
            dve.wait_ge(s_bw[e % NWB], 32 * (e // NWB + 1))
            if e >= 2:
                take(dve, ("B", "gu", 2 * e - 3, 1, 1))
            dve.wait_ge(s_bwh, e + 1)
            dve.tensor_tensor(b_wl[e % 2][:, :, :], b_w[e % NWB], b_wh[e % 2][:, :, :].bitcast(F32), ALU.subtract)\
                .then_inc(s_bwl, 1)
        s_blg, s_bex, s_bs = sem("b_logits"), sem("b_exp"), sem("b_scores")
        s_bu, s_bt, s_bsg, s_bh = sem("b_up"), sem("b_gated"), sem("b_sig"), sem("b_hidden")
        for b in range(B):
            plan(("B", "yt", b), b % 4)
        plan(("B", "lg"), 6)
        for c in range(2):
            plan(("B", "sT", c), 6 + c)
        for c in range(4):
            plan(("B", "bd", c), 6 + c % 2)
        NIT = 2 * NE
        gi = 0
        for i in range(NIT + 1):
            if i < NIT:
                for d in range(2):
                    for gu in range(2):
                        plan(("B", "gu", i, d, gu), gi % 6)
                        gi += 1
            if i > 0:
                for c in range(2):
                    plan(("B", "dn", i - 1, c), 6 + c)

        def B_sp(sp):
            for e in range(NE):
                s_ = e % NWB
                if e >= NWB:
                    bk, n = uses[("B", "dn", 2 * (e - NWB) + 1, 1)]
                    sp.wait_ge(filled[bk], n + 1)
                sp.dma_start(b_w[s_], guw_d[e]).then_inc(s_bw[s_], 16)
                sp.dma_start(b_d[s_], dw_d[e]).then_inc(s_bw[s_], 16)

        def B_pe(pe):
            yt_pe(pe, K_B, "B")
            pe.wait_ge(s_small, 32)
            o = claim(pe, ("B", "lg"))
            for b in range(B):
                have(pe, ("B", "yt", b))
            for t in range(T):
                for k in range(KD):
                    m = pe.matmul(o[:, t * NE:t * NE + NE], yT[:, k, t * P:t * P + P], b_rw[:, k, :],
                                  start=(k == 0), stop=(k == 1))
            fill(m, ("B", "lg"))

            def route():
                pe.wait_ge(s_bs, 1)
                for c in range(2):
                    o = claim(pe, ("B", "sT", c))
                    for j in range(4):
                        m = pe.transpose(o[0:NE, j * P:j * P + P], b_s[:, 4 * c + j, :], ident)
                    fill(m, ("B", "sT", c))
                for c in range(4):
                    o = claim(pe, ("B", "bd", c))
                    if c == 0:
                        have(pe, ("B", "sT", 0))
                        have(pe, ("B", "sT", 1))
                    for j in range(2):
                        t = 2 * c + j
                        m = pe.matmul(o[:, j * D:j * D + D], b_sT[0:NE, t * P:t * P + P], b_bd[0:NE, :],
                                      start=True, stop=True)
                    fill(m, ("B", "bd", c))

            for i in range(NIT + 1):
                if i < NIT:
                    e, half = i // 2, i % 2
                    if half == 0:
                        pe.wait_ge(s_bw[e % NWB], 32 * (e // NWB + 1))
                        pe.wait_ge(s_bwl, e + 1)
                    if i < 2:
                        pe.wait_ge(s_byl, i + 1)
                    for d in range(2):
                        for gu in range(2):
                            key = ("B", "gu", i, d, gu)
                            o = claim(pe, key)
                            c0 = (gu * 2 + d) * P
                            hs = slice(half * 512, half * 512 + 512)
                            parts = [(w[e % 2][:, k, c0:c0 + P], v[:, k, hs]) for k in range(KD)
                                     for w, v in ((b_wh, b_yh), (b_wh, b_yl), (b_wl, b_yh))]
                            for n, (w, v) in enumerate(parts):
                                m = pe.matmul(o[:, :], w, v, start=(n == 0), stop=(n == 5))
                            fill(m, key)
                if i == 0:
                    route()
                if i > 0:
                    j = i - 1
                    e = j // 2
                    pe.wait_ge(s_bh, 2 * (j + 1))
                    for c in range(2):
                        o = claim(pe, ("B", "dn", j, c))
                        for q in range(2):
                            for d in range(2):
                                m = pe.matmul(o[:, q * D:q * D + D],
                                              b_h[:, j % 2, d, (2 * c + q) * P:(2 * c + q) * P + P],
                                              b_d[e % NWB][:, d, :], start=(d == 0), stop=(d == 1))
                        fill(m, ("B", "dn", j, c))

        def B_act(act):
            yt_act(act, "B")
            split_y_act(act, 0)
            split_e_act(act, 0)
            split_y_act(act, 1)
            act.wait_ge(s_blg, 1)
            act.activation(b_s[:, :, :], b_lg[:, :, :], ACT.Exp).then_inc(s_bex, 1)
            for i in range(NIT):
                e, w = i // 2, i % 2
                for d in range(2):
                    n = 2 * i + d
                    if n >= 4:
                        act.wait_ge(s_bt, n - 3)
                    have(act, ("B", "gu", i, d, 0))
                    act.activation(b_sg[:, w, d, :], b_g[:, w, d, :], ACT.Sigmoid, scale=1.702).then_inc(s_bsg, 1)
                    if n >= 4:
                        act.wait_ge(s_bh, n - 3)
                    o = take(act, ("B", "gu", i, d, 1))
                    empty(act.activation(b_u[:, w, d, :], o[:, :], ACT.Identity, bias=col("bgu", e * 4 + 2 + d)),
                          ("B", "gu", i, d, 1))
                if w == 0 and e + 1 < NE:
                    split_e_act(act, e + 1)

        def B_pool(pool, C):
            for i in range(NIT):
                w = i % 2
                for d in range(2):
                    n = 2 * i + d
                    pool.wait_ge(s_bsg, n + 1)
                    pool.tensor_tensor(b_g[:, w, d, :], b_g[:, w, d, :], b_sg[:, w, d, :], ALU.mult).then_inc(s_bt, 1)
                    have(pool, ("B", "gu", i, d, 1))
                    pool.tensor_scalar(b_u[:, w, d, :], b_u[:, w, d, :], -7.0, 7.0, ALU.max, ALU.min)\
                        .then_inc(s_bu, 1)

        def B_dve(dve, V):
            split_y_dve(dve, 0)
            split_e_dve(dve, 0)
            o = take(dve, ("B", "lg"))
            lgf = b_lg[:, :, :]
            empty(dve.tensor_tensor(lgf, o[:, 0:T * NE].rearrange("p (t e) -> p t e", e=NE),
                                    row("rb").unsqueeze(1).to_broadcast([P, T, NE]), ALU.add), ("B", "lg"))
            V.do(dve.memset(b_z[:, :], 0.0))
            have(dve, ("B", "lg"))
            V.sync()
            for t in range(T):
                V.do(dve.max(out=b_m8[:, t, :], in_=b_lg[:, t, :]))
            V.sync()
            v4 = b_m8[:, :, TOPK - 1:TOPK].to_broadcast([P, T, NE])
            V.do(dve.tensor_tensor(b_gt[:, :, :], lgf, v4, ALU.is_gt))
            V.do(dve.tensor_tensor(b_eq[:, :, :], lgf, v4, ALU.is_equal))
            V.sync()
            for t in range(T):
                V.do(dve.tensor_tensor_scan(b_cs[:, t, :], b_z[:, 0:NE], b_eq[:, t, :], 0.0, ALU.add, ALU.add))
            V.do(dve.tensor_reduce(b_n[:, :], b_gt[:, :, :], AX.X, ALU.add))
            V.sync()
            V.do(dve.tensor_tensor(b_cs[:, :, :], b_cs[:, :, :], b_n[:, :].unsqueeze(2).to_broadcast([P, T, NE]),
                                   ALU.add))
            V.sync()
            V.do(dve.scalar_tensor_tensor(out=b_eq[:, :, :], in0=b_cs[:, :, :], scalar=float(TOPK),
                                          in1=b_eq[:, :, :], op0=ALU.is_le, op1=ALU.mult))
            V.sync()
            V.do(dve.tensor_tensor(b_gt[:, :, :], b_gt[:, :, :], b_eq[:, :, :], ALU.add))
            dve.tensor_tensor(lgf, lgf, b_m8[:, :, 0:1].to_broadcast([P, T, NE]), ALU.subtract).then_inc(s_blg, 1)
            V.sync()
            dve.wait_ge(s_bex, 1)
            V.do(dve.tensor_tensor(b_s[:, :, :], b_s[:, :, :], b_gt[:, :, :], ALU.mult))
            V.sync()
            V.do(dve.tensor_reduce(b_n[:, :], b_s[:, :, :], AX.X, ALU.add))
            V.sync()
            V.do(dve.reciprocal(b_n[:, :], b_n[:, :]))
            V.sync()
            dve.tensor_tensor(b_s[:, :, :], b_s[:, :, :], b_n[:, :].unsqueeze(2).to_broadcast([P, T, NE]),
                              ALU.mult).then_inc(s_bs, 1)

            def gate(i):
                e, w = i // 2, i % 2
                for d in range(2):
                    if i >= 2:
                        dve.wait_ge(s_bh, 2 * (i - 2) + d + 1)
                    o = take(dve, ("B", "gu", i, d, 0))
                    empty(dve.tensor_scalar(b_g[:, w, d, :], o[:, :], col("bgu", e * 4 + d), 7.0,
                                            ALU.add, ALU.min), ("B", "gu", i, d, 0))

            def hidden(i):
                w = i % 2
                for d in range(2):
                    n = 2 * i + d
                    if i >= 2:
                        bk, m = uses[("B", "dn", i - 2, 1)]
                        dve.wait_ge(filled[bk], m + 1)
                    dve.wait_ge(s_bt, n + 1)
                    dve.wait_ge(s_bu, n + 1)
                    dve.scalar_tensor_tensor(out=b_h[:, w, d, :], in0=b_u[:, w, d, :], scalar=1.0,
                                             in1=b_g[:, w, d, :], op0=ALU.add, op1=ALU.mult).then_inc(s_bh, 1)

            def add_out(i):
                e, half = i // 2, i % 2
                for c in range(2):
                    o = take(dve, ("B", "dn", i, c))
                    for q in range(2):
                        t = half * 4 + 2 * c + q
                        m = dve.scalar_tensor_tensor(out=x[:, t, :], in0=o[:, q * D:q * D + D],
                                                     scalar=b_s[:, t, e:e + 1], in1=x[:, t, :],
                                                     op0=ALU.mult, op1=ALU.add)
                        if q == 0:
                            V.do(m)
                    empty(m, ("B", "dn", i, c))

            split_y_dve(dve, 1)
            gate(0)
            for c in range(2):
                o = take(dve, ("B", "sT", c))
                empty(dve.tensor_copy(b_sT[0:NE, c * 512:c * 512 + 512], o[0:NE, :]), ("B", "sT", c))
            for c in range(4):
                o = take(dve, ("B", "bd", c))
                xb = x[:, 2 * c:2 * c + 2, :].rearrange("p t d -> p (t d)")
                empty(dve.tensor_tensor(xb, xb, o[:, :], ALU.add), ("B", "bd", c))
            for c in range(4):
                have(dve, ("B", "bd", c))
            dve.wait_ge(s_bs, 1)
            hidden(0)
            for i in range(1, NIT):
                gate(i)
                if i >= 2:
                    if i >= 3:
                        have(dve, ("B", "dn", i - 3, 1))
                        V.sync()
                    add_out(i - 2)
                if i % 2 == 1 and i + 1 < NIT:
                    split_e_dve(dve, (i + 1) // 2)
                hidden(i)
            V.sync()
            add_out(NIT - 2)
            V.sync()
            add_out(NIT - 1)
            have(dve, ("B", "dn", NIT - 1, 0))
            have(dve, ("B", "dn", NIT - 1, 1))

        for c in range(4):
            plan(("C", "qT", c), c)
        for t in range(T):
            plan(("C", "o", t), 4 + t % 4)

        def C_pe(pe):
            pe.wait_ge(s_cb, 1)
            pe.wait_ge(s_cq, 1)
            for c in range(4):
                o = claim(pe, ("C", "qT", c))
                ob = o[:, :].bitcast(BF16)
                for k in range(KD):
                    for h in range(2):
                        m = pe.transpose(ob[:, k * 256 + h * P:k * 256 + h * P + P], c_q[:, 2 * c + h, k, :],
                                         identb[:, :])
                fill(m, ("C", "qT", c))
            for t in range(T):
                o = claim(pe, ("C", "o", t))
                have(pe, ("C", "qT", t // 2))
                for k in range(KD):
                    m = pe.matmul(o[:, k * 256:k * 256 + 256], c_qT[:, k, t * P:t * P + P],
                                  cw_q[:, k, t // 2, :, :].rearrange("p a n -> p (a n)"), start=True, stop=True)
                fill(m, ("C", "o", t))

        def C_act(act):
            for c in range(4):
                o = take(act, ("C", "qT", c))
                empty(act.copy(c_qT[:, :, c * 256:c * 256 + 256],
                               o[:, :].bitcast(BF16)[:, 0:512].rearrange("p (k n) -> p k n", k=KD)), ("C", "qT", c))

        def C_dve(dve, V):
            yb = y[:, :, :].rearrange("p t (k n) -> p (t k) n", k=2)
            flat = "p t k -> p (t k)"
            dve.wait_ge(s_y, 8 * K_C + 8)
            V.do(dve.tensor_reduce(c_ax[:, :, :].rearrange(flat), yb, AX.X, ALU.max, apply_absolute_value=True))
            V.sync()
            V.do(dve.tensor_scalar(c_sx[:, :, :], c_ax[:, :, :], 1e-4, 1.0 / FP8_MAX, ALU.max, ALU.mult))
            V.sync()
            V.do(dve.reciprocal(c_rx[:, :, :], c_sx[:, :, :]))
            V.sync()
            V.do(dve.tensor_tensor(c_v.rearrange("p t k n -> p (t k) n"), yb,
                                   c_rx[:, :, :].rearrange(flat).unsqueeze(2).to_broadcast([P, 16, P]), ALU.mult))
            for t in range(T):
                for k in range(KD):
                    V.do(dve.tensor_scalar(c_c[:, t, k, :], c_sw[:, k, t // 2, :], c_sx[:, t, k:k + 1], None,
                                           ALU.mult))
            V.sync()
            fp8_round(dve, V, c_v.rearrange("p t k n -> p (t k n)"), c_e, c_m,
                      c_q.rearrange("p t k n -> p (t k n)"))
            V.sync()
            dve.tensor_copy(c_ax[:, 0, 0:1], c_sx[:, 0, 0:1]).then_inc(s_cq, 1)
            for t in range(T):
                o = take(dve, ("C", "o", t))
                for k in range(KD):
                    for n in range(2):
                        xs_ = x[:, t, n * P:n * P + P]
                        m = dve.scalar_tensor_tensor(out=xs_, in0=o[:, k * 256 + n * P:k * 256 + n * P + P],
                                                     scalar=c_c[:, t, k, n:n + 1], in1=xs_,
                                                     op0=ALU.mult, op1=ALU.add)
                        if (k, n) != (1, 1):
                            V.do(m)
                    if k == 0:
                        V.sync()
                empty(m, ("C", "o", t))
            for t in range(T):
                have(dve, ("C", "o", t))

        d_reg = Region(14800, 27600)
        d_gw = d_reg.take([KD, INTER])
        d_uw = d_reg.take([KD, INTER])
        d_dw = d_reg.take([NI, D])
        d_h = d_reg.take([NI, 512])
        d_sg = d_reg.take([2, 512])
        d_t = d_reg.take([2, 512])
        d_o = d_reg.take([2, 512])
        s_dw, s_dsg = sem("d_loaded"), sem("d_sig")
        for b in range(B):
            plan(("D", "yt", b), b)
        di = 4
        for half in range(2):
            for it in range(NI):
                for gu in range(2):
                    plan(("D", "gu", half, it, gu), di % 8)
                    di += 1
            for c in range(2):
                plan(("D", "dn", half, c), di % 8)
                di += 1
        rows_of = [P] * (NI - 1) + [INTER - P * (NI - 1)]

        def D_sp(sp):
            sp.dma_start(d_gw, gwT_d).then_inc(s_dw, 16)
            sp.dma_start(d_uw, uwT_d).then_inc(s_dw, 16)
            sp.dma_start(d_dw[:, 0:NI - 1, :], dwT_d[0:(NI - 1) * P, :].rearrange("(i p) d -> p i d", p=P))\
                .then_inc(s_dw, 16)
            sp.dma_start(d_dw[0:rows_of[-1], NI - 1, :], dwT_d[(NI - 1) * P:INTER, :]).then_inc(s_dw, 16)

        def D_pe(pe):
            yt_pe(pe, K_D, "D")
            pe.wait_ge(s_dw, 64)
            for half in range(2):
                have(pe, ("D", "yt", 2 * half))
                have(pe, ("D", "yt", 2 * half + 1))
                for it in range(NI):
                    r = rows_of[it]
                    for gu, w in enumerate((d_gw, d_uw)):
                        key = ("D", "gu", half, it, gu)
                        o = claim(pe, key)
                        for k in range(KD):
                            m = pe.matmul(o[0:r, :], w[:, k, it * P:it * P + r],
                                          yT[:, k, half * 512:half * 512 + 512], start=(k == 0), stop=(k == 1))
                        fill(m, key)
                for c in range(2):
                    key = ("D", "dn", half, c)
                    o = claim(pe, key)
                    pe.wait_ge(emptied[uses[("D", "gu", half, NI - 1, 1)][0]],
                               uses[("D", "gu", half, NI - 1, 1)][1] + 1)
                    for q in range(2):
                        for it in range(NI):
                            r = rows_of[it]
                            m = pe.matmul(o[:, q * D:q * D + D], d_h[0:r, it, (2 * c + q) * P:(2 * c + q) * P + P],
                                          d_dw[0:r, it, :], start=(it == 0), stop=(it == NI - 1))
                    fill(m, key)

        def D_act(act):
            yt_act(act, "D")
            for half in range(2):
                for it in range(NI):
                    n = half * NI + it
                    r = rows_of[it]
                    if n >= 2:
                        have(act, ("D", "gu", (n - 2) // NI, (n - 2) % NI, 0))
                    o = take(act, ("D", "gu", half, it, 0))
                    act.activation(d_sg[0:r, n % 2, :], o[0:r, :], ACT.Sigmoid, scale=col("gs", it, r))\
                        .then_inc(s_dsg, 1)

        def D_dve(dve, V):
            for half in range(2):
                for it in range(NI):
                    n = half * NI + it
                    r = rows_of[it]
                    dve.wait_ge(s_dsg, n + 1)
                    o = take(dve, ("D", "gu", half, it, 0))
                    empty(dve.scalar_tensor_tensor(out=d_t[0:r, n % 2, :], in0=o[0:r, :], scalar=col("gs", it, r),
                                                   in1=d_sg[0:r, n % 2, :], op0=ALU.mult, op1=ALU.mult),
                          ("D", "gu", half, it, 0))
                    have(dve, ("D", "gu", half, it, 0))
                    o = take(dve, ("D", "gu", half, it, 1))
                    if half == 1 and it == 0:
                        bk, m_ = uses[("D", "dn", 0, 1)]
                        dve.wait_ge(filled[bk], m_ + 1)
                    empty(dve.scalar_tensor_tensor(out=d_h[0:r, it, :], in0=o[0:r, :], scalar=col("us", it, r),
                                                   in1=d_t[0:r, n % 2, :], op0=ALU.mult, op1=ALU.mult),
                          ("D", "gu", half, it, 1))
                for c in range(2):
                    key = ("D", "dn", half, c)
                    o = take(dve, key)
                    empty(dve.tensor_tensor(d_o[:, c, :].rearrange("p (q d) -> p q d", q=2),
                                            o[:, :].rearrange("p (q d) -> p q d", q=2),
                                            row("ds").unsqueeze(1).to_broadcast([P, 2, D]), ALU.mult), key)
                    have(dve, key)
                    t = half * 4 + 2 * c
                    xb = x[:, t:t + 2, :].rearrange("p t d -> p (t d)")
                    V.do(dve.tensor_tensor(xb, xb, d_o[:, c, :], ALU.add))

        e_reg = Region(0, 14800)
        e_cm = e_reg.take([8, 256])
        e_v = e_reg.take([T, NH, 32])
        e_sel = e_reg.take([NH, P], BF16)
        e_mp = e_reg.take([T * P], BF16)
        e_wif = e_reg.take([6, 32])
        e_hT = e_reg.take([4, 256])
        e_reg2 = Region(14800, 27600)
        e_i = e_reg2.take([T * P])
        e_f = e_reg2.take([T * P])
        e_l = e_reg2.take([T * P])
        e_F = e_reg2.take([T * P])
        e_M = e_reg2.take([T * P])
        e_D = e_reg2.take([8, 384])
        e_C = e_reg2.take([8, 384])
        e_h = e_reg2.take([2, NH, DH])
        e_q = e_reg2.take([2, NH, DH])
        e_hs = e_l.rearrange("p (q n) -> p q n", q=2)
        e_aT = sb("e_aT", [P, T, NH])
        e_em = sb("e_em", [P, T, NH])
        e_n = sb("e_n", [P, 2, NH])
        e_r = sb("e_r", [P, 2, NH])
        s_eprep, s_wif = sem("e_ctx_prepared"), sem("e_weights_loaded")
        s_e1, s_e2, s_emp, s_eM, s_em = (sem("e_absf"), sem("e_log1p"), sem("e_negM_parts"), sem("e_a_and_m"),
                                         sem("e_exp_m"))
        s_ev, s_er = sem("e_head_var"), sem("e_head_rstd")
        NB = B * NH
        for b in range(B):
            plan(("E", "yt", b), b)
        for half in range(2):
            for gi_ in range(2):
                plan(("E", "g", half, gi_), 4 + 2 * half + gi_)
        plan(("E", "tr"), 0)
        NQ = NB // 4

        def head(n):
            b, quad, i = n // NH, n % NH // 4, n % 4
            return b, 8 * (quad // 2) + 2 * i + quad % 2, i

        ld_bank = 1
        for s_ in range(NQ + 3):
            if s_ < NQ:
                for i in range(4):
                    plan(("E", "ld", 4 * s_ + i), ld_bank)
                    ld_bank ^= 1
                for i in range(4):
                    plan(("E", "qk", 4 * s_ + i), 2 + i)
            if s_ >= 6 and s_ % 4 == 2:
                for q in range(2):
                    plan(("E", "hv", s_ // 4 - 1, q), ld_bank)
                    ld_bank ^= 1
            if 1 <= s_ <= NQ and (s_ - 1) % 2 == 0:
                plan(("E", "hT", (s_ - 1) // 2), 6 + (s_ - 1) // 2 % 2)

        def E_sp(sp):
            sp.wait_ge(s_stage, 2)
            sp.dma_start(e_wif, wif_d).then_inc(s_wif, 16)

        def E_prep_pool(pool, C):
            pool.wait_ge(s_stage, 2)
            C.do(pool.memset(e_v, 1.0))
            C.do(pool.memset(e_mp, 0.0))
            C.sync()
            for t in range(T):
                C.do(pool.tensor_copy(e_v[:, t, :, 0:DH], cx[:, t, :].rearrange("p (h c) -> p h c", c=DH)))
            pool.tensor_copy(e_sel[0:96, :, :], cst[0:96, 296:312].unsqueeze(2).to_broadcast([96, NH, P]))\
                .then_inc(s_eprep, 1)

        def E_pe(pe):
            yt_pe(pe, K_E, "E")
            pe.wait_ge(s_wif, 16)
            for half in range(2):
                have(pe, ("E", "yt", 2 * half))
                have(pe, ("E", "yt", 2 * half + 1))
                for gi_ in range(2):
                    o = claim(pe, ("E", "g", half, gi_))
                    for k in range(6):
                        src = yT[:, k, :] if k < KD else cxT[:, k % KD, :]
                        m = pe.matmul(o[0:NH, :], e_wif[:, k, gi_ * NH:gi_ * NH + NH],
                                      src[:, half * 512:half * 512 + 512], start=(k == 0), stop=(k == 5))
                    fill(m, ("E", "g", half, gi_))
            o = claim(pe, ("E", "tr"))
            pe.wait_ge(s_eM, 1)
            for w, src in enumerate((e_i, e_f)):
                for t in range(T):
                    m = pe.transpose(o[:, (w * T + t) * NH:(w * T + t) * NH + NH], src[0:NH, t * P:t * P + P],
                                     ident[0:NH, 0:NH])
            fill(m, ("E", "tr"))
            pe.wait_ge(s_emp, 1)
            pe.wait_ge(s_eprep, 1)
            for s_ in range(NQ + 3):
                if s_ < NQ:
                    for n2 in (4 * s_, 4 * s_ + 2):
                        for n in (n2, n2 + 1):
                            b, h, _ = head(n)
                            o = claim(pe, ("E", "ld", n))
                            pe.matmul(o[:, 0:256], e_sel[0:96, h, :], e_mp[0:96, b * 256:b * 256 + 256],
                                      start=True, stop=False, skip_group_check=True)
                            pe.matmul(o[:, 256:384], e_sel[0:96, h, :], e_mp[0:96, b * 256 + P:b * 256 + 256],
                                      start=False, stop=False, skip_group_check=True)
                            pe.matmul(o[:, 0:P], identb[:, :], causal[:, :], start=False, stop=False,
                                      skip_group_check=True)
                            fill(pe.matmul(o[:, 256:384], identb[:, :], causal[:, :], start=False, stop=True,
                                           skip_group_check=True), ("E", "ld", n))
                        for n in (n2, n2 + 1):
                            b, h, _ = head(n)
                            o = claim(pe, ("E", "qk", n))
                            pe.wait_ge(s_ecm, n + 1)
                            for tb in range(2):
                                m = pe.matmul(o[:, 256 * tb:256 * tb + 256 - P * tb], e_cm[:, n % 8, tb * P:tb * P + P],
                                              yT[:, h // 8, b * 256 + tb * P:b * 256 + 256], start=True, stop=True)
                            fill(m, ("E", "qk", n))
                if s_ >= 6 and s_ % 4 == 2:
                    b = s_ // 4 - 1
                    have(pe, ("E", "hT", 2 * b))
                    have(pe, ("E", "hT", 2 * b + 1))
                    for q in range(2):
                        o = claim(pe, ("E", "hv", b, q))
                        for gr in range(4):
                            m = pe.transpose(o[:, gr * P:gr * P + P], e_hT[:, gr, q * P:q * P + P], ident)
                        fill(m, ("E", "hv", b, q))
                if 1 <= s_ <= NQ:
                    c, odd = (s_ - 1) // 2, (s_ - 1) % 2
                    o = psum[uses[("E", "hT", c)][0]]
                    if not odd:
                        claim(pe, ("E", "hT", c))
                    for tb in range(2):
                        for j in range(4 * s_ - 4, 4 * s_):
                            b, h, i = head(j)
                            if tb == 0:
                                have(pe, ("E", "qk", j))
                            r, c0 = 32 * i, 256 * odd
                            m = pe.matmul(o[r:r + 32, c0 + tb * P:c0 + 256], e_v[:, 2 * b + tb, h, :],
                                          e_C[:, j % 8, 256 * tb:256 * tb + 256 - P * tb],
                                          start=(tb == 0), stop=(tb == 1))
                    if odd:
                        fill(m, ("E", "hT", c))
                    else:
                        m.then_inc(s_ehv, 1)

        s_ehv, s_ecm = sem("e_quad_used"), sem("e_ctx_masked")

        def used_C(eng, quad):
            if quad % 2:
                take(eng, ("E", "hT", quad // 2))
            else:
                eng.wait_ge(s_ehv, quad // 2 + 1)

        def E_act(act):
            yt_act(act, "E")
            act.wait_ge(s_e1, 1)
            act.activation(e_l[0:NH, :], e_l[0:NH, :], ACT.Exp, scale=-1.0).then_inc(s_e2, 1)
            act.wait_ge(s_e2, 1)
            act.activation(e_l[0:NH, :], e_l[0:NH, :], ACT.Ln, bias=1.0).then_inc(s_e2, 1)
            o = take(act, ("E", "tr"))
            act.wait_ge(s_em, 1)
            empty(act.activation(e_em[:, :, :], o[:, P:256].rearrange("p (t h) -> p t h", h=NH), ACT.Exp,
                                 scale=-1.0), ("E", "tr"))
            for s_ in range(NQ + 3):
                if s_ < NQ:
                    for n in range(4 * s_, 4 * s_ + 4):
                        b, h, _ = head(n)
                        if n >= 8:
                            have(act, ("E", "qk", n - 8))
                        o = take(act, ("E", "ld", n))
                        act.activation(e_D[:, n % 8, 0:256], o[:, 0:256], ACT.Exp, bias=e_aT[:, 2 * b, h:h + 1])
                        empty(act.activation(e_D[:, n % 8, 256:384], o[:, 256:384], ACT.Exp,
                                             bias=e_aT[:, 2 * b + 1, h:h + 1]), ("E", "ld", n))
                if s_ >= 3 and s_ % 2 == 1 and (s_ - 3) // 2 < 2 * B:
                    c = (s_ - 3) // 2
                    if c >= 2:
                        take(act, ("E", "hv", c // 2 - 1, 1))
                    o = take(act, ("E", "hT", c))
                    empty(act.copy(e_hT[:, 2 * (c % 2):2 * (c % 2) + 2, :],
                                   o[:, :].rearrange("p (g s) -> p g s", g=2)), ("E", "hT", c))
                if s_ >= 6 and s_ % 4 == 2:
                    b = s_ // 4 - 1
                    if b >= 1:
                        act.wait_ge(s_ev, b)
                    for q in range(2):
                        o = take(act, ("E", "hv", b, q))
                        for k in range(2):
                            m = act.copy(e_hs[:, q, k * 256:k * 256 + 256].rearrange("p (i r c) -> p i r c", i=4, r=2),
                                         o[:, k * 256:k * 256 + 256].rearrange("p (r i c) -> p i r c", r=2, i=4))
                        empty(m, ("E", "hv", b, q))

        def E_dve(dve, V):
            def mask_ctx(quad):
                for n in range(4 * quad, 4 * quad + 4):
                    b, h, _ = head(n)
                    dve.tensor_scalar(e_cm[:, n % 8, :], cxT[:, h // 8, b * 256:b * 256 + 256],
                                      cst[:, 256 + h % 8:257 + h % 8], None, ALU.mult).then_inc(s_ecm, 1)

            mask_ctx(0)
            mask_ctx(1)
            h16 = slice(0, NH)
            for half in range(2):
                hs = slice(half * 512, half * 512 + 512)
                for gi_, (dst, bias) in enumerate(((e_i, "bi"), (e_f, "bf"))):
                    o = take(dve, ("E", "g", half, gi_))
                    empty(dve.tensor_scalar(dst[h16, hs], o[h16, :], col(bias, 0, NH), None, ALU.add),
                          ("E", "g", half, gi_))
            for half in range(2):
                have(dve, ("E", "g", half, 0))
                have(dve, ("E", "g", half, 1))
            dve.scalar_tensor_tensor(out=e_l[h16, :], in0=e_f[h16, :], scalar=-1.0, in1=e_f[h16, :],
                                     op0=ALU.mult, op1=ALU.max).then_inc(s_e1, 1)
            dve.wait_ge(s_e2, 2)
            V.do(dve.scalar_tensor_tensor(out=e_l[h16, :], in0=e_f[h16, :], scalar=0.0, in1=e_l[h16, :],
                                          op0=ALU.min, op1=ALU.subtract))
            V.sync()
            for b in range(B):
                bs = slice(b * 256, b * 256 + 256)
                V.do(dve.tensor_tensor_scan(e_F[h16, bs], b_z[h16, :], e_l[h16, bs], 0.0, ALU.add, ALU.add))
            V.sync()
            V.do(dve.tensor_tensor(e_i[h16, :], e_i[h16, :], e_F[h16, :], ALU.subtract))
            V.sync()
            for b in range(B):
                bs = slice(b * 256, b * 256 + 256)
                V.do(dve.tensor_tensor_scan(e_M[h16, bs], e_i[h16, bs], e_i[h16, bs], -3e38, ALU.max, ALU.max))
            V.sync()
            dve.tensor_tensor(e_f[h16, :], e_F[h16, :], e_M[h16, :], ALU.add).then_inc(s_eM, 1)
            dve.wait_ge(s_eprep, 1)
            V.do(dve.tensor_scalar(e_mp[0:NH, :], e_M[h16, :], -1.0, None, ALU.mult))
            V.sync()
            V.do(dve.scalar_tensor_tensor(out=e_l[h16, :], in0=e_M[h16, :], scalar=-1.0, in1=e_mp[0:NH, :],
                                          op0=ALU.mult, op1=ALU.subtract))
            V.sync()
            V.do(dve.tensor_copy(e_mp[32:32 + NH, :], e_l[h16, :]))
            V.do(dve.tensor_copy(e_F[h16, :].bitcast(BF16)[:, 0:T * P], e_l[h16, :]))
            V.sync()
            V.do(dve.tensor_tensor(e_l[h16, :], e_l[h16, :], e_F[h16, :].bitcast(BF16)[:, 0:T * P], ALU.subtract))
            V.sync()
            dve.tensor_copy(e_mp[64:64 + NH, :], e_l[h16, :]).then_inc(s_emp, 1)
            o = take(dve, ("E", "tr"))
            dve.tensor_copy(e_aT[:, :, :], o[:, 0:P].rearrange("p (t h) -> p t h", h=NH)).then_inc(s_em, 1)
            have(dve, ("E", "tr"))

            def post_a(b):
                have(dve, ("E", "hv", b, 0))
                have(dve, ("E", "hv", b, 1))
                hv = e_hs.rearrange("p q (h c) -> p q h c", c=32)
                V.do(dve.scalar_tensor_tensor(out=e_n[:, :, :], in0=hv[:, :, :, DH], scalar=-1.0,
                                              in1=e_em[:, 2 * b:2 * b + 2, :], op0=ALU.mult, op1=ALU.max))
                V.sync()
                V.do(dve.tensor_tensor(e_n[:, :, :], hv[:, :, :, DH], e_n[:, :, :], ALU.max))
                V.sync()
                V.do(dve.tensor_scalar(e_n[:, :, :], e_n[:, :, :], 1e-6, None, ALU.add))
                V.sync()
                V.do(dve.reciprocal(e_n[:, :, :], e_n[:, :, :]))
                V.sync()
                for q in range(2):
                    V.do(dve.tensor_tensor(e_h[:, q, :, :], hv[:, q, :, 0:DH],
                                           e_n[:, q, :].unsqueeze(2).to_broadcast([P, NH, DH]), ALU.mult))
                V.sync()
                hf = e_h.rearrange("p q h c -> p (q h) c")
                qf = e_q.rearrange("p q h c -> p (q h) c")
                nf = e_n[:, :, :].rearrange("p q h -> p (q h)")
                V.do(dve.tensor_reduce(nf, hf, AX.X, ALU.add))
                V.sync()
                V.do(dve.tensor_scalar(nf, nf, 1.0 / DH, None, ALU.mult))
                V.sync()
                V.do(dve.tensor_tensor(hf, hf, nf.unsqueeze(2).to_broadcast([P, 2 * NH, DH]), ALU.subtract))
                V.sync()
                V.do(dve.tensor_tensor(qf, hf, hf, ALU.mult))
                V.sync()
                dve.tensor_reduce(e_r[:, :, :].rearrange("p q h -> p (q h)"), qf, AX.X, ALU.add).then_inc(s_ev, 1)

            def post_b(b):
                dve.wait_ge(s_er, b + 1)
                hf = e_h.rearrange("p q h c -> p (q h) c")
                V.do(dve.tensor_tensor(hf, hf, e_r[:, :, :].rearrange("p q h -> p (q h)").unsqueeze(2)
                                       .to_broadcast([P, 2 * NH, DH]), ALU.mult))
                V.sync()
                h2 = e_h.rearrange("p q h c -> p q (h c)")
                V.do(dve.tensor_tensor(h2, h2, row("lns").unsqueeze(1).to_broadcast([P, 2, D]), ALU.mult))
                V.sync()
                V.do(dve.tensor_tensor(x[:, 2 * b:2 * b + 2, :], x[:, 2 * b:2 * b + 2, :], h2, ALU.add))

            for s_ in range(NQ + 6):
                if s_ < NQ:
                    if s_ >= 2:
                        used_C(dve, s_ - 2)
                    for n in range(4 * s_, 4 * s_ + 4):
                        have(dve, ("E", "ld", n))
                        o = take(dve, ("E", "qk", n))
                        empty(dve.scalar_tensor_tensor(out=e_C[:, n % 8, :], in0=o[:, 0:384], scalar=0.25,
                                                       in1=e_D[:, n % 8, :], op0=ALU.mult, op1=ALU.mult),
                              ("E", "qk", n))
                if s_ + 2 < NQ:
                    mask_ctx(s_ + 2)
                if s_ >= 7 and s_ % 4 == 3:
                    post_a(s_ // 4 - 1)
                if s_ >= 9 and s_ % 4 == 1:
                    post_b(s_ // 4 - 2)

        def E_pool(pool, C):
            for b in range(B):
                pool.wait_ge(s_ev, b + 1)
                C.do(pool.tensor_scalar(e_r[:, :, :], e_r[:, :, :], 1.0 / DH, 1e-6, ALU.mult, ALU.add))
                C.sync()
                pool.tensor_tensor(e_r[:, :, :].rearrange("p q h -> p (q h)"),
                                   e_r[:, :, :].rearrange("p q h -> p (q h)"), mhalf[:, :], ALU.pow)\
                    .then_inc(s_er, 1)

        f_reg = Region(0, 14800)
        f_w = f_reg.take([KD, D])
        f_wq = f_reg.take([KD, D], BF16)
        f_v = f_reg.take([T, D])
        f_q = f_reg.take([T, D], BF16)
        f_qT = f_reg.take([KD, T * P], BF16)
        f_al = sb("f_al", [P, 4])
        f_s = sb("f_s", [P, 3, T])
        s_fw, s_fa, s_far, s_fq = sem("f_loaded"), sem("f_abs_sum"), sem("f_abs_all"), sem("f_quantised")
        for c in range(4):
            plan(("F", "qT", c), c)
        for c in range(4):
            plan(("F", "o", c), 4 + c)

        def F_sp(sp):
            sp.wait_ge(s_stage, 5)
            sp.dma_start(f_w, w2T_d).then_inc(s_fw, 16)

        def F_pool(pool, C):
            pool.wait_ge(s_fa, 1)
            pool.partition_all_reduce(f_al[:, 1:2], f_al[:, 0:1], P, RADD).then_inc(s_far, 1)

        def F_pe(pe):
            pe.wait_ge(s_fq, 1)
            for c in range(4):
                o = claim(pe, ("F", "qT", c))
                ob = o[:, :].bitcast(BF16)
                for k in range(KD):
                    for h in range(2):
                        m = pe.transpose(ob[:, k * 256 + h * P:k * 256 + h * P + P],
                                         f_q[:, 2 * c + h, k * P:k * P + P], identb[:, :])
                fill(m, ("F", "qT", c))
            for c in range(4):
                o = claim(pe, ("F", "o", c))
                have(pe, ("F", "qT", c))
                for h in range(2):
                    t = 2 * c + h
                    for k in range(KD):
                        m = pe.matmul(o[:, h * D:h * D + D], f_qT[:, k, t * P:t * P + P], f_wq[:, k, :],
                                      start=(k == 0), stop=(k == 1))
                fill(m, ("F", "o", c))

        def F_act(act):
            for c in range(4):
                o = take(act, ("F", "qT", c))
                empty(act.copy(f_qT[:, :, c * 256:c * 256 + 256],
                               o[:, :].bitcast(BF16)[:, 0:512].rearrange("p (k n) -> p k n", k=KD)), ("F", "qT", c))

        def F_dve(dve, V):
            dve.wait_ge(s_fw, 16)
            wf = f_w.rearrange("p k d -> p (k d)")
            dve.tensor_reduce(f_al[:, 0:1], wf, AX.X, ALU.add, apply_absolute_value=True).then_inc(s_fa, 1)
            dve.wait_ge(s_y, 8 * K_F + 8)
            V.do(dve.tensor_tensor(x[:, :, :], x[:, :, :], row("b2f").unsqueeze(1).to_broadcast([P, T, D]), ALU.add))
            V.do(dve.tensor_reduce(f_s[:, 0, :], y[:, :, :], AX.X, ALU.max, apply_absolute_value=True))
            V.sync()
            V.do(dve.tensor_scalar(f_s[:, 0, :], f_s[:, 0, :], 1e-5, 1.0 / 127.0, ALU.max, ALU.mult))
            V.sync()
            V.do(dve.reciprocal(f_s[:, 1, :], f_s[:, 0, :]))
            V.sync()
            for t in range(T):
                V.do(dve.tensor_scalar(f_v[:, t, :], y[:, t, :], f_s[:, 1, t:t + 1], ROUND23, ALU.mult, ALU.add))
            V.sync()
            V.do(dve.tensor_scalar(f_v, f_v, ROUND23, -128.0, ALU.subtract, ALU.max))
            V.sync()
            V.do(dve.tensor_scalar(f_q, f_v, 127.0, None, ALU.min))
            dve.wait_ge(s_far, 1)
            V.do(dve.tensor_scalar(f_al[:, 2:3], f_al[:, 1:2], 1.0 / (D * D), 1e-5, ALU.mult, ALU.max))
            V.sync()
            V.do(dve.reciprocal(f_al[:, 3:4], f_al[:, 2:3]))
            V.do(dve.tensor_scalar(f_s[:, 2, :], f_s[:, 0, :], f_al[:, 2:3], None, ALU.mult))
            V.sync()
            V.do(dve.tensor_scalar(wf, wf, f_al[:, 3:4], ROUND23, ALU.mult, ALU.add))
            V.sync()
            V.do(dve.tensor_scalar(wf, wf, ROUND23, -1.0, ALU.subtract, ALU.max))
            V.sync()
            dve.tensor_scalar(f_wq.rearrange("p k d -> p (k d)"), wf, 1.0, None, ALU.min).then_inc(s_fq, 1)
            for c in range(4):
                o = take(dve, ("F", "o", c))
                for h in range(2):
                    t = 2 * c + h
                    m = dve.scalar_tensor_tensor(out=x[:, t, :], in0=o[:, h * D:h * D + D], scalar=f_s[:, 2, t:t + 1],
                                                 in1=x[:, t, :], op0=ALU.mult, op1=ALU.add)
                    if h == 0:
                        V.do(m)
                empty(m, ("F", "o", c))
            for c in range(4):
                have(dve, ("F", "o", c))

        NG = G * B
        SCALE = float(HD) ** -0.5
        g_reg = Region(G_AT, 33416)
        g_tmp = [g_reg.take([KD, T * P]) for _ in range(2)]
        g_vb = g_reg.take([KD, T * P], BF16)
        g_eb = g_reg.take([KD * T * P], BF16)
        g_mb = [g_reg.take([KD, T * P], BF16) for _ in range(2)]
        g_reg.at = G_AT
        g_n = [g_reg.take([12, P]) for _ in range(2)]
        g_t = [g_reg.take([6, 256]) for _ in range(2)]
        g_v = [g_reg.take([2, 2, P]) for _ in range(3)]
        g_pt = g_reg.take([4, 2, 256])
        g_o = [g_reg.take([4, 256]) for _ in range(2)]
        g_om = [g_reg.take([4 * 256], BF16) for _ in range(2)]
        g_p = [y[:, :, :].rearrange("p t d -> p (t d)").rearrange("p (c q s) -> p c q s", c=4, q=2),
               yT[:, :, :].rearrange("p t d -> p (t d)").rearrange("p (c q s) -> p c q s", c=4, q=2)]
        cw_flat = cw_q[:, :, :, :, :].rearrange("p k b m n -> p (k b m n)")
        g_ob, g_oe = cw_flat[:, 0:1024], cw_flat[:, 1024:2048]
        w_reg = Region(33416, ARENA)
        g_wr = w_reg.take([KD, 768])
        g_wpr = w_reg.take([4, D])
        g_wc = [w_reg.take([KD, 256]) for _ in range(2)]
        g_rc = sb("g_rc", [P, 8])
        g_rsm = sb("g_rsm", [P, 32])
        g_bs = sb("g_bs", [P, 12, 6])
        g_mv = [sb(f"g_mv{i}", [P, 12, 2]) for i in range(2)]
        g_rs = [sb(f"g_rs{i}", [P, 12]) for i in range(2)]
        g_w1 = sb("g_w1", [P, 12])
        g_w2 = sb("g_w2", [P, 12])
        g_pc = sb("g_pc", [P, 1])
        g_mx = [sb(f"g_mx{i}", [P, 8]) for i in range(2)]
        g_sm = [sb(f"g_sm{i}", [P, 8]) for i in range(2)]
        s_gw, s_gwp = sem("g_weights_loaded"), sem("g_projection_loaded")
        s_gwc = [sem(f"g_cross_weights_loaded{i}") for i in range(2)]
        s_gwh, s_gwl = sem("g_weights_high"), sem("g_weights_low")
        s_gph, s_gpl = sem("g_projection_high"), sem("g_projection_low")
        g_nb = [sb(f"g_nb{i}", [P, 12]) for i in range(2)]
        s_gri = sem("g_reciprocal_sums")
        s_gk, s_gv1, s_gq, s_gx = sem("g_consts"), sem("g_scaled"), sem("g_rounded"), sem("g_inputs")
        s_gst, s_grs, s_gva, s_gnb, s_gp, s_gt, s_gc = (
            sem("g_stats"), sem("g_rstd"), sem("g_values"), sem("g_bias"), sem("g_probs"), sem("g_magic_sum"),
            sem("g_cat"))
        for b in range(B):
            plan(("G", "yt", b), b)
        gb = [0]

        def nxt(key):
            plan(key, 4 + gb[0] % 4)
            gb[0] += 1

        G_TRANSPOSES = (("pt", 0), ("tr", 0), ("pt", 1), ("tr", 1), ("tr", 2), ("pt", 2), ("pt", 3))
        for i in range(NG + 3):
            for what, c in G_TRANSPOSES:
                j = i - 2 if what == "pt" else i - 1
                if 0 <= j < NG:
                    nxt(("G", what, j, c))
            if i < NG:
                for c in range(4):
                    plan(("G", "qkv", i, c), c)
            if 0 <= i - 1 < NG:
                for c in range(4):
                    nxt(("G", "sc", i - 1, c))
            if 0 <= i - 2 < NG:
                for c in range(2):
                    nxt(("G", "pv", i - 2, c))
            if 0 <= i - 3 < NG:
                nxt(("G", "pj", i - 3))

        def G_sp(sp):
            sp.wait_ge(s_stage, 3)
            for g in range(G):
                if g >= 1:
                    sp.wait_ge(s_gwl, 8 * g)
                sp.dma_start(g_wr, wg_d[g, :, :, 0:768]).then_inc(s_gw, 16)
                if g >= 2:
                    take(sp, ("G", "qkv", 4 * (g - 2) + 3, 3))
                sp.dma_start(g_wc[g % 2], wg_d[g, :, :, 768:1024]).then_inc(s_gwc[g % 2], 16)
                if g >= 1:
                    sp.wait_ge(s_gpl, g)
                sp.dma_start(g_wpr, wp_d[g]).then_inc(s_gwp, 16)

        G_PARTS = ((0, 256, "q"), (256, 256, "qx"), (512, 128, "k"), (640, 128, "v"))

        ALL, FIRST, LAST = slice(0, 4), slice(0, 2), slice(2, 4)

        def split_w_act(act, g, parts):
            act.wait_ge(s_gw, 16 * (g + 1))
            for c0, cw, v in G_PARTS[parts]:
                for k in range(KD):
                    act.activation(g_wh[g % 2][:, k, c0:c0 + cw], g_wr[:, k, c0:c0 + cw], ACT.Identity,
                                   scale=col("sc_" + v, k)).then_inc(s_gwh, 1)

        def split_w_dve(dve, g, parts):
            dve.wait_ge(s_gw, 16 * (g + 1))
            for n in range(4)[parts]:
                c0, cw, v = G_PARTS[n]
                for k in range(KD):
                    dve.wait_ge(s_gwh, 8 * g + 2 * n + k + 1)
                    dve.scalar_tensor_tensor(out=g_wl[g % 2][:, k, c0:c0 + cw], in0=g_wr[:, k, c0:c0 + cw],
                                             scalar=col("sc_" + v, k), in1=g_wh[g % 2][:, k, c0:c0 + cw].bitcast(F32),
                                             op0=ALU.mult, op1=ALU.subtract).then_inc(s_gwl, 1)

        def split_p_act(act, g):
            act.wait_ge(s_gwp, 16 * (g + 1))
            if g >= 2:
                take(act, ("G", "pj", 4 * (g - 2) + 3))
            act.copy(g_ph[g % 2][:, :, :], g_wpr).then_inc(s_gph, 1)

        def split_p_dve(dve, g):
            dve.wait_ge(s_gwp, 16 * (g + 1))
            dve.wait_ge(s_gph, g + 1)
            dve.tensor_tensor(g_pl[g % 2][:, :, :], g_wpr, g_ph[g % 2][:, :, :].bitcast(F32), ALU.subtract)\
                .then_inc(s_gpl, 1)

        def G_pt(pe, j, c):
            if c % 2 == 0:
                pe.wait_ge(s_gp, 2 * j + c // 2 + 1)
            o = claim(pe, ("G", "pt", j, c))
            for kt in range(2):
                for st in range(2):
                    m = pe.transpose(o[:, kt * 256 + st * P:kt * 256 + st * P + P],
                                     g_p[j % 2][:, c, st, kt * P:kt * P + P], ident)
            fill(m, ("G", "pt", j, c))

        def G_tr(pe, j, c):
            o = claim(pe, ("G", "tr", j, c))
            if c == 0:
                for q in range(4):
                    have(pe, ("G", "qkv", j, q))
            for q in range(2):
                for tt in range(2):
                    m = pe.transpose(o[:, q * 256 + tt * P:q * 256 + tt * P + P],
                                     g_n[j % 2][:, tt * 6 + 2 * c + q, :], ident)
            fill(m, ("G", "tr", j, c))

        def G_pe(pe):
            for b in range(B):
                o = claim(pe, ("G", "yt", b))
                pe.wait_ge(s_y, 8 * K_G2 + 2 * b + 2)
                for d in range(KD):
                    for h in range(2):
                        m = pe.transpose(o[:, d * 256 + h * P:d * 256 + h * P + P],
                                         y[:, 2 * b + h, d * P:d * P + P], ident)
                fill(m, ("G", "yt", b))
            pe.wait_ge(s_gx, 4)
            for i in range(NG + 3):
                for what, c in G_TRANSPOSES:
                    if what == "pt" and 0 <= i - 2 < NG:
                        G_pt(pe, i - 2, c)
                    if what == "tr" and 0 <= i - 1 < NG:
                        G_tr(pe, i - 1, c)
                if i < NG:
                    g, b = i // B, i % B
                    if b == 0:
                        pe.wait_ge(s_gwl, 8 * (g + 1))
                        pe.wait_ge(s_gwc[g % 2], 16 * (g // 2 + 1))

                    def linear(o, v, c0, cw):
                        for k in range(KD):
                            for w in (g_wh, g_wl):
                                m = pe.matmul(o, g_xs[v][:, k, ts_], w[g % 2][:, k, c0:c0 + cw],
                                              start=(k == 0 and w is g_wh), stop=(k == 1 and w is g_wl))
                        return m

                    for tt in range(2):
                        ts_ = slice(b * 256 + tt * P, b * 256 + tt * P + P)
                        o = claim(pe, ("G", "qkv", i, tt))
                        linear(o[:, 0:256], 0, 0, 256)
                        fill(linear(o[:, 256:512], 1, 256, 256), ("G", "qkv", i, tt))
                    for tt in range(2):
                        ts_ = slice(b * 256 + tt * P, b * 256 + tt * P + P)
                        o = claim(pe, ("G", "qkv", i, 2 + tt))
                        linear(o[:, 0:P], 2, 512, P)
                        linear(o[:, P:2 * P], 3, 640, P)
                        for k in range(KD):
                            m = pe.matmul(o[:, 256:512], cxT[:, k, ts_], g_wc[g % 2][:, k, :],
                                          start=(k == 0), stop=(k == 1))
                        fill(m, ("G", "qkv", i, 2 + tt))
                if 0 <= i - 1 < NG:
                    j = i - 1
                    for c in range(4):
                        o = claim(pe, ("G", "sc", j, c))
                        have(pe, ("G", "tr", j, c // 2))
                        have(pe, ("G", "tr", j, 2))
                        for st in range(2):
                            m = pe.matmul(o[:, st * 256:st * 256 + 256], g_t[j % 2][:, c, st * P:st * P + P],
                                          g_t[j % 2][:, 4 + c // 2, :], start=True, stop=True)
                        fill(m, ("G", "sc", j, c))
                if 0 <= i - 2 < NG:
                    j = i - 2
                    for a in range(2):
                        o = claim(pe, ("G", "pv", j, a))
                        for q in range(2):
                            have(pe, ("G", "pt", j, 2 * a + q))
                            for kt in range(2):
                                m = pe.matmul(o[:, q * 256:q * 256 + 256], g_v[j % 3][:, kt, a, :],
                                              g_pt[:, 2 * a + q, kt, :], start=(kt == 0), stop=(kt == 1))
                        fill(m, ("G", "pv", j, a))
                if 0 <= i - 3 < NG:
                    j = i - 3
                    o = claim(pe, ("G", "pj", j))
                    pe.wait_ge(s_gc, j + 1)
                    if j % B == 0:
                        pe.wait_ge(s_gpl, j // B + 1)
                    for st in range(2):
                        for c in range(4):
                            for w in (g_ph, g_pl):
                                m = pe.matmul(o[:, st * D:st * D + D], g_c[j % 2][:, c, st * P:st * P + P],
                                              w[j // B % 2][:, c, :], start=(c == 0 and w is g_ph),
                                              stop=(c == 3 and w is g_pl))
                    fill(m, ("G", "pj", j))

        names = ("q", "qx", "k", "v")

        G_PT_DVE = (0, 2)

        def G_pt_act(act, j, c):
            o = take(act, ("G", "pt", j, c))
            empty(act.copy(g_pt[:, c, :, :], o[:, :].rearrange("p (k s) -> p k s", k=2)), ("G", "pt", j, c))

        def G_tr_act(act, j, c):
            o = take(act, ("G", "tr", j, c))
            t = g_t[j % 2]
            if c < 2:
                w_ = ("q", "qx")[c]
                empty(act.activation(t[:, 2 * c:2 * c + 2, :], o[:, :].rearrange("p (q s) -> p q s", q=2),
                                     ACT.Identity, scale=col(w_ + "w"), bias=col(w_ + "b")), ("G", "tr", j, c))
            else:
                act.activation(t[:, 4, :], o[:, 0:256], ACT.Identity, scale=col("kw"), bias=col("kb"))
                empty(act.activation(t[:, 5, :], o[:, 256:512], ACT.Identity, scale=col("kxw"), bias=col("kxb")),
                      ("G", "tr", j, c))

        def G_act(act):
            for b in range(B):
                o = take(act, ("G", "yt", b))
                for d in range(KD):
                    m = act.activation(yT[:, d, b * 256:b * 256 + 256], o[:, d * 256:d * 256 + 256], ACT.Identity,
                                       scale=col("lnw", d), bias=col("lnb", d))
                empty(m, ("G", "yt", b))
            for b in range(B):
                have(act, ("G", "yt", b))
            act.wait_ge(s_gk, 1)
            for v in range(4):
                if v >= 2:
                    act.wait_ge(s_gx, v - 1)
                for d in range(KD):
                    act.activation(g_tmp[v % 2][:, d, :], yT[:, d, :], ACT.Identity,
                                   scale=g_rc[:, 2 * v + d:2 * v + d + 1]).then_inc(s_gv1, 1)
            act.wait_ge(s_gv1, 8)
            split_w_act(act, 0, ALL)
            split_p_act(act, 0)
            act.wait_ge(s_gx, 4)
            for i in range(NG + 3):
                if 0 <= i - 2 < NG and i >= 3:
                    take(act, ("G", "pv", i - 3, 1))
                if i >= 3 and i - 1 < NG:
                    take(act, ("G", "sc", i - 3, 3))
                for what, c in G_TRANSPOSES:
                    if what == "pt" and 0 <= i - 2 < NG and c not in G_PT_DVE:
                        G_pt_act(act, i - 2, c)
                    if what == "tr" and 0 <= i - 1 < NG:
                        G_tr_act(act, i - 1, c)
                if i < NG:
                    if i >= 3:
                        take(act, ("G", "pv", i - 3, 1))
                    for tt in range(2):
                        o = take(act, ("G", "qkv", i, 2 + tt))
                        act.activation(g_v[i % 3][:, tt, 0, :], o[:, P:2 * P], ACT.Identity, scale=row("s_v"))
                        act.copy(g_v[i % 3][:, tt, 1, :], o[:, 3 * P:4 * P]).then_inc(s_gva, 1)
                if 0 <= i - 1 < NG:
                    j = i - 1
                    if j >= 2:
                        take(act, ("G", "pt", j - 2, 3))
                    for c in range(4):
                        act.wait_ge(s_gnb, 4 * j + c + 1)
                        o = psum[uses[("G", "sc", j, c)][0]]
                        for st in range(2):
                            m = act.activation(g_p[j % 2][:, c, st, :], o[:, st * 256:st * 256 + 256], ACT.Exp,
                                               scale=SCALE, bias=g_mx[j % 2][:, 2 * c + st:2 * c + st + 1],
                                               accum_out=g_sm[j % 2][:, 2 * c + st:2 * c + st + 1])
                        empty(m, ("G", "sc", j, c))
                if i < NG:
                    act.wait_ge(s_grs, i + 1)
                    if i >= 2:
                        take(act, ("G", "tr", i - 2, 2))
                    for tt in range(2):
                        o = psum[uses[("G", "qkv", i, 2 + tt)][0]]
                        for h, a0 in ((4, 0), (5, 256)):
                            s_ = tt * 6 + h
                            m = act.activation(g_n[i % 2][:, s_, :], o[:, a0:a0 + P], ACT.Identity,
                                               scale=g_rs[i % 2][:, s_:s_ + 1], bias=g_nb[i % 2][:, s_:s_ + 1])
                        empty(m, ("G", "qkv", i, 2 + tt))
                if 0 <= i - 2 < NG:
                    j = i - 2
                    if j >= 2:
                        act.wait_ge(s_gc, j - 1)
                    for a in range(2):
                        o = take(act, ("G", "pv", j, a))
                        for q in range(2):
                            f = a * 16 + 2 * (j // B) + q
                            m = act.activation(g_o[j % 2][:, 2 * a + q, :], o[:, q * 256:q * 256 + 256], ACT.Identity,
                                               scale=g_rsm[:, f:f + 1])
                        empty(m, ("G", "pv", j, a))
                if i < NG - B and i % B < 2:
                    split_w_act(act, i // B + 1, (FIRST, LAST)[i % B])
                if i < NG - B and i % B == 3:
                    split_p_act(act, i // B + 1)

        def G_pt_dve(dve, j, c):
            o = take(dve, ("G", "pt", j, c))
            empty(dve.tensor_copy(g_pt[:, c, :, :], o[:, :].rearrange("p (k s) -> p k s", k=2)), ("G", "pt", j, c))

        def G_dve(dve, V):
            ln_dve(dve, V, K_G2, y, EPS, after=8 * K_G + 8)
            c0 = COLS["sc_q"][0]
            V.do(dve.reciprocal(g_rc[:, :], cols[:, c0:c0 + 8]))
            V.do(dve.reciprocal(g_rsm[:, :], cols[:, COLS["smooth"][0]:COLS["smooth"][1]]))
            V.do(dve.tensor_tensor(g_pc[:, :], row("s_pw"), row("s_pi"), ALU.mult))
            V.do(dve.memset(g_w1[:, :], 1.0))
            V.sync()
            for tt in range(2):
                for s_, n in ((0, "s_q"), (1, "s_q"), (2, "s_qx"), (3, "s_qx"), (4, "s_k")):
                    V.do(dve.tensor_copy(g_w1[:, tt * 6 + s_:tt * 6 + s_ + 1], row(n)))
            V.sync()
            V.do(dve.tensor_tensor(g_w2[:, :], g_w1[:, :], g_w1[:, :], ALU.mult))
            V.sync()
            V.do(dve.reciprocal(g_w2[:, :], g_w2[:, :]))
            V.sync()
            dve.tensor_scalar(g_w2[:, :], g_w2[:, :], EPS, None, ALU.mult).then_inc(s_gk, 1)
            flat = "p k n -> p (k n)"
            for v in range(4):
                dve.wait_ge(s_gv1, 2 * (v + 1))
                if v >= 2:
                    dve.wait_ge(s_gx, v - 1)
                tmp, vb, mb = g_tmp[v % 2].rearrange(flat), g_vb.rearrange(flat), g_mb[v % 2].rearrange(flat)
                V.do(dve.tensor_scalar(vb, tmp, FP8_MAX, -FP8_MAX, ALU.min, ALU.max))
                V.sync()
                V.do(dve.tensor_scalar(g_eb.bitcast(U16), vb.bitcast(U16), 0x7F80, None, ALU.bitwise_and))
                V.sync()
                V.do(dve.tensor_scalar(mb, g_eb, FP8_TINY, FP8_MAGIC, ALU.max, ALU.mult))
                V.sync()
                dve.tensor_tensor(tmp, vb, mb, ALU.add).then_inc(s_gq, 1)
                dve.wait_ge(s_gq, v + 1)
            split_w_dve(dve, 0, ALL)
            split_p_dve(dve, 0)
            dve.wait_ge(s_gx, 4)
            for i in range(NG + 4):
                if 0 <= i - 4 < NG:
                    j = i - 4
                    o = take(dve, ("G", "pj", j))
                    b = j % B
                    xb = x[:, 2 * b:2 * b + 2, :].rearrange("p t d -> p (t d)")
                    if j >= B:
                        have(dve, ("G", "pj", j - B))
                    empty(dve.scalar_tensor_tensor(out=xb, in0=o[:, :], scalar=g_pc[:, :], in1=xb,
                                                   op0=ALU.mult, op1=ALU.add), ("G", "pj", j))
                if 0 <= i - 2 < NG:
                    if i >= 3:
                        take(dve, ("G", "pv", i - 3, 1))
                    if 0 in G_PT_DVE:
                        G_pt_dve(dve, i - 2, 0)
                if 0 <= i - 3 < NG:
                    j = i - 3
                    have(dve, ("G", "pv", j, 0))
                    have(dve, ("G", "pv", j, 1))
                    if j >= 2:
                        dve.wait_ge(s_gc, j - 1)
                    V.do(dve.tensor_scalar(g_ob, g_o[j % 2].rearrange(flat), FP8_MAX, -FP8_MAX, ALU.min, ALU.max))
                    V.sync()
                    V.do(dve.tensor_scalar(g_oe.bitcast(U16), g_ob.bitcast(U16), 0x7F80, None, ALU.bitwise_and))
                    V.sync()
                    V.do(dve.tensor_scalar(g_om[j % 2], g_oe, FP8_TINY, FP8_MAGIC, ALU.max, ALU.mult))
                    V.sync()
                    dve.tensor_tensor(g_o[j % 2].rearrange(flat), g_ob, g_om[j % 2], ALU.add).then_inc(s_gt, 1)
                if 0 <= i - 2 < NG:
                    if 2 in G_PT_DVE:
                        G_pt_dve(dve, i - 2, 2)
                if i < NG:
                    for tt in range(2):
                        o = take(dve, ("G", "qkv", i, tt))
                        for h in range(4):
                            V.do(dve.bn_stats(g_bs[:, tt * 6 + h, :], o[:, h * P:h * P + P]))
                    for tt in range(2):
                        o = take(dve, ("G", "qkv", i, 2 + tt))
                        dve.wait_ge(s_gva, 2 * i + tt + 1)
                        for h in range(2):
                            V.do(dve.bn_stats(g_bs[:, tt * 6 + 4 + h, :], o[:, h * 256:h * 256 + P]))
                    V.sync()
                    for s_ in range(12):
                        m = dve.bn_aggr(g_mv[i % 2][:, s_, :], g_bs[:, s_, :])
                    m.then_inc(s_gst, 1)
                if 0 <= i - 1 < NG:
                    j = i - 1
                    for c in range(4):
                        o = take(dve, ("G", "sc", j, c))
                        V.do(dve.tensor_reduce(g_mx[j % 2][:, 2 * c:2 * c + 2], o[:, :].rearrange("p (q s) -> p q s", q=2),
                                               AX.X, ALU.max, negate=True))
                        V.sync()
                        dve.tensor_scalar(g_mx[j % 2][:, 2 * c:2 * c + 2], g_mx[j % 2][:, 2 * c:2 * c + 2], SCALE,
                                          None, ALU.mult).then_inc(s_gnb, 1)
                for tt in range(2):
                    if 0 <= i - 1 < NG:
                        j = i - 1
                        for c in (2 * tt, 2 * tt + 1):
                            have(dve, ("G", "sc", j, c))
                        sums = g_sm[j % 2][:, 4 * tt:4 * tt + 4]
                        dve.reciprocal(sums, sums).then_inc(s_gri, 1)
                    if i < NG:
                        if tt == 0:
                            dve.wait_ge(s_grs, i + 1)
                            if i >= 2:
                                take(dve, ("G", "tr", i - 2, 2))
                        o = psum[uses[("G", "qkv", i, tt)][0]]
                        for h in range(4):
                            s_ = tt * 6 + h
                            m = dve.tensor_scalar(g_n[i % 2][:, s_, :], o[:, h * P:h * P + P],
                                                  g_mv[i % 2][:, s_, 0:1], g_rs[i % 2][:, s_:s_ + 1],
                                                  ALU.subtract, ALU.mult)
                        empty(m, ("G", "qkv", i, tt))
                if i < NG - B and 1 <= i % B < 3:
                    split_w_dve(dve, i // B + 1, (FIRST, LAST)[i % B - 1])
                if 0 < i < NG and i % B == 0:
                    split_p_dve(dve, i // B)
            for j in range(NG - B, NG):
                have(dve, ("G", "pj", j))

        def G_pool(pool, C):
            ln_pool(pool, C, K_G2, EPS)
            pool.wait_ge(s_gk, 1)
            for v in range(4):
                pool.wait_ge(s_gq, v + 1)
                pool.tensor_tensor(g_xs[v][:, :, :].rearrange("p k n -> p (k n)"),
                                   g_tmp[v % 2].rearrange("p k n -> p (k n)"),
                                   g_mb[v % 2].rearrange("p k n -> p (k n)"), ALU.subtract).then_inc(s_gx, 1)
            for i in range(NG + 3):
                if i >= 3:
                    j = i - 3
                    pool.wait_ge(s_gt, j + 1)
                    if j >= 2:
                        take(pool, ("G", "pj", j - 2))
                    pool.tensor_tensor(g_c[j % 2][:, :, :].rearrange("p c s -> p (c s)"), g_o[j % 2].rearrange("p c s -> p (c s)"),
                                       g_om[j % 2], ALU.subtract).then_inc(s_gc, 1)
                if i < NG:
                    pool.wait_ge(s_gst, i + 1)
                    if i >= 2:
                        have(pool, ("G", "qkv", i - 2, 1))
                        have(pool, ("G", "qkv", i - 2, 3))
                    r_, n_ = g_rs[i % 2][:, :], g_nb[i % 2][:, :]
                    C.do(pool.tensor_tensor(r_, g_mv[i % 2][:, :, 1], g_w2[:, :], ALU.add))
                    C.do(pool.tensor_scalar(n_, g_mv[i % 2][:, :, 0], -1.0, None, ALU.mult))
                    C.sync()
                    C.do(pool.tensor_tensor(r_, r_, mhalf[:, 0:12], ALU.pow))
                    C.sync()
                    pool.tensor_tensor(n_, n_, r_, ALU.mult).then_inc(s_grs, 1)
                if 1 <= i <= NG:
                    j = i - 1
                    for half in range(2):
                        pool.wait_ge(s_gri, 2 * j + half + 1)
                        pf = g_p[j % 2][:, 2 * half:2 * half + 2, :, :].rearrange("p c q s -> p (c q) s")
                        sums = g_sm[j % 2][:, 4 * half:4 * half + 4].unsqueeze(2).to_broadcast([P, 4, 256])
                        pool.tensor_tensor(pf, pf, sums, ALU.mult).then_inc(s_gp, 1)

        h_reg = Region(0, 30000)
        h_w2 = h_reg.take([NF, D])
        h_w1 = cx[:, :, :].rearrange("p t d -> p (t d)").rearrange("p (k f) -> p k f", k=KD)
        h_wr = h_reg.take([KD, B * B])
        h_lg = h_reg.take([256])
        h_wk = h_reg.take([2, 256])
        h_m8 = h_reg.take([SLOTS])
        h_sel = h_reg.take([256])
        h_pos = h_reg.take([256])
        h_ew = h_reg.take([256])
        h_sm = h_reg.take([2])
        h_pT = h_reg.take([2, 2, B])
        h_oh = h_reg.take([T, SLOTS])
        h_ohT = h_reg.take([2, P])
        h_fx = h_reg.take([KD, P])
        h_h = h_reg.take([NF, P])
        h_out = h_reg.take([D])
        s_hw1, s_hw2, s_hwr = sem("h_w1_loaded"), sem("h_w2_loaded"), sem("h_router_weights")
        s_hmx, s_hex, s_hpos, s_hoh = sem("h_shifted"), sem("h_exp"), sem("h_slots"), sem("h_onehot")
        for b in range(B):
            plan(("H", "yt", b), b)
        plan(("H", "lg"), 4)
        plan(("H", "pT"), 5)
        plan(("H", "fx"), 6)
        for c in range(2):
            plan(("H", "ohT", c), 4 + c)
        for c in range(2):
            plan(("H", "h", c), c)
        plan(("H", "out"), 7)
        for b in range(B):
            plan(("H", "add", b), b)

        def H_sp(sp):
            sp.wait_ge(s_stage, 5)
            sp.dma_start(h_w1, W1_d).then_inc(s_hw1, 16)
            sp.wait_ge(s_stage, 7)
            sp.dma_start(h_w2, W2_d).then_inc(s_hw2, 16)

        def H_pe(pe):
            yt_pe(pe, K_H, "H")
            pe.wait_ge(s_hwr, 1)
            o = claim(pe, ("H", "lg"))
            for b in range(B):
                have(pe, ("H", "yt", b))
                for k in range(KD):
                    m = pe.matmul(o[0:B, 0:256], h_wr[:, k, b * B:b * B + B], yT[:, k, b * 256:b * 256 + 256],
                                  start=(b == 0 and k == 0), stop=(b == B - 1 and k == 1))
            fill(m, ("H", "lg"))
            o = claim(pe, ("H", "pT"))
            pe.wait_ge(s_hpos, 1)
            for w, src in enumerate((h_pos, h_ew)):
                for q in range(2):
                    m = pe.transpose(o[:, (w * 2 + q) * B:(w * 2 + q) * B + B], src[0:B, q * P:q * P + P],
                                     ident[0:B, 0:B])
            fill(m, ("H", "pT"))
            o = claim(pe, ("H", "fx"))
            pe.wait_ge(s_hoh, 1)
            for d in range(KD):
                for b in range(B):
                    for q in range(2):
                        m = pe.matmul(o[:, d * P + b * SLOTS:d * P + b * SLOTS + SLOTS],
                                      y[:, 2 * b + q, d * P:d * P + P], h_oh[:, 2 * b + q, :],
                                      start=(q == 0), stop=(q == 1))
            fill(m, ("H", "fx"))
            for c in range(2):
                o = claim(pe, ("H", "ohT", c))
                for j in range(4):
                    m = pe.transpose(o[0:SLOTS, j * P:j * P + P], h_oh[:, 4 * c + j, :], ident)
                fill(m, ("H", "ohT", c))
            pe.wait_ge(s_hw1, 16)
            have(pe, ("H", "fx"))
            for c in range(2):
                o = claim(pe, ("H", "h", c))
                for j in range(4):
                    f = 4 * c + j
                    for k in range(KD):
                        m = pe.matmul(o[:, j * P:j * P + P], h_w1[:, k, f * P:f * P + P], h_fx[:, k, :],
                                      start=(k == 0), stop=(k == 1))
                fill(m, ("H", "h", c))
            o = claim(pe, ("H", "out"))
            pe.wait_ge(s_hw2, 16)
            for f in range(NF):
                have(pe, ("H", "h", f // 4))
                m = pe.matmul(o[:, 0:D], h_h[:, f, :], h_w2[:, f, :], start=(f == 0), stop=(f == NF - 1))
            fill(m, ("H", "out"))
            have(pe, ("H", "out"))
            have(pe, ("H", "ohT", 0))
            have(pe, ("H", "ohT", 1))
            for b in range(B):
                o = claim(pe, ("H", "add", b))
                r = 32 * b
                for q in range(2):
                    m = pe.matmul(o[:, q * D:q * D + D], h_ohT[r:r + 32, q, :], h_out[r:r + 32, :],
                                  start=True, stop=True)
                fill(m, ("H", "add", b))

        def H_act(act):
            yt_act(act, "H")
            act.wait_ge(s_hmx, 1)
            act.activation(h_ew[0:B, :], h_lg[0:B, :], ACT.Exp).then_inc(s_hex, 1)
            for c in range(2):
                o = take(act, ("H", "h", c))
                for j in range(4):
                    f = 4 * c + j
                    m = act.activation(h_h[:, f, :], o[:, j * P:j * P + P], ACT.Gelu, bias=col("b1", f))
                empty(m, ("H", "h", c))

        def H_dve(dve, V):
            V.do(dve.memset(h_wr, 0.0))
            V.sync()
            for k in range(KD):
                m = dve.tensor_copy(h_wr[:, k, 0:B * B:B + 1], col("Wr", k).to_broadcast([P, B]))
            m.then_inc(s_hwr, 1)
            b4 = slice(0, B)
            o = take(dve, ("H", "lg"))
            empty(dve.tensor_scalar(h_lg[b4, :], o[b4, 0:256], row("br", B), None, ALU.add), ("H", "lg"))
            have(dve, ("H", "lg"))
            V.do(dve.tensor_copy(h_wk[b4, 0, :], h_lg[b4, :]))
            V.sync()
            for r in range(SLOTS // 8):
                V.do(dve.max(out=h_m8[b4, 8 * r:8 * r + 8], in_=h_wk[b4, r % 2, :]))
                V.sync()
                V.do(dve.match_replace(out=h_wk[b4, 1 - r % 2, :], in_to_replace=h_m8[b4, 8 * r:8 * r + 8],
                                       in_values=h_wk[b4, r % 2, :], imm_value=-3e38))
                V.sync()
            V.do(dve.tensor_tensor(h_sel[b4, :], h_wk[b4, 0, :], h_lg[b4, :], ALU.not_equal))
            V.sync()
            V.do(dve.tensor_tensor_scan(h_pos[b4, :], b_z[b4, :], h_sel[b4, :], 0.0, ALU.add, ALU.add))
            dve.tensor_scalar(h_lg[b4, :], h_lg[b4, :], h_m8[b4, 0:1], None, ALU.subtract).then_inc(s_hmx, 1)
            V.sync()
            V.do(dve.tensor_tensor(h_pos[b4, :], h_pos[b4, :], h_sel[b4, :], ALU.mult))
            V.sync()
            V.do(dve.tensor_scalar(h_pos[b4, :], h_pos[b4, :], -1.0, None, ALU.add))
            dve.wait_ge(s_hex, 1)
            V.do(dve.tensor_tensor(h_ew[b4, :], h_ew[b4, :], h_sel[b4, :], ALU.mult))
            V.sync()
            V.do(dve.tensor_reduce(h_sm[b4, 0:1], h_ew[b4, :], AX.X, ALU.add))
            V.sync()
            V.do(dve.reciprocal(h_sm[b4, 1:2], h_sm[b4, 0:1]))
            V.sync()
            dve.tensor_scalar(h_ew[b4, :], h_ew[b4, :], h_sm[b4, 1:2], None, ALU.mult).then_inc(s_hpos, 1)
            o = take(dve, ("H", "pT"))
            empty(dve.tensor_copy(h_pT.rearrange("p a b c -> p (a b c)"), o[:, 0:16]), ("H", "pT"))
            have(dve, ("H", "pT"))
            for t in range(T):
                m = dve.tensor_scalar(h_oh[:, t, :], cst[:, 264:296], h_pT[:, 0, t % 2, t // 2:t // 2 + 1], None,
                                      ALU.is_equal)
                if t < T - 1:
                    V.do(m)
            m.then_inc(s_hoh, 1)
            dve.wait_ge(s_y, 8 * K_H + 8)
            V.do(dve.tensor_tensor(x[:, :, :], x[:, :, :], y[:, :, :], ALU.add))
            o = take(dve, ("H", "fx"))
            empty(dve.tensor_copy(h_fx.rearrange("p k n -> p (k n)"), o[:, 0:256]), ("H", "fx"))
            for c in range(2):
                o = take(dve, ("H", "ohT", c))
                for j in range(4):
                    t = 4 * c + j
                    r = 32 * (t // 2)
                    m = dve.tensor_copy(h_ohT[r:r + 32, t % 2, :], o[0:SLOTS, j * P:j * P + P])
                    if j < 3:
                        V.do(m)
                empty(m, ("H", "ohT", c))
            o = take(dve, ("H", "out"))
            empty(dve.tensor_tensor(h_out, o[:, 0:D], row("b2"), ALU.add), ("H", "out"))
            V.sync()
            for b in range(B):
                o = take(dve, ("H", "add", b))
                for q in range(2):
                    t = 2 * b + q
                    m = dve.scalar_tensor_tensor(out=x[:, t, :], in0=o[:, q * D:q * D + D],
                                                 scalar=h_pT[:, 1, q, b:b + 1], in1=x[:, t, :],
                                                 op0=ALU.mult, op1=ALU.add)
                    if q == 0:
                        V.do(m)
                empty(m, ("H", "add", b))
            for b in range(B):
                have(dve, ("H", "add", b))

        s_out = sem("stored")

        block = ctx_mgr.enter_context(nc.Block())

        @block.sync
        def _(sp):
            sp.dma_start(x[:, :, :], x_d.rearrange("b (h p) d -> p (b h) d", p=P)).then_inc(s_x, 16)
            sp.dma_start(cst[:, :], cst_d).then_inc(s_cst, 16)
            sp.dma_start(cols[:, :], cols_d).then_inc(s_cst, 16)
            sp.dma_start(rows[:, :], rows_d.partition_broadcast(P)).then_inc(s_cst, 16)
            sp.dma_start(cx[:, :, :], ctx_d.rearrange("b (h p) d -> p (b h) d", p=P)).then_inc(s_ctx, 16)
            sp.dma_start(cxT[:, :, :], ctxT_d).then_inc(s_ctxT, 16)
            sp.dma_start(b_rw[:, :, :], rw_d).then_inc(s_small, 16)
            D_sp(sp)
            sp.dma_start(b_bd[0:NE, :], bd_d).then_inc(s_small, 16)
            B_sp(sp)
            E_sp(sp)
            F_sp(sp)
            G_sp(sp)
            H_sp(sp)
            sp.wait_ge(s_stage, 8)
            sp.dma_start(out_d.rearrange("b (h p) d -> p (b h) d", p=P), x[:, :, :]).then_inc(s_out, 16)
            sp.wait_ge(s_out, 16)

        @block.tensor
        def _(pe):
            A_pe(pe)
            B_pe(pe)
            C_pe(pe)
            D_pe(pe)
            E_pe(pe)
            F_pe(pe)
            G_pe(pe)
            H_pe(pe)

        @block.scalar
        def _(act):
            A_act(act)
            B_act(act)
            C_act(act)
            D_act(act)
            E_act(act)
            F_act(act)
            G_act(act)
            H_act(act)

        @block.vector
        def _(dve):
            V = Chain(dve, s_dve)

            def done():
                V.sync()
                dve.tensor_copy(b_n[:, 1:2], mv[:, 0, 0:1]).then_inc(s_stage, 1)

            dve.wait_ge(s_x, 16)
            ln_dve(dve, V, K_A, x, EPS)
            setup_dve(dve, V)
            ctx_quant_dve(dve, V)
            A_dve(dve, V)
            done()
            for k, f in ((K_B, B_dve), (K_C, C_dve), (K_D, D_dve), (K_E, E_dve), (K_F, F_dve), (K_G, G_dve),
                         (K_H, H_dve)):
                ln_dve(dve, V, k, x, EPS)
                f(dve, V)
                done()

        @block.gpsimd
        def _(pool):
            C = Chain(pool, s_pool)
            setup_pool(pool, C)
            ln_pool(pool, C, K_A, EPS)
            ctx_quant_pool(pool, C)
            ln_pool(pool, C, K_B, EPS)
            B_pool(pool, C)
            ln_pool(pool, C, K_C, EPS)
            E_prep_pool(pool, C)
            ln_pool(pool, C, K_D, EPS)
            ln_pool(pool, C, K_E, EPS)
            E_pool(pool, C)
            ln_pool(pool, C, K_F, EPS)
            F_pool(pool, C)
            ln_pool(pool, C, K_G, EPS)
            G_pool(pool, C)
            ln_pool(pool, C, K_H, EPS)


_OUTS = [((4, 256, 256), "float32")]


def _layout(i):
    import numpy as np

    def c(a):
        return np.ascontiguousarray(a)

    def kxm(w):
        return c(w.reshape(w.shape[0] // P, P, w.shape[1]).transpose(1, 0, 2))

    def column(v, n):
        v = np.asarray(v).reshape(-1)
        full = np.zeros((n * P,), np.float32)
        full[:v.size] = v
        return full.reshape(n, P).T

    i = {k: np.asarray(v) for k, v in i.items()}
    ctx = i["ctx_2048"]
    cst = np.zeros((P, NCST), np.float32)
    cst[:, 0:128] = np.eye(P)
    r = np.arange(P)
    cst[:, 128:256] = np.where(r[None, :] >= r[:, None], 0.0, -BIG)
    cst[:, 256:264] = (r // DH)[:, None] == np.arange(8)[None, :]
    cst[:, 264:296] = np.arange(32)[None, :]
    cst[:, 296:312] = (r % 32)[:, None] == np.arange(16)[None, :]
    gu = i["L0_ffn_gate_up_proj"]
    gu = np.concatenate([gu[..., 0::2], gu[..., 1::2]], axis=-1)
    bgu = i["L0_ffn_gate_up_proj_bias"]
    bgu = np.concatenate([bgu[..., 0::2], bgu[..., 1::2]], axis=-1)
    cv = {"bgu": column(bgu, 64), "gs": column(i["L1_ffn_gate_s"], NI), "us": column(i["L1_ffn_up_s"], NI),
          "bi": column(i["L2_xattn_bi"], 1), "bf": column(i["L2_xattn_bf"], 1),
          "lnw": column(i["L3_xattn_ln_w"], 2), "lnb": column(i["L3_xattn_ln_b"], 2),
          "sc_q": column(i["L3_xattn_q_in_scale"], 2), "sc_qx": column(i["L3_xattn_qx_in_scale"], 2),
          "sc_k": column(i["L3_xattn_k_in_scale"], 2), "sc_v": column(i["L3_xattn_v_in_scale"], 2),
          "smooth": column(i["L3_xattn_proj_smooth"], 32), "Wr": column(i["L3_ffn_Wr"], 2),
          "b1": column(i["L3_ffn_b1"], NF)}
    for s, l in (("q", "q"), ("k", "k"), ("qx", "qx"), ("kx", "kx")):
        cv[s + "w"] = column(i[f"L3_xattn_{l}ln_w"], 1)
        cv[s + "b"] = column(i[f"L3_xattn_{l}ln_b"], 1)
    cols = np.zeros((P, NCOL), np.float32)
    for n, (a, z) in COLS.items():
        cols[:, a:z] = cv[n]
    rv = {"rb": i["L0_ffn_router_bias"], "ds": i["L1_ffn_down_s"], "lns": i["L2_xattn_ln_scale"],
          "b2f": i["L2_ffn_bias"], "b2": i["L3_ffn_b2"], "s_q": i["L3_xattn_wq_scale"],
          "s_qx": i["L3_xattn_wqx_scale"], "s_k": i["L3_xattn_wk_scale"], "s_v": i["L3_xattn_wv_scale"],
          "s_pw": i["L3_xattn_proj_w_scale"], "s_pi": i["L3_xattn_proj_in_scale"], "br": i["L3_ffn_br"]}
    rows = np.zeros((NROW,), np.float32)
    for n, (a, z) in ROWS.items():
        rows[a:z] = rv[n].reshape(-1)

    def heads(w, per):
        return w.reshape(G, per * HD, D).transpose(0, 2, 1)

    kv = i["L3_xattn_w_kv_x"]
    wg = np.concatenate([heads(i["L3_xattn_wq"], 2), heads(i["L3_xattn_wqx"], 2), heads(i["L3_xattn_wk"], 1),
                         heads(i["L3_xattn_wv"], 1), heads(kv[:G * HD], 1), heads(kv[G * HD:], 1)], axis=2)
    wp = i["L3_xattn_wproj"].T.reshape(2, G, 2, HD, D).transpose(1, 3, 0, 2, 4).reshape(G, HD, 4, D)
    return [
        i["x"], ctx, kxm(ctx.reshape(B * S, D).T), cst, cols, rows,
        kxm(i["L0_ffn_router_weight"].T),
        c(gu.reshape(NE, KD, P, 4 * P).transpose(0, 2, 1, 3)),
        c(i["L0_ffn_down_proj"].reshape(NE, KD, P, D).transpose(0, 2, 1, 3)),
        i["L0_ffn_down_proj_bias"],
        kxm(i["L1_ffn_gate_w"].T), kxm(i["L1_ffn_up_w"].T), c(i["L1_ffn_down_w"].T),
        kxm(np.concatenate([i["L2_xattn_Wi"], i["L2_xattn_Wf"]], axis=1)),
        kxm(i["L2_ffn_weight"].T),
        c(wg.reshape(G, KD, P, 1024).transpose(0, 2, 1, 3)), c(wp),
        kxm(i["L3_ffn_W1"]), kxm(i["L3_ffn_W2"]),
    ]


def kernel(**inputs):
    import numpy as _np
    import concourse.bacc as _bacc
    from concourse import mybir as _mybir
    from concourse.bass_utils import run_bass_kernel_spmd as _run

    nc = _bacc.Bacc("TRN2", target_bir_lowering=False, num_devices=1)
    arrays, args = {}, []
    for n, a in enumerate(_layout(inputs)):
        a = _np.ascontiguousarray(a)
        arrays[f"in_{n}_dram"] = a
        args.append(nc.dram_tensor(f"in_{n}_dram", a.shape, _mybir.dt.from_np(a.dtype), kind="ExternalInput").ap())
    for i, (shape, dtype) in enumerate(_OUTS):
        dt = _mybir.dt.from_np(_np.dtype(dtype))
        args.append(nc.dram_tensor(f"out_{i}_dram", shape, dt, kind="ExternalOutput").ap())
    build(nc, *args)
    r = _run(nc, [arrays], core_ids=[0])
    return r.results[0]["out_0_dram"]
```
